# Optimizing a Trainium2 kernel written in Bass

```python
import numpy as np
import jax
import jax.numpy as jnp

def _softmax(x, axis=-1):
    return jax.nn.softmax(x, axis=axis)

def _gelu(x):
    return jax.nn.gelu(x, approximate=True)

def _silu(x):
    return jax.nn.silu(x)

def _sigmoid(x):
    return jax.nn.sigmoid(x)

def _layernorm(x, axis=-1, eps=1e-05):
    m = jnp.mean(x, axis=axis, keepdims=True)
    v = jnp.var(x, axis=axis, keepdims=True)
    return (x - m) / jnp.sqrt(v + eps)

def _scatter_add(tgt, idx, src, axis=0):
    return tgt.at[idx].add(src)

def _segment_sum(src, seg, n):
    return jax.ops.segment_sum(src, seg, n)
kernel_name = 'mk_xattn_seq_d4_seqx_r8_c7be42'

def setup_inputs(seed: int=0):
    np.random.seed(seed)
    _w = jnp.asarray

    def _rec_inputs():
        import jax
        import jax.numpy as jnp
        _rk = jax.random.key(seed)
        x = -0.0002928 + 1 * jax.random.normal(jax.random.fold_in(_rk, 1), (32, 128, 128), jnp.float32)
        _lenS = 128 - jax.random.randint(jax.random.fold_in(_rk, 7), (32,), 0, max(1, 128 // 4) + 1, jnp.int32)
        _lenS2 = 128 - jax.random.randint(jax.random.fold_in(_rk, 8), (32,), 0, max(1, 128 // 4) + 1, jnp.int32)
        _ctx_1024P = jax.random.normal(jax.random.fold_in(_rk, 11), (32, 16, 128), jnp.float32)
        _ctx_1024c = jax.random.dirichlet(jax.random.fold_in(_rk, 511), 0.3 * jnp.ones((16,), jnp.float32), (32, 128))
        _ctx_1024t = jnp.einsum('bsk,bkd->bsd', _ctx_1024c, _ctx_1024P)
        _ctx_1024t = _ctx_1024t * jax.lax.rsqrt(jnp.mean(jnp.square(_ctx_1024t)) + 1e-12) * 0.953939
        ctx_1024 = -1.39393e-06 + 0.999914 * (_ctx_1024t + 0.3 * jax.random.normal(jax.random.fold_in(_rk, 611), (32, 128, 128), jnp.float32))
        itok_BxS2_4_31999 = jax.random.randint(jax.random.fold_in(_rk, 14), (32, 128), 4, 4000, jnp.int32)
        _ctxb_2048x64P = jax.random.normal(jax.random.fold_in(_rk, 15), (32, 16, 64), jnp.float32)
        _ctxb_2048x64c = jax.random.dirichlet(jax.random.fold_in(_rk, 515), 0.3 * jnp.ones((16,), jnp.float32), (32, 128))
        _ctxb_2048x64t = jnp.einsum('bsk,bkd->bsd', _ctxb_2048x64c, _ctxb_2048x64P)
        _ctxb_2048x64t = _ctxb_2048x64t * jax.lax.rsqrt(jnp.mean(jnp.square(_ctxb_2048x64t)) + 1e-12) * 0.953939
        ctxb_2048x64 = 0.50053 + 0.288505 * (_ctxb_2048x64t + 0.3 * jax.random.normal(jax.random.fold_in(_rk, 615), (32, 128, 64), jnp.float32))
        _validS = jnp.arange(128)[None, :] < _lenS[:, None]
        _validS2 = jnp.arange(128)[None, :] < _lenS2[:, None]
        _causal = jnp.tril(jnp.ones((128, 128), dtype=bool))
        mask_BxS2_bf1 = jnp.ones((32, 128), dtype=bool)
        mask_BxS_ik0 = jnp.where(jnp.broadcast_to(_validS[:, :], (32, 128)), 0, 1).astype(jnp.int32)
        return (x, ctx_1024, itok_BxS2_4_31999, ctxb_2048x64, mask_BxS2_bf1, mask_BxS_ik0)
    x, ctx_1024, itok_BxS2_4_31999, ctxb_2048x64, mask_BxS2_bf1, mask_BxS_ik0 = _rec_inputs()

    def _L0_xattn_setup():
        import jax, jax.numpy as jnp
        import numpy as np
        import math
        E = 128
        H = 16
        DK = 64
        DV = 64
        B = 2
        S = 256
        NEG_INF = float('-inf')

        def _layer_norm(x, gamma, beta, eps=1e-12):
            mean = x.mean(-1, keepdims=True)
            var = ((x - mean) ** 2).mean(-1, keepdims=True)
            return gamma * (x - mean) / jnp.sqrt(var + eps) + beta

        def _mha(q_in, k_in, v_in, wq, bq, wk, bk, wv, bv, wo, bo, padding_mask, causal):
            Bq, Sq, _ = q_in.shape
            Sk = k_in.shape[1]
            q = (q_in @ wq + bq).reshape(Bq, Sq, H, DK).transpose(0, 2, 1, 3)
            k = (k_in @ wk + bk).reshape(Bq, Sk, H, DK).transpose(0, 2, 1, 3)
            v = (v_in @ wv + bv).reshape(Bq, Sk, H, DV).transpose(0, 2, 1, 3)
            scores = jnp.einsum('bhqd,bhkd->bhqk', q, k)
            if causal:
                causal_mask = jnp.triu(jnp.ones((Sq, Sk), dtype=bool), k=1)
                scores = jnp.where(causal_mask[None, None], NEG_INF, scores)
            if padding_mask is not None:
                scores = jnp.where(padding_mask[:, None, None, :], scores, NEG_INF)
            attn = jax.nn.softmax(scores / math.sqrt(DK), axis=-1)
            attn = jnp.nan_to_num(attn, nan=0.0, posinf=0.0, neginf=0.0)
            out = jnp.einsum('bhqk,bhkd->bhqd', attn, v)
            out = out.transpose(0, 2, 1, 3).reshape(Bq, Sq, H * DV)
            return out @ wo + bo
        key = jax.random.key(seed)
        ks = jax.random.split(key, 24)
        s = 0.02

        def w(i, shape):
            return (s * jax.random.normal(ks[i], shape)).astype(jnp.float32)
        inp = {'input': jax.random.normal(ks[0], (B, S, E), dtype=jnp.float32), 'encoder_output': jax.random.normal(ks[1], (B, S, E), dtype=jnp.float32), 'src_mask': jnp.ones((B, S), dtype=bool), 'trg_mask': jnp.ones((B, S), dtype=bool), 'sa_wq': w(2, (E, H * DK)), 'sa_bq': jnp.zeros((H * DK,), jnp.float32), 'sa_wk': w(3, (E, H * DK)), 'sa_bk': jnp.zeros((H * DK,), jnp.float32), 'sa_wv': w(4, (E, H * DV)), 'sa_bv': jnp.zeros((H * DV,), jnp.float32), 'sa_wo': w(5, (H * DV, E)), 'sa_bo': jnp.zeros((E,), jnp.float32), 'ca_wq': w(6, (E, H * DK)), 'ca_bq': jnp.zeros((H * DK,), jnp.float32), 'ca_wk': w(7, (E, H * DK)), 'ca_bk': jnp.zeros((H * DK,), jnp.float32), 'ca_wv': w(8, (E, H * DV)), 'ca_bv': jnp.zeros((H * DV,), jnp.float32), 'ca_wo': w(9, (H * DV, E)), 'ca_bo': jnp.zeros((E,), jnp.float32), 'ffn_w1': w(10, (E, 4 * E)), 'ffn_b1': jnp.zeros((4 * E,), jnp.float32), 'ffn_w2': w(11, (4 * E, E)), 'ffn_b2': jnp.zeros((E,), jnp.float32), 'ln1_g': jnp.ones((E,), jnp.float32), 'ln1_b': jnp.zeros((E,), jnp.float32), 'ln2_g': jnp.ones((E,), jnp.float32), 'ln2_b': jnp.zeros((E,), jnp.float32), 'ln3_g': jnp.ones((E,), jnp.float32), 'ln3_b': jnp.zeros((E,), jnp.float32)}
        return inp
    _L0_xattn_all = _L0_xattn_setup()
    _L0_xattn_in = {k: v for k, v in _L0_xattn_all.items() if k in ('sa_wq', 'sa_bq', 'sa_wk', 'sa_bk', 'sa_wv', 'sa_bv', 'sa_wo', 'sa_bo', 'ca_wq', 'ca_bq', 'ca_wk', 'ca_bk', 'ca_wv', 'ca_bv', 'ca_wo', 'ca_bo', 'ffn_w1', 'ffn_b1', 'ffn_w2', 'ffn_b2', 'ln1_g', 'ln1_b', 'ln2_g', 'ln2_b', 'ln3_g', 'ln3_b')}
    del _L0_xattn_all

    def _L1_xattn_setup():
        import jax, jax.numpy as jnp
        import numpy as np
        B, S, D, H = (2, 256, 128, 16)
        HD = D // H

        def _split_heads(x):
            b, s, d = x.shape
            return x.reshape(b, s, H, HD).transpose(0, 2, 1, 3)
        key = jax.random.key(seed)
        ks = jax.random.split(key, 10)
        inp = {'queries': jax.random.normal(ks[0], (B, S, D), dtype=jnp.float32), 'keys': jax.random.normal(ks[1], (B, S, D), dtype=jnp.float32), 'values': jax.random.normal(ks[2], (B, S, D), dtype=jnp.float32), 'attention_mask': jax.random.randint(ks[3], (B, S), 0, 2, dtype=jnp.int32), 'Wq': jax.random.normal(ks[4], (D, D), dtype=jnp.float32) / np.sqrt(D), 'bq': jnp.zeros((D,), dtype=jnp.float32), 'Wk': jax.random.normal(ks[5], (D, D), dtype=jnp.float32) / np.sqrt(D), 'bk': jnp.zeros((D,), dtype=jnp.float32), 'Wv': jax.random.normal(ks[6], (D, D), dtype=jnp.float32) / np.sqrt(D), 'bv': jnp.zeros((D,), dtype=jnp.float32)}
        return inp
    _L1_xattn_all = _L1_xattn_setup()
    _L1_xattn_in = {k: v for k, v in _L1_xattn_all.items() if k in ('Wq', 'bq', 'Wk', 'bk', 'Wv', 'bv')}
    del _L1_xattn_all

    def _L2_xattn_setup():
        import jax, jax.numpy as jnp
        import numpy as np
        N, L, C, NHEAD = (4, 256, 128, 8)
        D = C // NHEAD
        EPS_ATTN = 1e-06
        EPS_LN = 1e-05

        def _w(key, shape, scale=0.02):
            return jax.random.normal(key, shape, dtype=jnp.float32) * scale

        def layernorm(x, g, b):
            m = jnp.mean(x, axis=-1, keepdims=True)
            v = jnp.mean(jnp.square(x - m), axis=-1, keepdims=True)
            return (x - m) * jax.lax.rsqrt(v + EPS_LN) * g + b

        def linear_attention(q, k, v):
            Q = jax.nn.elu(q) + 1.0
            K = jax.nn.elu(k) + 1.0
            vlen = v.shape[1]
            v = v / vlen
            KV = jnp.einsum('nshd,nshv->nhdv', K, v)
            Z = 1.0 / (jnp.einsum('nlhd,nhd->nlh', Q, K.sum(axis=1)) + EPS_ATTN)
            out = jnp.einsum('nlhd,nhdv,nlh->nlhv', Q, KV, Z) * vlen
            return out

        def heads(x):
            n, l, c = x.shape
            return x.reshape(n, l, NHEAD, D)

        def encoder_layer(x, wq, wk, wv, wm, w1, w2, g1, b1, g2, b2):
            n, l, c = x.shape
            msg = linear_attention(heads(x @ wq), heads(x @ wk), heads(x @ wv))
            msg = msg.reshape(n, l, c) @ wm
            x = x + layernorm(msg, g1, b1)
            x = x + layernorm(jax.nn.relu(x @ w1) @ w2, g2, b2)
            return x

        def decoder_layer(x, src, wq0, wk0, wv0, wm0, wq1, wk1, wv1, wm1, w1, w2, g0, b0, g1, b1, g2, b2):
            n, l, c = x.shape
            msg = linear_attention(heads(x @ wq0), heads(x @ wk0), heads(x @ wv0))
            msg = msg.reshape(n, l, c) @ wm0
            x = x + layernorm(msg, g0, b0)
            msg = linear_attention(heads(x @ wq1), heads(src @ wk1), heads(src @ wv1))
            msg = msg.reshape(n, l, c) @ wm1
            x = x + layernorm(msg, g1, b1)
            x = x + layernorm(jax.nn.relu(x @ w1) @ w2, g2, b2)
            return x
        key = jax.random.key(seed)
        ks = jax.random.split(key, 32)
        inp = {'depth_feat': jax.random.normal(ks[0], (N, L, C), dtype=jnp.float32), 'context_feat': jax.random.normal(ks[1], (N, L, C), dtype=jnp.float32), 'depth_pos': jax.random.normal(ks[2], (N, L, C), dtype=jnp.float32), 'e_wq': _w(ks[3], (C, C)), 'e_wk': _w(ks[4], (C, C)), 'e_wv': _w(ks[5], (C, C)), 'e_wm': _w(ks[6], (C, C)), 'e_w1': _w(ks[7], (C, 2 * C)), 'e_w2': _w(ks[8], (2 * C, C)), 'e_g1': jnp.ones((C,), jnp.float32), 'e_b1': jnp.zeros((C,), jnp.float32), 'e_g2': jnp.ones((C,), jnp.float32), 'e_b2': jnp.zeros((C,), jnp.float32), 'd_wq0': _w(ks[9], (C, C)), 'd_wk0': _w(ks[10], (C, C)), 'd_wv0': _w(ks[11], (C, C)), 'd_wm0': _w(ks[12], (C, C)), 'd_wq1': _w(ks[13], (C, C)), 'd_wk1': _w(ks[14], (C, C)), 'd_wv1': _w(ks[15], (C, C)), 'd_wm1': _w(ks[16], (C, C)), 'd_w1': _w(ks[17], (C, 2 * C)), 'd_w2': _w(ks[18], (2 * C, C)), 'd_g0': jnp.ones((C,), jnp.float32), 'd_b0': jnp.zeros((C,), jnp.float32), 'd_g1': jnp.ones((C,), jnp.float32), 'd_b1': jnp.zeros((C,), jnp.float32), 'd_g2': jnp.ones((C,), jnp.float32), 'd_b2': jnp.zeros((C,), jnp.float32)}
        return inp
    _L2_xattn_all = _L2_xattn_setup()
    _L2_xattn_in = {k: v for k, v in _L2_xattn_all.items() if k in ('e_wq', 'e_wk', 'e_wv', 'e_wm', 'e_w1', 'e_w2', 'e_g1', 'e_b1', 'e_g2', 'e_b2', 'd_wq0', 'd_wk0', 'd_wv0', 'd_wm0', 'd_wq1', 'd_wk1', 'd_wv1', 'd_wm1', 'd_w1', 'd_w2', 'd_g0', 'd_b0', 'd_g1', 'd_b1', 'd_g2', 'd_b2')}
    del _L2_xattn_all

    def _L3_xattn_setup():
        import jax, jax.numpy as jnp
        import numpy as np
        BATCH, T, H, S, P, NH = (4, 256, 128, 64, 64, 8)
        HD = H // NH

        def _layernorm(x, g, b):
            mu = jnp.mean(x, axis=-1, keepdims=True)
            var = jnp.mean((x - mu) ** 2, axis=-1, keepdims=True)
            return (x - mu) * jax.lax.rsqrt(var + 1e-05) * g + b

        def _mha(q_in, kv_in, W_qkv, b_qkv, W_o, b_o):
            Wq, Wk, Wv = jnp.split(W_qkv, 3, axis=0)
            bq, bk, bv = jnp.split(b_qkv, 3, axis=0)

            def heads(x, W, b):
                y = x @ W.T + b
                return y.reshape(y.shape[0], y.shape[1], NH, HD).transpose(0, 2, 1, 3)
            q, k, v = (heads(q_in, Wq, bq), heads(kv_in, Wk, bk), heads(kv_in, Wv, bv))
            scores = jnp.einsum('bhqd,bhkd->bhqk', q, k) * (1.0 / np.sqrt(HD))
            attn = jax.nn.softmax(scores, axis=-1)
            out = jnp.einsum('bhqk,bhkd->bhqd', attn, v)
            out = out.transpose(0, 2, 1, 3).reshape(q_in.shape)
            return out @ W_o.T + b_o
        key = jax.random.key(seed)
        ks = jax.random.split(key, 16)
        sH = 1.0 / np.sqrt(H)
        d = {}
        d['builder_state'] = jax.random.normal(ks[0], (BATCH, T, H), jnp.float32)
        d['base_state'] = jax.random.normal(ks[1], (BATCH, T, H), jnp.float32)
        d['input_ids'] = jax.random.randint(ks[2], (BATCH, T), 0, 4000)
        d['program_probs'] = jax.random.uniform(ks[3], (BATCH, T, P), jnp.float32)
        d['A'] = jax.random.normal(ks[4], (S, S), jnp.float32) * (0.5 / np.sqrt(S))
        d['Bmat'] = jax.random.normal(ks[5], (H, S), jnp.float32) * sH
        d['Cmat'] = jax.random.normal(ks[6], (S, H), jnp.float32) * (1.0 / np.sqrt(S))
        d['W_in'] = jax.random.normal(ks[7], (H, H), jnp.float32) * sH
        d['b_in'] = jnp.zeros((H,), jnp.float32)
        d['W_qkv'] = jax.random.normal(ks[8], (3 * H, H), jnp.float32) * sH
        d['b_qkv'] = jnp.zeros((3 * H,), jnp.float32)
        d['W_o'] = jax.random.normal(ks[9], (H, H), jnp.float32) * sH
        d['b_o'] = jnp.zeros((H,), jnp.float32)
        d['W_prog'] = jax.random.normal(ks[10], (H, P), jnp.float32) * (1.0 / np.sqrt(P))
        d['b_prog'] = jnp.zeros((H,), jnp.float32)
        d['g1'] = jnp.ones((H,), jnp.float32)
        d['beta1'] = jnp.zeros((H,), jnp.float32)
        d['g2'] = jnp.ones((H,), jnp.float32)
        d['beta2'] = jnp.zeros((H,), jnp.float32)
        return d
    _L3_xattn_all = _L3_xattn_setup()
    _L3_xattn_in = {k: v for k, v in _L3_xattn_all.items() if k in ('A', 'Bmat', 'Cmat', 'W_in', 'b_in', 'W_qkv', 'b_qkv', 'W_o', 'b_o', 'W_prog', 'b_prog', 'g1', 'beta1', 'g2', 'beta2')}
    del _L3_xattn_all
    return {'x': x, 'ctx_1024': ctx_1024, 'itok_BxS2_4_31999': itok_BxS2_4_31999, 'ctxb_2048x64': ctxb_2048x64, 'mask_BxS2_bf1': mask_BxS2_bf1, 'mask_BxS_ik0': mask_BxS_ik0, 'L0_xattn_sa_wq': _L0_xattn_in['sa_wq'], 'L0_xattn_sa_bq': _L0_xattn_in['sa_bq'], 'L0_xattn_sa_wk': _L0_xattn_in['sa_wk'], 'L0_xattn_sa_bk': _L0_xattn_in['sa_bk'], 'L0_xattn_sa_wv': _L0_xattn_in['sa_wv'], 'L0_xattn_sa_bv': _L0_xattn_in['sa_bv'], 'L0_xattn_sa_wo': _L0_xattn_in['sa_wo'], 'L0_xattn_sa_bo': _L0_xattn_in['sa_bo'], 'L0_xattn_ca_wq': _L0_xattn_in['ca_wq'], 'L0_xattn_ca_bq': _L0_xattn_in['ca_bq'], 'L0_xattn_ca_wk': _L0_xattn_in['ca_wk'], 'L0_xattn_ca_bk': _L0_xattn_in['ca_bk'], 'L0_xattn_ca_wv': _L0_xattn_in['ca_wv'], 'L0_xattn_ca_bv': _L0_xattn_in['ca_bv'], 'L0_xattn_ca_wo': _L0_xattn_in['ca_wo'], 'L0_xattn_ca_bo': _L0_xattn_in['ca_bo'], 'L0_xattn_ffn_w1': _L0_xattn_in['ffn_w1'], 'L0_xattn_ffn_b1': _L0_xattn_in['ffn_b1'], 'L0_xattn_ffn_w2': _L0_xattn_in['ffn_w2'], 'L0_xattn_ffn_b2': _L0_xattn_in['ffn_b2'], 'L0_xattn_ln1_g': _L0_xattn_in['ln1_g'], 'L0_xattn_ln1_b': _L0_xattn_in['ln1_b'], 'L0_xattn_ln2_g': _L0_xattn_in['ln2_g'], 'L0_xattn_ln2_b': _L0_xattn_in['ln2_b'], 'L0_xattn_ln3_g': _L0_xattn_in['ln3_g'], 'L0_xattn_ln3_b': _L0_xattn_in['ln3_b'], 'L1_xattn_Wq': _L1_xattn_in['Wq'], 'L1_xattn_bq': _L1_xattn_in['bq'], 'L1_xattn_Wk': _L1_xattn_in['Wk'], 'L1_xattn_bk': _L1_xattn_in['bk'], 'L1_xattn_Wv': _L1_xattn_in['Wv'], 'L1_xattn_bv': _L1_xattn_in['bv'], 'L2_xattn_e_wq': _L2_xattn_in['e_wq'], 'L2_xattn_e_wk': _L2_xattn_in['e_wk'], 'L2_xattn_e_wv': _L2_xattn_in['e_wv'], 'L2_xattn_e_wm': _L2_xattn_in['e_wm'], 'L2_xattn_e_w1': _L2_xattn_in['e_w1'], 'L2_xattn_e_w2': _L2_xattn_in['e_w2'], 'L2_xattn_e_g1': _L2_xattn_in['e_g1'], 'L2_xattn_e_b1': _L2_xattn_in['e_b1'], 'L2_xattn_e_g2': _L2_xattn_in['e_g2'], 'L2_xattn_e_b2': _L2_xattn_in['e_b2'], 'L2_xattn_d_wq0': _L2_xattn_in['d_wq0'], 'L2_xattn_d_wk0': _L2_xattn_in['d_wk0'], 'L2_xattn_d_wv0': _L2_xattn_in['d_wv0'], 'L2_xattn_d_wm0': _L2_xattn_in['d_wm0'], 'L2_xattn_d_wq1': _L2_xattn_in['d_wq1'], 'L2_xattn_d_wk1': _L2_xattn_in['d_wk1'], 'L2_xattn_d_wv1': _L2_xattn_in['d_wv1'], 'L2_xattn_d_wm1': _L2_xattn_in['d_wm1'], 'L2_xattn_d_w1': _L2_xattn_in['d_w1'], 'L2_xattn_d_w2': _L2_xattn_in['d_w2'], 'L2_xattn_d_g0': _L2_xattn_in['d_g0'], 'L2_xattn_d_b0': _L2_xattn_in['d_b0'], 'L2_xattn_d_g1': _L2_xattn_in['d_g1'], 'L2_xattn_d_b1': _L2_xattn_in['d_b1'], 'L2_xattn_d_g2': _L2_xattn_in['d_g2'], 'L2_xattn_d_b2': _L2_xattn_in['d_b2'], 'L3_xattn_A': _L3_xattn_in['A'], 'L3_xattn_Bmat': _L3_xattn_in['Bmat'], 'L3_xattn_Cmat': _L3_xattn_in['Cmat'], 'L3_xattn_W_in': _L3_xattn_in['W_in'], 'L3_xattn_b_in': _L3_xattn_in['b_in'], 'L3_xattn_W_qkv': _L3_xattn_in['W_qkv'], 'L3_xattn_b_qkv': _L3_xattn_in['b_qkv'], 'L3_xattn_W_o': _L3_xattn_in['W_o'], 'L3_xattn_b_o': _L3_xattn_in['b_o'], 'L3_xattn_W_prog': _L3_xattn_in['W_prog'], 'L3_xattn_b_prog': _L3_xattn_in['b_prog'], 'L3_xattn_g1': _L3_xattn_in['g1'], 'L3_xattn_beta1': _L3_xattn_in['beta1'], 'L3_xattn_g2': _L3_xattn_in['g2'], 'L3_xattn_beta2': _L3_xattn_in['beta2']}

def reference(x, ctx_1024, itok_BxS2_4_31999, ctxb_2048x64, mask_BxS2_bf1, mask_BxS_ik0, L0_xattn_sa_wq, L0_xattn_sa_bq, L0_xattn_sa_wk, L0_xattn_sa_bk, L0_xattn_sa_wv, L0_xattn_sa_bv, L0_xattn_sa_wo, L0_xattn_sa_bo, L0_xattn_ca_wq, L0_xattn_ca_bq, L0_xattn_ca_wk, L0_xattn_ca_bk, L0_xattn_ca_wv, L0_xattn_ca_bv, L0_xattn_ca_wo, L0_xattn_ca_bo, L0_xattn_ffn_w1, L0_xattn_ffn_b1, L0_xattn_ffn_w2, L0_xattn_ffn_b2, L0_xattn_ln1_g, L0_xattn_ln1_b, L0_xattn_ln2_g, L0_xattn_ln2_b, L0_xattn_ln3_g, L0_xattn_ln3_b, L1_xattn_Wq, L1_xattn_bq, L1_xattn_Wk, L1_xattn_bk, L1_xattn_Wv, L1_xattn_bv, L2_xattn_e_wq, L2_xattn_e_wk, L2_xattn_e_wv, L2_xattn_e_wm, L2_xattn_e_w1, L2_xattn_e_w2, L2_xattn_e_g1, L2_xattn_e_b1, L2_xattn_e_g2, L2_xattn_e_b2, L2_xattn_d_wq0, L2_xattn_d_wk0, L2_xattn_d_wv0, L2_xattn_d_wm0, L2_xattn_d_wq1, L2_xattn_d_wk1, L2_xattn_d_wv1, L2_xattn_d_wm1, L2_xattn_d_w1, L2_xattn_d_w2, L2_xattn_d_g0, L2_xattn_d_b0, L2_xattn_d_g1, L2_xattn_d_b1, L2_xattn_d_g2, L2_xattn_d_b2, L3_xattn_A, L3_xattn_Bmat, L3_xattn_Cmat, L3_xattn_W_in, L3_xattn_b_in, L3_xattn_W_qkv, L3_xattn_b_qkv, L3_xattn_W_o, L3_xattn_b_o, L3_xattn_W_prog, L3_xattn_b_prog, L3_xattn_g1, L3_xattn_beta1, L3_xattn_g2, L3_xattn_beta2):
    import jax
    import jax.numpy as jnp

    def _L0_xattn_ref(input, encoder_output, src_mask, trg_mask, sa_wq, sa_bq, sa_wk, sa_bk, sa_wv, sa_bv, sa_wo, sa_bo, ca_wq, ca_bq, ca_wk, ca_bk, ca_wv, ca_bv, ca_wo, ca_bo, ffn_w1, ffn_b1, ffn_w2, ffn_b2, ln1_g, ln1_b, ln2_g, ln2_b, ln3_g, ln3_b):
        import jax, jax.numpy as jnp
        import numpy as np
        import math
        E = 128
        H = 16
        DK = 64
        DV = 64
        B = 2
        S = 256
        NEG_INF = float('-inf')

        def _layer_norm(x, gamma, beta, eps=1e-12):
            mean = x.mean(-1, keepdims=True)
            var = ((x - mean) ** 2).mean(-1, keepdims=True)
            return gamma * (x - mean) / jnp.sqrt(var + eps) + beta

        def _mha(q_in, k_in, v_in, wq, bq, wk, bk, wv, bv, wo, bo, padding_mask, causal):
            Bq, Sq, _ = q_in.shape
            Sk = k_in.shape[1]
            q = (q_in @ wq + bq).reshape(Bq, Sq, H, DK).transpose(0, 2, 1, 3)
            k = (k_in @ wk + bk).reshape(Bq, Sk, H, DK).transpose(0, 2, 1, 3)
            v = (v_in @ wv + bv).reshape(Bq, Sk, H, DV).transpose(0, 2, 1, 3)
            scores = jnp.einsum('bhqd,bhkd->bhqk', q, k)
            if causal:
                causal_mask = jnp.triu(jnp.ones((Sq, Sk), dtype=bool), k=1)
                scores = jnp.where(causal_mask[None, None], NEG_INF, scores)
            if padding_mask is not None:
                scores = jnp.where(padding_mask[:, None, None, :], scores, NEG_INF)
            attn = jax.nn.softmax(scores / math.sqrt(DK), axis=-1)
            attn = jnp.nan_to_num(attn, nan=0.0, posinf=0.0, neginf=0.0)
            out = jnp.einsum('bhqk,bhkd->bhqd', attn, v)
            out = out.transpose(0, 2, 1, 3).reshape(Bq, Sq, H * DV)
            return out @ wo + bo
        residual = input
        sa = _mha(input, input, input, sa_wq, sa_bq, sa_wk, sa_bk, sa_wv, sa_bv, sa_wo, sa_bo, trg_mask, causal=True)
        x = _layer_norm(sa + residual, ln1_g, ln1_b)
        residual = x
        ca = _mha(x, encoder_output, encoder_output, ca_wq, ca_bq, ca_wk, ca_bk, ca_wv, ca_bv, ca_wo, ca_bo, src_mask, causal=False)
        x = _layer_norm(ca + residual, ln2_g, ln2_b)
        residual = x
        h = jax.nn.relu(x @ ffn_w1 + ffn_b1)
        x = _layer_norm(h @ ffn_w2 + ffn_b2 + residual, ln3_g, ln3_b)
        return x

    def _L1_xattn_ref(queries, keys, values, attention_mask, Wq, bq, Wk, bk, Wv, bv):
        import jax, jax.numpy as jnp
        import numpy as np
        B, S, D, H = (2, 256, 128, 16)
        HD = D // H

        def _split_heads(x):
            b, s, d = x.shape
            return x.reshape(b, s, H, HD).transpose(0, 2, 1, 3)
        q = jax.nn.relu(queries @ Wq.T + bq)
        k = jax.nn.relu(keys @ Wk.T + bk)
        v = jax.nn.relu(values @ Wv.T + bv)
        qh, kh, vh = (_split_heads(q), _split_heads(k), _split_heads(v))
        score = jnp.einsum('bhqd,bhkd->bhqk', qh, kh) / jnp.sqrt(jnp.float32(HD))
        row_mask = (attention_mask == 0)[:, None, :, None]
        score = jnp.where(row_mask, jnp.float32(-1000000000.0), score)
        attn = jax.nn.softmax(score, axis=-1)
        a = jnp.einsum('bhqk,bhkd->bhqd', attn, vh)
        a = a.transpose(0, 1, 3, 2).reshape(q.shape[0], q.shape[1], q.shape[2])
        return a + queries

    def _L2_xattn_ref(depth_feat, context_feat, depth_pos, e_wq, e_wk, e_wv, e_wm, e_w1, e_w2, e_g1, e_b1, e_g2, e_b2, d_wq0, d_wk0, d_wv0, d_wm0, d_wq1, d_wk1, d_wv1, d_wm1, d_w1, d_w2, d_g0, d_b0, d_g1, d_b1, d_g2, d_b2):
        import jax, jax.numpy as jnp
        import numpy as np
        N, L, C, NHEAD = (4, 256, 128, 8)
        D = C // NHEAD
        EPS_ATTN = 1e-06
        EPS_LN = 1e-05

        def _w(key, shape, scale=0.02):
            return jax.random.normal(key, shape, dtype=jnp.float32) * scale

        def layernorm(x, g, b):
            m = jnp.mean(x, axis=-1, keepdims=True)
            v = jnp.mean(jnp.square(x - m), axis=-1, keepdims=True)
            return (x - m) * jax.lax.rsqrt(v + EPS_LN) * g + b

        def linear_attention(q, k, v):
            Q = jax.nn.elu(q) + 1.0
            K = jax.nn.elu(k) + 1.0
            vlen = v.shape[1]
            v = v / vlen
            KV = jnp.einsum('nshd,nshv->nhdv', K, v)
            Z = 1.0 / (jnp.einsum('nlhd,nhd->nlh', Q, K.sum(axis=1)) + EPS_ATTN)
            out = jnp.einsum('nlhd,nhdv,nlh->nlhv', Q, KV, Z) * vlen
            return out

        def heads(x):
            n, l, c = x.shape
            return x.reshape(n, l, NHEAD, D)

        def encoder_layer(x, wq, wk, wv, wm, w1, w2, g1, b1, g2, b2):
            n, l, c = x.shape
            msg = linear_attention(heads(x @ wq), heads(x @ wk), heads(x @ wv))
            msg = msg.reshape(n, l, c) @ wm
            x = x + layernorm(msg, g1, b1)
            x = x + layernorm(jax.nn.relu(x @ w1) @ w2, g2, b2)
            return x

        def decoder_layer(x, src, wq0, wk0, wv0, wm0, wq1, wk1, wv1, wm1, w1, w2, g0, b0, g1, b1, g2, b2):
            n, l, c = x.shape
            msg = linear_attention(heads(x @ wq0), heads(x @ wk0), heads(x @ wv0))
            msg = msg.reshape(n, l, c) @ wm0
            x = x + layernorm(msg, g0, b0)
            msg = linear_attention(heads(x @ wq1), heads(src @ wk1), heads(src @ wv1))
            msg = msg.reshape(n, l, c) @ wm1
            x = x + layernorm(msg, g1, b1)
            x = x + layernorm(jax.nn.relu(x @ w1) @ w2, g2, b2)
            return x
        ctx = context_feat + depth_pos
        ctx = encoder_layer(ctx, e_wq, e_wk, e_wv, e_wm, e_w1, e_w2, e_g1, e_b1, e_g2, e_b2)
        out = decoder_layer(depth_feat, ctx, d_wq0, d_wk0, d_wv0, d_wm0, d_wq1, d_wk1, d_wv1, d_wm1, d_w1, d_w2, d_g0, d_b0, d_g1, d_b1, d_g2, d_b2)
        return out

    def _L3_xattn_ref(builder_state, base_state, input_ids, program_probs, A, Bmat, Cmat, W_in, b_in, W_qkv, b_qkv, W_o, b_o, W_prog, b_prog, g1, beta1, g2, beta2):
        import jax, jax.numpy as jnp
        import numpy as np
        BATCH, T, H, S, P, NH = (4, 256, 128, 64, 64, 8)
        HD = H // NH

        def _layernorm(x, g, b):
            mu = jnp.mean(x, axis=-1, keepdims=True)
            var = jnp.mean((x - mu) ** 2, axis=-1, keepdims=True)
            return (x - mu) * jax.lax.rsqrt(var + 1e-05) * g + b

        def _mha(q_in, kv_in, W_qkv, b_qkv, W_o, b_o):
            Wq, Wk, Wv = jnp.split(W_qkv, 3, axis=0)
            bq, bk, bv = jnp.split(b_qkv, 3, axis=0)

            def heads(x, W, b):
                y = x @ W.T + b
                return y.reshape(y.shape[0], y.shape[1], NH, HD).transpose(0, 2, 1, 3)
            q, k, v = (heads(q_in, Wq, bq), heads(kv_in, Wk, bk), heads(kv_in, Wv, bv))
            scores = jnp.einsum('bhqd,bhkd->bhqk', q, k) * (1.0 / np.sqrt(HD))
            attn = jax.nn.softmax(scores, axis=-1)
            out = jnp.einsum('bhqk,bhkd->bhqd', attn, v)
            out = out.transpose(0, 2, 1, 3).reshape(q_in.shape)
            return out @ W_o.T + b_o
        residual = builder_state
        x = _layernorm(builder_state, g1, beta1)
        base_n = _layernorm(base_state, g1, beta1)
        x = residual + _mha(x, base_n, W_qkv, b_qkv, W_o, b_o)
        residual = x
        xn = _layernorm(x, g2, beta2)
        U = (xn @ W_in.T + b_in) @ Bmat

        def step(s, u_t):
            s = jax.nn.silu(s @ A.T) + u_t
            return (s, s)
        _, states = jax.lax.scan(step, jnp.zeros((builder_state.shape[0], S), U.dtype), U.transpose(1, 0, 2))
        ssm_out = jnp.einsum('tbs,sh->bth', states, Cmat)
        x = residual + ssm_out
        mod = program_probs.mean(axis=1) @ W_prog.T + b_prog
        return x + mod[:, None, :]
    x = _L0_xattn_ref(x, ctx_1024, mask_BxS2_bf1, mask_BxS2_bf1, L0_xattn_sa_wq, L0_xattn_sa_bq, L0_xattn_sa_wk, L0_xattn_sa_bk, L0_xattn_sa_wv, L0_xattn_sa_bv, L0_xattn_sa_wo, L0_xattn_sa_bo, L0_xattn_ca_wq, L0_xattn_ca_bq, L0_xattn_ca_wk, L0_xattn_ca_bk, L0_xattn_ca_wv, L0_xattn_ca_bv, L0_xattn_ca_wo, L0_xattn_ca_bo, L0_xattn_ffn_w1, L0_xattn_ffn_b1, L0_xattn_ffn_w2, L0_xattn_ffn_b2, L0_xattn_ln1_g, L0_xattn_ln1_b, L0_xattn_ln2_g, L0_xattn_ln2_b, L0_xattn_ln3_g, L0_xattn_ln3_b)
    x = _L1_xattn_ref(x, ctx_1024, ctx_1024, mask_BxS_ik0, L1_xattn_Wq, L1_xattn_bq, L1_xattn_Wk, L1_xattn_bk, L1_xattn_Wv, L1_xattn_bv)
    x = _L2_xattn_ref(x, ctx_1024, ctx_1024, L2_xattn_e_wq, L2_xattn_e_wk, L2_xattn_e_wv, L2_xattn_e_wm, L2_xattn_e_w1, L2_xattn_e_w2, L2_xattn_e_g1, L2_xattn_e_b1, L2_xattn_e_g2, L2_xattn_e_b2, L2_xattn_d_wq0, L2_xattn_d_wk0, L2_xattn_d_wv0, L2_xattn_d_wm0, L2_xattn_d_wq1, L2_xattn_d_wk1, L2_xattn_d_wv1, L2_xattn_d_wm1, L2_xattn_d_w1, L2_xattn_d_w2, L2_xattn_d_g0, L2_xattn_d_b0, L2_xattn_d_g1, L2_xattn_d_b1, L2_xattn_d_g2, L2_xattn_d_b2)
    x = _L3_xattn_ref(x, ctx_1024, itok_BxS2_4_31999, ctxb_2048x64, L3_xattn_A, L3_xattn_Bmat, L3_xattn_Cmat, L3_xattn_W_in, L3_xattn_b_in, L3_xattn_W_qkv, L3_xattn_b_qkv, L3_xattn_W_o, L3_xattn_b_o, L3_xattn_W_prog, L3_xattn_b_prog, L3_xattn_g1, L3_xattn_beta1, L3_xattn_g2, L3_xattn_beta2)
    return x

_drawn_inputs = setup_inputs


def setup_inputs(seed=0):
    import zlib

    import numpy as np

    out = dict(_drawn_inputs(seed))
    spreads = {'L0_xattn_sa_bq': (0.0, 0.8),
     'L0_xattn_sa_bk': (0.0, 2.0),
     'L0_xattn_sa_bv': (0.0, 0.1),
     'L0_xattn_sa_bo': (0.0, 0.1),
     'L0_xattn_ca_bq': (0.0, 0.8),
     'L0_xattn_ca_bk': (0.0, 2.0),
     'L0_xattn_ca_bv': (0.0, 0.1),
     'L0_xattn_ca_bo': (0.0, 0.1),
     'L0_xattn_ffn_b1': (0.0, 0.1),
     'L0_xattn_ffn_b2': (0.0, 0.1),
     'L0_xattn_ln1_g': (1.0, 0.2),
     'L0_xattn_ln1_b': (0.0, 0.1),
     'L0_xattn_ln2_g': (1.0, 0.2),
     'L0_xattn_ln2_b': (0.0, 0.1),
     'L0_xattn_ln3_g': (1.0, 0.2),
     'L0_xattn_ln3_b': (0.0, 0.1),
     'L1_xattn_bq': (0.0, 0.8),
     'L1_xattn_bk': (0.0, 2.0),
     'L1_xattn_bv': (0.0, 0.326),
     'L2_xattn_e_g1': (1.0, 0.2),
     'L2_xattn_e_b1': (0.0, 0.1),
     'L2_xattn_e_g2': (1.0, 0.2),
     'L2_xattn_e_b2': (0.0, 0.1),
     'L2_xattn_d_g0': (1.0, 0.2),
     'L2_xattn_d_b0': (0.0, 0.1),
     'L2_xattn_d_g1': (1.0, 0.2),
     'L2_xattn_d_b1': (0.0, 0.1),
     'L2_xattn_d_g2': (1.0, 0.2),
     'L2_xattn_d_b2': (0.0, 0.1),
     'L3_xattn_b_in': (0.0, 0.1),
     'L3_xattn_b_qkv': (0.0, 0.1),
     'L3_xattn_b_o': (0.0, 0.1),
     'L3_xattn_b_prog': (0.0, 0.1),
     'L3_xattn_g1': (1.0, 0.2),
     'L3_xattn_beta1': (0.0, 0.1),
     'L3_xattn_g2': (1.0, 0.2),
     'L3_xattn_beta2': (0.0, 0.1)}
    factors = {'L0_xattn_sa_wq': 8.0,
     'L0_xattn_sa_wk': 8.0,
     'L0_xattn_ca_wq': 8.0,
     'L0_xattn_ca_wk': 8.0,
     'L1_xattn_Wq': 5.381,
     'L1_xattn_Wk': 4.617,
     'L2_xattn_e_wq': 65.461,
     'L2_xattn_e_wk': 4.135,
     'L2_xattn_d_wq0': 8.0,
     'L2_xattn_d_wk0': 5.551,
     'L2_xattn_d_wq1': 8.0,
     'L2_xattn_d_wk1': 4.127}
    for name, (base, spread) in spreads.items():
        noise = np.random.default_rng([zlib.crc32(name.encode()), seed]).standard_normal(out[name].shape)
        drawn = base * np.exp(spread * noise) if base else spread * noise
        out[name] = jnp.asarray(drawn.astype(out[name].dtype))
    for name, factor in factors.items():
        out[name] = (out[name] * factor).astype(out[name].dtype)
    return out
```

```python
from contextlib import ExitStack

import numpy as np
import concourse.bass as bass
from concourse import mybir

F32 = mybir.dt.float32
BF16 = mybir.dt.bfloat16
I32 = mybir.dt.int32
U8 = mybir.dt.uint8
ALU = mybir.AluOpType
ACT = mybir.ActivationFunctionType
AX = mybir.AxisListType

B, T, E = 32, 128, 128
G = 4
GROUPS = B // G
GT = G * T
H0, D0 = 16, 64
C0 = H0 * D0 // 128
H1, D1 = 16, 8
H2, D2 = 8, 16
H3, D3 = 8, 16
FC0 = 4
FC2 = 2
NS = 64
NP = 64
BIG = 2.0 ** 100
QUADS = 4 * G
ATTENTIONS = {"sa": (4, 65), "ca": (4, 65), "l1": (4, 9), "l3": (2, 17)}


QKV = [(k, c) for c in range(C0) for k in "qvk"]
TAG_MAX = {"sa": 0, "ca": 1, "l1": 2, "l3": 3}


def plan(last_stage=99):
    order = []

    def ring(names):
        for n, name in enumerate(names):
            order.append((name, n % 8, "AD"[n % 2]))

    def projections(tag):
        for n, (k, c) in enumerate(QKV):
            order.append(((tag, k, c), n % 8, "D" if k == "v" or c % 4 == 3 else "A"))

    def attention(tag):
        turns = [0]

        def turn(name):
            order.append((name, 4 + turns[0] % 2, "DA"[turns[0] % 2]))
            turns[0] += 1

        def out(u):
            if tag in ("sa", "ca"):
                order.append(((tag, "o", u), 6 + u % 2, "D"))
            elif u % 4 == 3:
                order.append(((tag, "o", u // 4), 6 + (u // 4) % 2, "D"))

        for u in (0, 1):
            order.append(((tag, "s", u), u, "A"))
        for p in range(QUADS // 2):
            if 2 * p + 2 < QUADS:
                for u in (2 * p + 2, 2 * p + 3):
                    order.append(((tag, "s", u), u % 4, "A"))
            turn((tag, "t", 2 * p))
            if p:
                out(2 * p - 1)
            turn((tag, "t", 2 * p + 1))
            out(2 * p)
            if tag in ("sa", "ca") and p % 2 == 0 and p:
                turn((tag, "ot", 2 * (p // 2 - 1)))
                turn((tag, "ot", 2 * (p // 2 - 1) + 1))
        out(QUADS - 1)
        if tag in ("sa", "ca"):
            turn((tag, "ot", 2 * G - 2))
            turn((tag, "ot", 2 * G - 1))

    def norm(tag):
        order.append(((tag, "y"), 0, "D"))
        order.append(((tag, "n"), 1, "D"))

    ring([("in", n) for n in range(2)])
    projections("sa")
    attention("sa")
    norm("ln1")
    projections("ca")
    attention("ca")
    norm("ln2")
    ring([("ffn", c) for c in range(FC0)])
    norm("ln3")
    order.append((("l1", "q"), 0, "D"))
    order.append((("l1", "k"), 1, "A"))
    order.append((("l1", "v"), 2, "A"))
    attention("l1")
    for blk in ("en", "d0", "d1"):
        order.append(((blk, "q"), 0, "D"))
        order.append(((blk, "k"), 1, "D"))
        order.append(((blk, "v"), 2, "A"))
        for n in range(2):
            order.append(((blk, "kv", n), 3 + n, "D"))
        for n in range(2):
            order.append(((blk, "o", n), 5 + n, "D"))
        order.append(((blk, "ot"), 7, "A"))
        norm(blk)
        if blk in ("en", "d1"):
            for c in range(FC2):
                order.append(((blk, "f", c), 2 + c, "A"))
            norm(blk + "f")
    for n, blk in enumerate(("b3", "x3")):
        order.append(((blk, "y"), 0 + 2 * n, "D"))
        order.append(((blk, "n"), 1 + 2 * n, "D"))
    order.append((("l3", "q"), 4, "D"))
    order.append((("l3", "k"), 5, "A"))
    order.append((("l3", "v"), 6, "A"))
    attention("l3")
    order.append((("l3", "ot"), 0, "A"))
    order.append((("l3", "x"), 1, "D"))
    order.append((("z3", "y"), 2, "D"))
    order.append((("z3", "n"), 3, "D"))
    order.append((("l3", "z"), 4, "A"))
    order.append((("l3", "u"), 5, "D"))
    return order


PLAN = plan()
FILL = {name: n + 1 for n, (name, _, _) in enumerate(PLAN)}
BANK = {name: bank for name, bank, _ in PLAN}
BY = {name: by for name, _, by in PLAN}
RANK = {}
for _name, _bank, _by in PLAN:
    RANK[_name] = 1 + sum(1 for other in RANK if BY[other] == _by)
FILLS = len(PLAN)
EMPTIES = {by: sum(1 for x in PLAN if x[2] == by) for by in "AD"}

LN_TAGS = ("ln1", "ln2", "ln3", "en", "enf", "d0", "d1", "d1f", "b3", "x3", "z3")
COLUMNS = ("L0_xattn_sa_bq", "L0_xattn_sa_bk", "L0_xattn_ca_bq", "L0_xattn_ca_bk", "L0_xattn_ffn_b1")
VECTORS = ("L0_xattn_ln1_g", "L0_xattn_ln1_b", "L0_xattn_ln2_g", "L0_xattn_ln2_b", "L0_xattn_ln3_g",
           "L0_xattn_ln3_b", "L1_xattn_bq", "L1_xattn_bk", "L2_xattn_e_g1", "L2_xattn_e_b1",
           "L2_xattn_e_g2", "L2_xattn_e_b2", "L2_xattn_d_g0", "L2_xattn_d_b0", "L2_xattn_d_g1",
           "L2_xattn_d_b1", "L2_xattn_d_g2", "L2_xattn_d_b2", "L3_xattn_b_in", "L3_xattn_b_o",
           "L3_xattn_b_prog", "L3_xattn_g1", "L3_xattn_beta1", "L3_xattn_g2", "L3_xattn_beta2")
COLUMN_WIDTH = {n: FC0 if n.endswith("ffn_b1") else C0 for n in COLUMNS}
COLUMN_WIDTH["L3_xattn_b_qkv"] = 3
COLUMN_WIDTH.update({n: 1 for n in VECTORS})
COLUMN_AT, NCOLS = {}, 0
for _name, _width in COLUMN_WIDTH.items():
    COLUMN_AT[_name] = NCOLS
    NCOLS += _width
ROWS = ("L0_xattn_sa_bo", "L0_xattn_ca_bo", "L0_xattn_ffn_b2", "L1_xattn_bv")
GB = {"ln1": ("L0_xattn_ln1_g", "L0_xattn_ln1_b"), "ln2": ("L0_xattn_ln2_g", "L0_xattn_ln2_b"),
      "ln3": ("L0_xattn_ln3_g", "L0_xattn_ln3_b"), "en": ("L2_xattn_e_g1", "L2_xattn_e_b1"),
      "enf": ("L2_xattn_e_g2", "L2_xattn_e_b2"), "d0": ("L2_xattn_d_g0", "L2_xattn_d_b0"),
      "d1": ("L2_xattn_d_g1", "L2_xattn_d_b1"), "d1f": ("L2_xattn_d_g2", "L2_xattn_d_b2"),
      "b3": ("L3_xattn_g1", "L3_xattn_beta1"), "x3": ("L3_xattn_g1", "L3_xattn_beta1"),
      "z3": ("L3_xattn_g2", "L3_xattn_beta2")}
EPS = {"ln1": 1e-12, "ln2": 1e-12, "ln3": 1e-12}
SQUARES = ("L2_xattn_e_wq", "L2_xattn_e_wk", "L2_xattn_e_wv", "L2_xattn_e_wm", "L2_xattn_d_wq0",
           "L2_xattn_d_wk0", "L2_xattn_d_wv0", "L2_xattn_d_wm0", "L2_xattn_d_wq1", "L2_xattn_d_wk1",
           "L2_xattn_d_wv1", "L2_xattn_d_wm1")
L2W = {"en": "L2_xattn_e_w{}", "d0": "L2_xattn_d_w{}0", "d1": "L2_xattn_d_w{}1"}
TURNED = (("L1_xattn_Wq", 128, 128, 0), ("L1_xattn_Wk", 128, 128, 0), ("L1_xattn_Wv", 128, 128, 0),
          ("L3_xattn_W_qkv", 128, 128, 0), ("L3_xattn_W_qkv", 128, 128, 128),
          ("L3_xattn_W_qkv", 128, 128, 256), ("L3_xattn_W_o", 128, 128, 0),
          ("L3_xattn_W_in", 128, 128, 0), ("L3_xattn_W_prog", 128, 64, 0), ("L3_xattn_A", 64, 64, 0))
TURN = {(n, r0): k for k, (n, _, _, r0) in enumerate(TURNED)}

VSTEPS = 106
SETUP_VSTEPS = 20
PSTEPS = len(LN_TAGS)


def build_program(nc, I, out):
    with ExitStack() as ctx:
        def sb(name, shape, dt=F32):
            return ctx.enter_context(nc.sbuf_tensor(name, shape, dt))

        def sem(name):
            return ctx.enter_context(nc.semaphore(name))

        ps = ctx.enter_context(nc.psum_tensor("ps", [128, 8, 512], F32))

        ident = sb("ident", [128, 128])
        ident_h = sb("ident_h", [128, 128], BF16)
        causal = sb("causal", [128, 128], BF16)
        causal_f = sb("causal_f", [128, 128])
        block16 = sb("block16", [128, 128])
        head16 = sb("head16", [128, 8])
        head8 = sb("head8", [128, 16])
        quad8 = sb("quad8", [128, 4])
        quad16 = sb("quad16", [128, 2])
        ones_row = sb("ones_row", [1, 128])
        mean_col = sb("mean_col", [128, 1])
        minus_half = sb("minus_half", [128, G])
        w_qkv = {t: sb(f"w_qkv_{t}", [128, 3, H0 * D0]) for t in ("sa", "ca")}
        w_o = {t: sb(f"w_o_{t}", [128, C0, E]) for t in ("sa", "ca")}
        bv_all = {t: sb(f"bv_all_{t}", [128, H0 * D0]) for t in ("sa", "ca")}
        w_f1 = sb("w_f1", [128, FC0 * 128])
        w_f2 = sb("w_f2", [128, FC0, E])
        w_sq = sb("w_sq", [128, len(SQUARES), 128])
        w_l2f1 = {b: sb(f"w_l2f1_{b}", [128, FC2 * 128]) for b in ("en", "d1")}
        w_l2f2 = {b: sb(f"w_l2f2_{b}", [128, FC2, E]) for b in ("en", "d1")}
        turned = sb("turned", [128, len(TURNED), 128])
        w_b = sb("w_b", [128, NS])
        w_c = sb("w_c", [NS, E])
        col_rows = sb("col_rows", [NCOLS, 128])
        col_all = sb("col_all", [128, NCOLS])
        cols = {n: col_all[:, COLUMN_AT[n]:COLUMN_AT[n] + w] for n, w in COLUMN_WIDTH.items()}
        qkvb = cols["L3_xattn_b_qkv"]
        rows = sb("rows", [1, len(ROWS) + 1, 128])
        scaled_bq = {t: sb(f"scaled_bq_{t}", [128, C0]) for t in ("sa", "ca")}
        x_in = sb("x_in", [128, G, E])
        c_in = sb("c_in", [128, G, E])
        valid_in = sb("valid_in", [128, GT], U8)
        skip_in = sb("skip_in", [128, GT], I32)
        cT = sb("cT", [128, GT])
        xT = {n: sb("xT" + n, [128, GT]) for n in ("a", "b")}
        big1 = sb("big1", [128, C0, GT])
        big2 = sb("big2", [128, C0, GT])
        values = sb("values", [128, G, H0, D0 + 1])
        mask_sa = sb("mask_sa", [128, G, T], BF16)
        mask_ca = sb("mask_ca", [128, G, T], BF16)
        row_ok = {"sa": sb("row_ok_sa", [128, G]), "ca": sb("row_ok_ca", [128, G])}
        attend = sb("attend", [128, GT])
        neg_max = sb("neg_max", [128, QUADS, 4])
        probs = sb("probs", [128, 4, 512])
        probsT = sb("probsT", [128, 2, 512])
        inv = sb("inv", [128, 2, 16])
        heads = sb("heads", [128, 2, H0 * D0])
        stats = sb("stats", [128, G, 6])
        meanvar = sb("meanvar", [128, G, 2])
        var_eps = sb("var_eps", [128, G])
        scratch = sb("scratch", [128, 1])
        rstd = sb("rstd", [128, G])
        normed = sb("normed", [128, G, E])
        hidden = sb("hidden", [128, FC0, GT])
        x2_all = sb("x2_all", [128, B * T])
        u_all = sb("u_all", [NS, T, B])
        prog_in = hidden[:, :, :].rearrange("p c n -> p (c n)").rearrange("p (b n) -> p b n", b=B)
        prog_mean = sb("prog_mean", [NP, B])
        mod = sb("mod", [128, B])
        state = sb("state", [NS, 2, B])

        l1q, l1k0 = big2[:, 0, :], big2[:, 1, :]
        kx = big2[:, 2:6, :]
        l1v = values[:, :, :, 0:D1 + 1]
        x1T = big2[:, 6, :]
        c2T = big2[:, 7, :]
        encT = xT["a"]
        l2qT, l2k = big2[:, 0, :], big2[:, 1, :]
        l2t = big2[:, 2, :]
        l2e = big2[:, 3, :]
        l2m = big2[:, 4, :]
        l2mT = big2[:, 5, :]
        l2v = values[:, :, 0:2, :].rearrange("p g a b -> p g (a b)")[:, :, 0:129]
        kvb = hidden[:, 2:4, :].rearrange("p a n -> p (a n)")[:, 0:G * 136].rearrange(
            "p (g n) -> p g n", g=G)
        l3x, l3b = hidden[:, 0, :], hidden[:, 1, :]
        l3v = values[:, :, 0:H3, 0:D3 + 1]
        l2z = sb("l2z", [128, 2, 2 * H2])

        loaded_first = sem("loaded_first")
        loaded_rest = sem("loaded_rest")
        group_in = sem("group_in")
        masks_taken = sem("masks_taken")
        keys_ready = sem("keys_ready")
        neg_ready = sem("neg_ready")
        consts_ready = sem("consts_ready")
        filled = sem("filled")
        emptied = {"A": sem("emptied_by_scalar"), "D": sem("emptied_by_vector")}
        max_ready = sem("max_ready")
        exp_ready = sem("exp_ready")
        vector_step = sem("vector_step")
        stats_ready = sem("stats_ready")
        rstd_ready = sem("rstd_ready")
        setup_filled = sem("setup_filled")
        setup_emptied = sem("setup_emptied")
        scan_mm = sem("scan_mm")
        scan_silu = sem("scan_silu")
        scan_add = sem("scan_add")
        fin_mm = sem("fin_mm")
        fin_add = sem("fin_add")
        fin_turn = sem("fin_turn")
        fin_copy = sem("fin_copy")
        stored = sem("stored")
        block = ctx.enter_context(nc.Block())

        def v1(name):
            return cols[name]

        def bank(name):
            return ps[:, BANK[name], :]

        def wait_filled(eng, i, name):
            eng.wait_ge(filled, i * FILLS + FILL[name])

        def wait_emptied(eng, i, name):
            by = BY[name]
            eng.wait_ge(emptied[by], i * EMPTIES[by] + RANK[name])

        NFIRST = [0]
        NREST = [0]
        NCONST = [0]

        @block.sync
        def _(sp):
            def first(dst, src):
                sp.dma_start(dst, src).then_inc(loaded_first, 16)
                NFIRST[0] += 16

            def rest(dst, src):
                sp.dma_start(dst, src).then_inc(loaded_rest, 16)
                NREST[0] += 16

            def load_group(g):
                sp.dma_start(x_in[:, :, :], I["x"][bass.ds(g * G, G), :, :].rearrange("g t e -> t g e")).then_inc(group_in, 16)
                sp.dma_start(c_in[:, :, :], I["ctx_1024"][bass.ds(g * G, G), :, :].rearrange("g t e -> t g e")).then_inc(group_in, 16)

            def load_masks(g):
                m = I["mask_BxS2_bf1"].rearrange("b t -> (b t)")[bass.ds(g * GT, GT)].partition_broadcast(128)
                sp.dma_start(valid_in[:, :], m).then_inc(group_in, 16)
                m = I["mask_BxS_ik0"].rearrange("b t -> (b t)")[bass.ds(g * GT, GT)].partition_broadcast(128)
                sp.dma_start(skip_in[:, :], m).then_inc(group_in, 16)

            load_group(0)
            load_masks(0)
            for t in ("sa", "ca"):
                for k, n in enumerate("qkv"):
                    first(w_qkv[t][:, k, :], I[f"L0_xattn_{t}_w{n}"])
                first(w_o[t][:, :, :], I[f"L0_xattn_{t}_wo"].rearrange("(c p) n -> p c n", p=128))
                first(bv_all[t][:, :], I[f"L0_xattn_{t}_bv"].partition_broadcast(128))
            for n, w in COLUMN_WIDTH.items():
                first(col_rows[COLUMN_AT[n]:COLUMN_AT[n] + w, :], I[n].rearrange("(c p) -> c p", p=128))
            for k, n in enumerate(ROWS):
                first(rows[:, k, :], I[n].rearrange("(a n) -> a n", a=1))
            first(rows[:, len(ROWS), :], I["L3_xattn_b_qkv"].rearrange("(a n) -> a n", a=1)[:, 256:384])
            first(w_f1[:, :], I["L0_xattn_ffn_w1"])
            first(w_f2[:, :, :], I["L0_xattn_ffn_w2"].rearrange("(c p) n -> p c n", p=128))
            for k, n in enumerate(SQUARES):
                rest(w_sq[:, k, :], I[n])
            for b, n in (("en", "e"), ("d1", "d")):
                rest(w_l2f1[b][:, :], I[f"L2_xattn_{n}_w1"])
                rest(w_l2f2[b][:, :, :], I[f"L2_xattn_{n}_w2"].rearrange("(c p) n -> p c n", p=128))
            rest(w_b[:, :], I["L3_xattn_Bmat"])
            rest(w_c[:, :], I["L3_xattn_Cmat"])
            for k, (n, r, c, r0) in enumerate(TURNED):
                rest(big1[0:r, k // 4, (k % 4) * 128:(k % 4) * 128 + c], I[n][r0:r0 + r, :])
            rest(prog_in, I["ctxb_2048x64"].rearrange("b t n -> t b n"))
            for g in range(1, GROUPS):
                sp.wait_ge(filled, (g - 1) * FILLS + FILL["in", 1])
                load_group(g)
                sp.wait_ge(masks_taken, g)
                load_masks(g)
            o = out.rearrange("b t e -> t b e")
            for g in range(GROUPS):
                sp.wait_ge(fin_copy, g + 1)
                sp.dma_start(o[:, bass.ds(g * G, G), :],
                             x2_all[:, bass.ds(g * GT, GT)].rearrange("p (g e) -> p g e", g=G)).then_inc(stored, 16)
            sp.wait_ge(stored, 16 * GROUPS)

        @block.gpsimd
        def _(pool):
            step = [0]

            def link(ins):
                step[0] += 1
                ins.then_inc(consts_ready, 1)
                pool.wait_ge(consts_ready, step[0])

            def band(m, n, width, dt_fill):
                link(nc.gpsimd.memset(m, dt_fill))
                link(nc.gpsimd.affine_select(out=m, in_=m, compare_op=ALU.is_ge, fill=0.0, base=0,
                                             pattern=[[-width, n]], channel_multiplier=1))
                link(nc.gpsimd.affine_select(out=m, in_=m, compare_op=ALU.is_ge, fill=0.0, base=width - 1,
                                             pattern=[[width, n]], channel_multiplier=-1))

            link(nc.gpsimd.memset(ident[:, :], 0.0))
            link(nc.gpsimd.affine_select(out=ident[:, :], in_=ident[:, :], compare_op=ALU.not_equal, fill=1.0,
                                         base=0, pattern=[[-1, 128]], channel_multiplier=1))
            link(nc.gpsimd.memset(causal_f[:, :], 0.0))
            link(nc.gpsimd.affine_select(out=causal_f[:, :], in_=causal_f[:, :], compare_op=ALU.is_ge, fill=-BIG,
                                         base=0, pattern=[[-1, 128]], channel_multiplier=1))
            band(head16[:, :], 8, 16, 1.0)
            band(head8[:, :], 16, 8, 1.0)
            link(nc.gpsimd.memset(ones_row[:, :], 1.0))
            link(nc.gpsimd.memset(mean_col[:, :], 1.0 / T))
            link(nc.gpsimd.memset(minus_half[:, :], -0.5))
            link(nc.gpsimd.memset(values[:, :, :, D0:D0 + 1], 1.0))
            NCONST[0] = step[0]
            with pool.Fori(0, GROUPS) as i:
                for n, tag in enumerate(LN_TAGS):
                    pool.wait_ge(stats_ready, i * PSTEPS + n + 1)
                    nc.gpsimd.tensor_tensor(rstd[:, :], var_eps[:, :], minus_half[:, :], ALU.pow).then_inc(rstd_ready, 1)

        @block.tensor
        def _(pe):
            mm = nc.tensor.matmul
            pe.wait_ge(loaded_first, NFIRST[0])
            pe.wait_ge(loaded_rest, NREST[0])
            pe.wait_ge(consts_ready, NCONST[0])
            for k, (n, r, c, r0) in enumerate(TURNED):
                last = nc.tensor.transpose(ps[0:c, k // 4, (k % 4) * 128:(k % 4) * 128 + r],
                                           big1[0:r, k // 4, (k % 4) * 128:(k % 4) * 128 + c], ident[0:r, 0:r])
            last.then_inc(setup_filled, 1)
            nc.tensor.transpose(ps[:, 5, 0:NCOLS], col_rows[:, :], ident[0:NCOLS, 0:NCOLS]).then_inc(setup_filled, 1)
            for b in range(B):
                last = mm(ps[0:NP, 3, b:b + 1], prog_in[:, b, :], mean_col[:, :], start=True, stop=True)
            last.then_inc(setup_filled, 1)
            pe.wait_ge(setup_emptied, 1)
            mm(ps[:, 4, 0:B], turned[0:NP, TURN["L3_xattn_W_prog", 0], :], prog_mean[:, :],
               start=True, stop=True).then_inc(setup_filled, 1)
            pe.wait_ge(setup_emptied, 2)

            def turn4(name, src):
                for b in range(G):
                    last = nc.tensor.transpose(bank(name)[:, b * 128:b * 128 + 128], src(b), ident[:, :])
                last.then_inc(filled, 1)

            def attention(i, tag, scores, value):
                hpb, d1 = ATTENTIONS[tag]
                w = hpb * 128

                def pair(p):
                    for u in (2 * p, 2 * p + 1):
                        if u >= 4:
                            wait_emptied(pe, i, (tag, "s", u - 4))
                    scores(i, p)

                def turn(u):
                    wait_emptied(pe, i, (tag, "s", u))
                    if u >= 2:
                        wait_emptied(pe, i, (tag, "t", u - 2))
                    if tag in ("sa", "ca") and u % 4 >= 2 and u >= 6:
                        wait_emptied(pe, i, (tag, "ot", 2 * (u // 4 - 1) + u % 2))
                    name = (tag, "t", u)
                    for h in range(hpb):
                        last = nc.tensor.transpose(bank(name)[:, h * 128:h * 128 + 128],
                                                   probs[:, u % 4, h * 128:h * 128 + 128], ident[:, :])
                    last.then_inc(filled, 1)

                def outp(u):
                    b, q = u // 4, u % 4
                    wait_emptied(pe, i, (tag, "t", u))
                    if tag in ("sa", "ca"):
                        if u >= 2:
                            wait_emptied(pe, i, (tag, "o", u - 2))
                        dst, name = ps[:, BANK[tag, "o", u], 0:hpb * d1], (tag, "o", u)
                    else:
                        if q == 0 and b >= 2:
                            wait_emptied(pe, i, (tag, "o", b - 2))
                        dst, name = ps[:, BANK[tag, "o", b], q * hpb * d1:(q + 1) * hpb * d1], None
                        if q == 3:
                            name = (tag, "o", b)
                    for h in range(hpb):
                        last = mm(dst[:, h * d1:(h + 1) * d1], probsT[:, u % 2, h * 128:h * 128 + 128],
                                  value(b, q, h), start=True, stop=True)
                    if name:
                        last.then_inc(filled, 1)

                def turn_heads(b):
                    for n in range(2):
                        wait_emptied(pe, i, (tag, "o", 4 * b + 3))
                        wait_emptied(pe, i, (tag, "t", min(4 * b + 4, QUADS - 2) + n))
                        name = (tag, "ot", 2 * b + n)
                        turn4(name, lambda c: heads[:, b % 2, (4 * n + c) * 128:(4 * n + c + 1) * 128])

                pair(0)
                for p in range(QUADS // 2):
                    if 2 * p + 2 < QUADS:
                        pair(p + 1)
                    turn(2 * p)
                    if p:
                        outp(2 * p - 1)
                    turn(2 * p + 1)
                    outp(2 * p)
                    if tag in ("sa", "ca") and p % 2 == 0 and p:
                        turn_heads(p // 2 - 1)
                outp(QUADS - 1)
                if tag in ("sa", "ca"):
                    turn_heads(G - 1)

            def scores0(tag):
                mask = mask_sa if tag == "sa" else mask_ca

                def fn(i, p):
                    b, o = p // 2, p % 2
                    for j in range(4):
                        for half in range(2):
                            h = 8 * o + 2 * j + half
                            q = slice(64 * half, 64 * half + 64)
                            col = slice(b * T, b * T + T)
                            mm(bank((tag, "s", 2 * p + half))[:, j * 128:j * 128 + 128],
                               big1[q, h // 2, col], big2[q, h // 2, col], start=(j == 0), stop=False,
                               skip_group_check=True)
                    for half in range(2):
                        mm(bank((tag, "s", 2 * p + half)), ident_h[:, :],
                           mask[:, b, :].unsqueeze(1).broadcast_to([128, 4, T]), start=False, stop=True,
                           skip_group_check=True).then_inc(filled, 1)
                return fn

            def scores_small(tag, width, qT):
                def fn(i, p):
                    for u in (2 * p, 2 * p + 1):
                        b, q = u // 4, u % 4
                        part = slice(32 * q, 32 * q + 32)
                        mm(bank((tag, "s", u))[:, 0:width * 128], qT[part, b * T:b * T + T],
                           kx[part, 0:width, b * T:b * T + T], start=True, stop=True).then_inc(filled, 1)
                return fn

            def norm_in(i, tag, terms, row=None):
                for b in range(G):
                    dst = bank((tag, "y"))[:, b * 128:b * 128 + 128]
                    todo = list(terms(b))
                    if row is not None:
                        todo.append((ones_row[0:1, :], rows[0:1, row, :]))
                    for n, (l, r) in enumerate(todo):
                        last = mm(dst, l, r, start=(n == 0), stop=(n == len(todo) - 1))
                last.then_inc(filled, 1)

            def norm_turn(i, tag):
                wait_emptied(pe, i, (tag, "y"))
                turn4((tag, "n"), lambda b: normed[:, b, :])
                wait_emptied(pe, i, (tag, "n"))

            def qkv0(i, tag, q_src, kv_src):
                w = w_qkv[tag]
                n = [0]

                def one(name, lhs, rhs):
                    if n[0] >= 8:
                        wait_emptied(pe, i, (tag, *QKV[n[0] - 8]))
                    n[0] += 1
                    mm(bank(name), lhs, rhs, start=True, stop=True).then_inc(filled, 1)

                for k, c in QKV:
                    if k == "v":
                        b, half = c // 2, c % 2
                        one((tag, "v", c), kv_src[:, b * T:b * T + T], w[:, 2, half * 512:half * 512 + 512])
                    elif k == "q":
                        one((tag, "q", c), w[:, 0, c * 128:c * 128 + 128], q_src)
                    else:
                        one((tag, "k", c), w[:, 1, c * 128:c * 128 + 128], kv_src)
                wait_emptied(pe, i, (tag, "k", C0 - 2))
                wait_emptied(pe, i, (tag, "k", C0 - 1))

            with pe.Fori(0, GROUPS) as i:
                pe.wait_ge(group_in, i * 64 + 64)
                turn4(("in", 0), lambda b: x_in[:, b, :])
                turn4(("in", 1), lambda b: c_in[:, b, :])
                pe.wait_ge(masks_taken, i + 1)
                wait_emptied(pe, i, ("in", 0))
                wait_emptied(pe, i, ("in", 1))
                qkv0(i, "sa", xT["a"][:, :], xT["a"][:, :])
                attention(i, "sa", scores0("sa"), lambda b, q, h: values[:, b, 8 * (q // 2) + 2 * h + q % 2, :])
                for c in (0, 1):
                    wait_emptied(pe, i, ("sa", "ot", 2 * G - 2 + c))
                norm_in(i, "ln1", lambda b: [(big1[:, c, b * T:b * T + T], w_o["sa"][:, c, :]) for c in range(C0)]
                        + [(xT["a"][:, b * T:b * T + T], ident[:, :])], 0)
                norm_turn(i, "ln1")
                qkv0(i, "ca", xT["b"][:, :], cT[:, :])
                attention(i, "ca", scores0("ca"), lambda b, q, h: values[:, b, 8 * (q // 2) + 2 * h + q % 2, :])
                for c in (0, 1):
                    wait_emptied(pe, i, ("ca", "ot", 2 * G - 2 + c))
                norm_in(i, "ln2", lambda b: [(big1[:, c, b * T:b * T + T], w_o["ca"][:, c, :]) for c in range(C0)]
                        + [(xT["b"][:, b * T:b * T + T], ident[:, :])], 1)
                norm_turn(i, "ln2")
                for c in range(FC0):
                    mm(bank(("ffn", c)), w_f1[:, c * 128:c * 128 + 128], xT["a"][:, :],
                       start=True, stop=True).then_inc(filled, 1)
                for c in (FC0 - 2, FC0 - 1):
                    wait_emptied(pe, i, ("ffn", c))
                norm_in(i, "ln3", lambda b: [(hidden[:, c, b * T:b * T + T], w_f2[:, c, :]) for c in range(FC0)]
                        + [(xT["a"][:, b * T:b * T + T], ident[:, :])], 2)
                norm_turn(i, "ln3")
                wT = lambda n, r0=0: turned[:, TURN[n, r0], :]
                mm(bank(("l1", "q")), wT("L1_xattn_Wq"), xT["b"][:, :], start=True, stop=True).then_inc(filled, 1)
                mm(bank(("l1", "k")), wT("L1_xattn_Wk"), cT[:, :], start=True, stop=True).then_inc(filled, 1)
                for b in range(G):
                    dst = bank(("l1", "v"))[:, b * 128:b * 128 + 128]
                    mm(dst, cT[:, b * T:b * T + T], wT("L1_xattn_Wv"), start=True, stop=False)
                    last = mm(dst, ones_row[0:1, :], rows[0:1, 3, :], start=False, stop=True)
                last.then_inc(filled, 1)
                pe.wait_ge(keys_ready, 2 * i + 1)
                wait_emptied(pe, i, ("l1", "v"))
                wait_emptied(pe, i, ("l1", "q"))
                attention(i, "l1", scores_small("l1", 4, l1q), lambda b, q, h: l1v[:, b, 4 * q + h, :])
                wait_emptied(pe, i, ("l1", "o", G - 1))
                for blk, q_src, kv_src in (("en", c2T, c2T), ("d0", x1T, x1T), ("d1", xT["b"][:, :], encT[:, :])):
                    w = lambda k: w_sq[:, SQUARES.index(L2W[blk].format(k)), :]
                    mm(bank((blk, "q")), w("q"), q_src, start=True, stop=True).then_inc(filled, 1)
                    for k in "kv":
                        for b in range(G):
                            last = mm(bank((blk, k))[:, b * 128:b * 128 + 128], kv_src[:, b * T:b * T + T], w(k),
                                      start=True, stop=True)
                        last.then_inc(filled, 1)
                    wait_emptied(pe, i, (blk, "k"))
                    wait_emptied(pe, i, (blk, "v"))
                    for b in range(G):
                        last = mm(bank((blk, "kv", b // 2))[:, (b % 2) * 129:(b % 2) * 129 + 129],
                                  l2k[:, b * 128:b * 128 + 128], l2v[:, b, :], start=True, stop=True)
                        if b % 2:
                            last.then_inc(filled, 1)
                    for n in range(2):
                        wait_emptied(pe, i, (blk, "kv", n))
                    for b in range(G):
                        last = mm(bank((blk, "o", b // 2))[:, (b % 2) * 136:(b % 2) * 136 + 136],
                                  l2qT[:, b * T:b * T + T], kvb[:, b, :], start=True, stop=True)
                        if b % 2:
                            last.then_inc(filled, 1)
                    for n in range(2):
                        wait_emptied(pe, i, (blk, "o", n))
                    turn4((blk, "ot"), lambda b: l2m[:, b * 128:b * 128 + 128])
                    wait_emptied(pe, i, (blk, "ot"))
                    norm_in(i, blk, lambda b: [(l2mT[:, b * T:b * T + T], w("m"))])
                    norm_turn(i, blk)
                    if blk != "d0":
                        src = encT if blk == "en" else x1T
                        for c in range(FC2):
                            mm(bank((blk, "f", c)), w_l2f1[blk][:, c * 128:c * 128 + 128], src[:, :],
                               start=True, stop=True).then_inc(filled, 1)
                        wait_emptied(pe, i, (blk, "f", FC2 - 1))
                        norm_in(i, blk + "f", lambda b: [(hidden[:, c, b * T:b * T + T], w_l2f2[blk][:, c, :])
                                                         for c in range(FC2)])
                        norm_turn(i, blk + "f")
                turn4(("b3", "y"), lambda b: cT[:, b * T:b * T + T])
                norm_turn(i, "b3")
                turn4(("x3", "y"), lambda b: xT["b"][:, b * T:b * T + T])
                norm_turn(i, "x3")
                mm(bank(("l3", "q")), wT("L3_xattn_W_qkv"), l3x, start=True, stop=True).then_inc(filled, 1)
                mm(bank(("l3", "k")), wT("L3_xattn_W_qkv", 128), l3b, start=True, stop=True).then_inc(filled, 1)
                for b in range(G):
                    dst = bank(("l3", "v"))[:, b * 128:b * 128 + 128]
                    mm(dst, l3b[:, b * T:b * T + T], wT("L3_xattn_W_qkv", 256), start=True, stop=False)
                    last = mm(dst, ones_row[0:1, :], rows[0:1, len(ROWS), :], start=False, stop=True)
                last.then_inc(filled, 1)
                pe.wait_ge(keys_ready, 2 * i + 2)
                wait_emptied(pe, i, ("l3", "v"))
                wait_emptied(pe, i, ("l3", "q"))
                attention(i, "l3", scores_small("l3", 2, l1q), lambda b, q, h: l3v[:, b, 2 * q + h, :])
                wait_emptied(pe, i, ("l3", "o", G - 1))
                turn4(("l3", "ot"), lambda b: l2m[:, b * 128:b * 128 + 128])
                wait_emptied(pe, i, ("l3", "ot"))
                mm(bank(("l3", "x")), wT("L3_xattn_W_o"), l2mT, start=True, stop=True).then_inc(filled, 1)
                wait_emptied(pe, i, ("l3", "x"))
                turn4(("z3", "y"), lambda b: x1T[:, b * T:b * T + T])
                norm_turn(i, "z3")
                mm(bank(("l3", "z")), wT("L3_xattn_W_in"), l3x, start=True, stop=True).then_inc(filled, 1)
                wait_emptied(pe, i, ("l3", "z"))
                mm(ps[0:NS, BANK["l3", "u"], :], w_b[:, :], l2t, start=True, stop=True).then_inc(filled, 1)
                wait_emptied(pe, i, ("l3", "u"))

            aT = turned[0:NS, TURN["L3_xattn_A", 0], :]
            with pe.Fori(1, T) as t:
                pe.wait_ge(scan_add, t)
                mm(ps[:, 0, 0:B], aT, u_all[:, bass.ds(t - 1, 1), :].rearrange("p a b -> p (a b)"),
                   start=True, stop=True).then_inc(scan_mm, 1)
            pe.wait_ge(scan_add, T)
            ub = u_all[:, :, :].rearrange("p t b -> p b t")
            with pe.Fori(0, GROUPS) as g:
                mm(ps[:, 1, :], w_c[:, :], ub[:, bass.ds(g * G, G), :], start=True, stop=True).then_inc(fin_mm, 1)
                pe.wait_ge(fin_add, g + 1)
                for b in range(G):
                    last = nc.tensor.transpose(ps[:, 2, b * 128:b * 128 + 128], cT[:, b * T:b * T + T], ident[:, :])
                last.then_inc(fin_turn, 1)
                pe.wait_ge(fin_copy, g + 1)

        @block.scalar
        def _(act):
            A = nc.scalar.activation
            act.wait_ge(loaded_first, NFIRST[0])
            act.wait_ge(vector_step, SETUP_VSTEPS)

            def take(i, name, fn, width=512):
                wait_filled(act, i, name)
                fn(bank(name)).then_inc(emptied["A"], 1)

            def attention(i, tag):
                hpb, d1 = ATTENTIONS[tag]
                k0 = TAG_MAX[tag]

                def exps(u):
                    act.wait_ge(max_ready, i * 4 * QUADS + k0 * QUADS + u + 1)
                    for h in range(hpb):
                        last = A(probs[:, u % 4, h * 128:h * 128 + 128], bank((tag, "s", u))[:, h * 128:h * 128 + 128],
                                 ACT.Exp, bias=neg_max[:, u, h:h + 1], scale=1.0)
                    last.then_inc(emptied["A"], 1)

                def turn(name, dst, width):
                    if BY[name] == "A":
                        wait_filled(act, i, name)
                        A(dst, bank(name)[:, 0:width], ACT.Copy).then_inc(emptied["A"], 1)

                def turn_heads(b):
                    for n in range(2):
                        name = (tag, "ot", 2 * b + n)
                        if BY[name] == "A":
                            wait_filled(act, i, name)
                            A(big1[:, 4 * n:4 * n + 4, b * T:b * T + T],
                              bank(name).rearrange("p (c t) -> p c t", c=4), ACT.Copy).then_inc(emptied["A"], 1)

                exps(0)
                exps(1)
                for p in range(QUADS // 2):
                    more = 2 * p + 2 < QUADS
                    if more:
                        exps(2 * p + 2)
                    turn((tag, "t", 2 * p), probsT[:, 0, 0:hpb * 128], hpb * 128)
                    if more:
                        exps(2 * p + 3)
                    turn((tag, "t", 2 * p + 1), probsT[:, 1, 0:hpb * 128], hpb * 128)
                    if tag in ("sa", "ca") and p % 2 == 0 and p:
                        turn_heads(p // 2 - 1)
                if tag in ("sa", "ca"):
                    turn_heads(G - 1)

            def qkv0(i, tag):
                for k, c in QKV:
                    if BY[tag, k, c] == "D":
                        continue
                    if k == "q":
                        take(i, (tag, k, c), lambda s: A(big1[:, c, :], s, ACT.Identity,
                                                         bias=scaled_bq[tag][:, c:c + 1], scale=D0 ** -0.5))
                    else:
                        take(i, (tag, k, c), lambda s: A(big2[:, c, :], s, ACT.Identity,
                                                         bias=cols[f"L0_xattn_{tag}_bk"][:, c:c + 1], scale=1.0))

            with act.Fori(0, GROUPS) as i:
                take(i, ("in", 0), lambda s: A(xT["a"][:, :], s, ACT.Copy))
                qkv0(i, "sa")
                attention(i, "sa")
                qkv0(i, "ca")
                attention(i, "ca")
                for c in range(FC0):
                    if BY["ffn", c] == "A":
                        take(i, ("ffn", c), lambda s: A(hidden[:, c, :], s, ACT.Relu,
                                                        bias=cols["L0_xattn_ffn_b1"][:, c:c + 1], scale=1.0))
                take(i, ("l1", "k"), lambda s: A(l1k0, s, ACT.Relu, bias=v1("L1_xattn_bk"), scale=1.0))
                take(i, ("l1", "v"), lambda s: A(l1v[:, :, :, 0:D1], s.rearrange("p (g h d) -> p g h d", g=G, h=H1), ACT.Relu))
                attention(i, "l1")
                for n, blk in enumerate(("en", "d0", "d1")):
                    for m in range(2):
                        act.wait_ge(neg_ready, i * 6 + 2 * n + m + 1)
                        A(l2e, l2t, ACT.Exp).then_inc(exp_ready, 1)
                    take(i, (blk, "v"), lambda s: A(l2v[:, :, 0:128], s.rearrange("p (g n) -> p g n", g=G), ACT.Copy))
                    take(i, (blk, "ot"), lambda s: A(l2mT, s, ACT.Copy))
                    if blk != "d0":
                        for c in range(FC2):
                            take(i, (blk, "f", c), lambda s: A(hidden[:, c, :], s, ACT.Relu))
                take(i, ("l3", "k"), lambda s: A(l1k0, s, ACT.Identity, bias=qkvb[:, 1:2], scale=1.0))
                take(i, ("l3", "v"), lambda s: A(l3v[:, :, :, 0:D3], s.rearrange("p (g h d) -> p g h d", g=G, h=H3), ACT.Copy))
                attention(i, "l3")
                take(i, ("l3", "ot"), lambda s: A(l2mT, s, ACT.Copy))
                take(i, ("l3", "z"), lambda s: A(l2t, s, ACT.Identity, bias=v1("L3_xattn_b_in"), scale=1.0))

            with act.Fori(1, T) as t:
                act.wait_ge(scan_mm, t)
                A(state[:, 0, :], ps[0:NS, 0, 0:B], ACT.Silu).then_inc(scan_silu, 1)

        @block.vector
        def _(dve):
            V = nc.vector
            count = [0, 0]

            def link(i, ins):
                count[0] += 1
                ins.then_inc(vector_step, 1)
                dve.wait_ge(vector_step, i * VSTEPS + count[1] + count[0])

            dve.wait_ge(consts_ready, NCONST[0])
            dve.wait_ge(loaded_first, NFIRST[0])
            link(0, V.tensor_copy(ident_h[:, :], ident[:, :]))
            link(0, V.tensor_copy(causal[:, :], causal_f[:, :]))
            link(0, V.tensor_copy(block16[:, :].rearrange("p (h d) -> p h d", d=16),
                                  head16[:, :].unsqueeze(2).broadcast_to([128, 8, 16])))
            link(0, V.tensor_reduce(quad8[:, :], head8[:, :].rearrange("p (g j) -> p j g", j=4), AX.X, ALU.add))
            link(0, V.tensor_reduce(quad16[:, :], head16[:, :].rearrange("p (g j) -> p j g", j=2), AX.X, ALU.add))
            dve.wait_ge(setup_filled, 3)
            link(0, V.tensor_copy(col_all[:, :], ps[:, 5, 0:NCOLS]))
            for t in ("sa", "ca"):
                link(0, V.tensor_scalar(scaled_bq[t][:, :], cols[f"L0_xattn_{t}_bq"][:, :], D0 ** -0.5, None, ALU.mult))
            for k, (n, r, c, r0) in enumerate(TURNED):
                link(0, V.tensor_copy(turned[0:c, k, 0:r], ps[0:c, k // 4, (k % 4) * 128:(k % 4) * 128 + r]))
            link(0, V.memset(turned[0:NS, TURN["L3_xattn_A", 0], NS:128], 0.0))
            V.tensor_copy(prog_mean[:, :], ps[0:NP, 3, 0:B]).then_inc(setup_emptied, 1)
            dve.wait_ge(setup_filled, 4)
            V.tensor_scalar(mod[:, :], ps[:, 4, 0:B], v1("L3_xattn_b_prog"), None, ALU.add).then_inc(setup_emptied, 1)
            link(0, V.memset(var_eps[:, :], 1.0))
            assert count[0] == SETUP_VSTEPS, count
            count = [0, SETUP_VSTEPS]

            def take(i, name, fn):
                wait_filled(dve, i, name)
                fn(bank(name)).then_inc(emptied["D"], 1)

            def attention(i, tag):
                hpb, d1 = ATTENTIONS[tag]
                k0 = TAG_MAX[tag]
                wide = tag in ("sa", "ca")

                def maxes(u):
                    wait_filled(dve, i, (tag, "s", u))
                    V.tensor_reduce(neg_max[:, u, 0:hpb],
                                    bank((tag, "s", u))[:, 0:hpb * 128].rearrange("p (h k) -> p h k", h=hpb),
                                    AX.X, ALU.max, negate=True).then_inc(max_ready, 1)

                def recip(u, n):
                    wait_filled(dve, i, (tag, "o", u))
                    o = ps[:, BANK[tag, "o", u], 0:n * d1].rearrange("p (h d) -> p h d", d=d1)
                    link(i, V.reciprocal(inv[:, u % 2, 0:n].unsqueeze(2), o[:, :, d1 - 1:d1]))
                    return o

                def norm0(u):
                    b, q = u // 4, u % 4
                    o = recip(u, 4)
                    dst = heads[:, b % 2, :].rearrange("p (o j x d) -> p o x j d", o=2, j=4, x=2)[:, q // 2, q % 2]
                    V.scalar_tensor_tensor(out=dst, in0=o[:, :, 0:D0], scalar=row_ok[tag][:, b:b + 1],
                                           in1=inv[:, u % 2, 0:4].unsqueeze(2).broadcast_to([128, 4, D0]),
                                           op0=ALU.mult, op1=ALU.mult).then_inc(emptied["D"], 1)

                def norm1(b):
                    n, d = 4 * hpb, d1 - 1
                    o = recip(b, n)
                    cols_ = slice(b * T, b * T + T)
                    dst = l2m[:, cols_]
                    last = V.tensor_tensor(dst.rearrange("p (h d) -> p h d", d=d), o[:, :, 0:d],
                                           inv[:, b % 2, 0:n].unsqueeze(2).broadcast_to([128, n, d]), ALU.mult)
                    if tag == "l1":
                        link(i, last)
                        last = V.tensor_tensor(x1T[:, cols_], dst, xT["b"][:, cols_], ALU.add)
                    last.then_inc(emptied["D"], 1)

                def norm(u):
                    if wide:
                        norm0(u)
                    elif u % 4 == 3:
                        norm1(u // 4)

                def turn(u):
                    name = (tag, "t", u)
                    if BY[name] == "D":
                        wait_filled(dve, i, name)
                        V.tensor_copy(probsT[:, u % 2, 0:hpb * 128], bank(name)[:, 0:hpb * 128]).then_inc(emptied["D"], 1)

                def turn_heads(b):
                    for n in range(2):
                        name = (tag, "ot", 2 * b + n)
                        if BY[name] == "D":
                            wait_filled(dve, i, name)
                            V.tensor_copy(big1[:, 4 * n:4 * n + 4, b * T:b * T + T],
                                          bank(name).rearrange("p (c t) -> p c t", c=4)).then_inc(emptied["D"], 1)

                maxes(0)
                maxes(1)
                for p in range(QUADS // 2):
                    more = 2 * p + 2 < QUADS
                    if more:
                        maxes(2 * p + 2)
                        maxes(2 * p + 3)
                    turn(2 * p)
                    if p:
                        norm(2 * p - 1)
                    turn(2 * p + 1)
                    norm(2 * p)
                    if wide and p % 2 == 0 and p:
                        turn_heads(p // 2 - 1)
                norm(QUADS - 1)
                if wide:
                    turn_heads(G - 1)

            def normalise(i, tag):
                wait_filled(dve, i, (tag, "y"))
                y = bank((tag, "y"))
                for b in range(G):
                    last = V.bn_stats(stats[:, b, :], y[:, b * 128:b * 128 + 128])
                link(i, last)
                V.memset(scratch[:, :], 0.0)
                for b in range(G):
                    last = V.bn_aggr(meanvar[:, b, :], stats[:, b, :])
                link(i, last)
                V.tensor_scalar(var_eps[:, :].unsqueeze(2), meanvar[:, :, 1:2], EPS.get(tag, 1e-5), None,
                                ALU.add).then_inc(stats_ready, 1)
                dve.wait_ge(rstd_ready, i * len(LN_TAGS) + LN_TAGS.index(tag) + 1)
                for b in range(G):
                    last = V.tensor_scalar(normed[:, b, :], y[:, b * 128:b * 128 + 128], meanvar[:, b, 0:1],
                                           rstd[:, b:b + 1], ALU.subtract, ALU.mult)
                last.then_inc(emptied["D"], 1)

            def gain(i, tag, dst, plus=None):
                g, b = (v1(n) for n in GB[tag])
                wait_filled(dve, i, (tag, "n"))
                s = bank((tag, "n"))
                if plus is None:
                    V.tensor_scalar(dst, s, g, b, ALU.mult, ALU.add).then_inc(emptied["D"], 1)
                else:
                    link(i, V.scalar_tensor_tensor(out=l2e, in0=s, scalar=g, in1=plus, op0=ALU.mult, op1=ALU.add))
                    V.tensor_scalar(dst, l2e, b, None, ALU.add).then_inc(emptied["D"], 1)

            def qkv0(i, tag):
                for k, c in QKV:
                    if BY[tag, k, c] == "A":
                        continue
                    if k == "q":
                        take(i, (tag, k, c), lambda s: V.tensor_scalar(
                            big1[:, c, :], s, cols[f"L0_xattn_{tag}_bq"][:, c:c + 1], D0 ** -0.5, ALU.add, ALU.mult))
                    elif k == "k":
                        take(i, (tag, k, c), lambda s: V.tensor_scalar(
                            big2[:, c, :], s, cols[f"L0_xattn_{tag}_bk"][:, c:c + 1], None, ALU.add))
                    else:
                        hs = slice(8 * (c % 2), 8 * (c % 2) + 8)
                        take(i, (tag, k, c), lambda s: V.tensor_tensor(
                            values[:, c // 2, hs, 0:D0], s.rearrange("p (h d) -> p h d", d=D0),
                            bv_all[tag][:, (c % 2) * 512:(c % 2) * 512 + 512].rearrange("p (h d) -> p h d", d=D0), ALU.add))

            with dve.Fori(0, GROUPS) as i:
                count[0] = 0
                dve.wait_ge(group_in, i * 64 + 64)
                link(i, V.tensor_scalar(mask_ca[:, :, :].rearrange("p g t -> p (g t)"), valid_in[:, :], 0.0, -BIG,
                                        ALU.is_equal, ALU.mult))
                link(i, V.tensor_tensor(mask_sa[:, :, :], mask_ca[:, :, :],
                                        causal[:, :].unsqueeze(1).broadcast_to([128, G, T]), ALU.min))
                for t, m in (("sa", mask_sa), ("ca", mask_ca)):
                    link(i, V.tensor_reduce(row_ok[t][:, :], m[:, :, :], AX.X, ALU.max))
                    link(i, V.tensor_scalar(row_ok[t][:, :], row_ok[t][:, :], -1.0, None, ALU.is_ge))
                V.tensor_scalar(attend[:, :], skip_in[:, :], 0.0, D1 ** -0.5, ALU.not_equal, ALU.mult).then_inc(masks_taken, 1)
                dve.wait_ge(masks_taken, i + 1)
                take(i, ("in", 1), lambda s: V.tensor_copy(cT[:, :], s))
                qkv0(i, "sa")
                attention(i, "sa")
                normalise(i, "ln1")
                gain(i, "ln1", xT["b"][:, :])
                qkv0(i, "ca")
                attention(i, "ca")
                normalise(i, "ln2")
                gain(i, "ln2", xT["a"][:, :])
                for c in range(FC0):
                    if BY["ffn", c] == "D":
                        take(i, ("ffn", c), lambda s: V.tensor_scalar(hidden[:, c, :], s, cols["L0_xattn_ffn_b1"][:, c:c + 1],
                                                                      0.0, ALU.add, ALU.max))
                normalise(i, "ln3")
                gain(i, "ln3", xT["b"][:, :])
                wait_filled(dve, i, ("l1", "q"))
                link(i, V.tensor_scalar(l2e, bank(("l1", "q")), v1("L1_xattn_bq"), 0.0, ALU.add, ALU.max))
                V.tensor_tensor(l1q, l2e, attend[:, :], ALU.mult).then_inc(emptied["D"], 1)
                link(i, V.memset(l1v[:, :, :, D1:D1 + 1], 1.0))
                link(i, V.memset(l2v[:, :, 128:129], 1.0))
                link(i, V.tensor_scalar(c2T, cT[:, :], 2.0, None, ALU.mult))
                wait_emptied(dve, i, ("l1", "k"))
                for j in range(4):
                    last = V.tensor_scalar(kx[:, j, :], l1k0, quad8[:, j:j + 1], None, ALU.mult)
                    if j < 3:
                        link(i, last)
                last.then_inc(keys_ready, 1)
                attention(i, "l1")
                for n, blk in enumerate(("en", "d0", "d1")):
                    for m, (name, dst) in enumerate((((blk, "q"), l2qT), ((blk, "k"), l2k))):
                        wait_filled(dve, i, name)
                        V.tensor_scalar(l2t, bank(name), 0.0, None, ALU.min).then_inc(neg_ready, 1)
                        dve.wait_ge(exp_ready, i * 6 + 2 * n + m + 1)
                        V.scalar_tensor_tensor(out=dst, in0=bank(name), scalar=0.0, in1=l2e,
                                               op0=ALU.max, op1=ALU.add).then_inc(emptied["D"], 1)
                    for m in range(2):
                        name = (blk, "kv", m)
                        wait_filled(dve, i, name)
                        s = bank(name)[:, 0:258].rearrange("p (g n) -> p g n", g=2)
                        link(i, V.tensor_tensor(kvb[:, 2 * m:2 * m + 2, 0:128], s[:, :, 0:128],
                                                block16[:, :].unsqueeze(1).broadcast_to([128, 2, 128]), ALU.mult))
                        V.tensor_tensor(kvb[:, 2 * m:2 * m + 2, 128:136], s[:, :, 128:129].broadcast_to([128, 2, 8]),
                                        head16[:, :].unsqueeze(1).broadcast_to([128, 2, 8]), ALU.mult).then_inc(emptied["D"], 1)
                    for m in range(2):
                        name = (blk, "o", m)
                        wait_filled(dve, i, name)
                        s = bank(name)[:, 0:272].rearrange("p (g n) -> p g n", g=2)
                        z = l2z[:, m, :].rearrange("p (g h) -> p g h", g=2)
                        link(i, V.tensor_scalar(z, s[:, :, 128:136], 1e-6, None, ALU.add))
                        link(i, V.reciprocal(z, z))
                        V.tensor_tensor(l2m[:, 2 * m * 128:2 * m * 128 + 256].rearrange("p (g h d) -> p g h d", g=2, d=D2),
                                        s[:, :, 0:128].rearrange("p g (h d) -> p g h d", d=D2),
                                        z.unsqueeze(3).broadcast_to([128, 2, H2, D2]), ALU.mult).then_inc(emptied["D"], 1)
                    normalise(i, blk)
                    if blk == "en":
                        gain(i, "en", encT[:, :], c2T)
                        normalise(i, "enf")
                        gain(i, "enf", encT[:, :], encT[:, :])
                    elif blk == "d0":
                        gain(i, "d0", xT["b"][:, :], x1T)
                    else:
                        gain(i, "d1", x1T, xT["b"][:, :])
                        normalise(i, "d1f")
                        gain(i, "d1f", xT["b"][:, :], x1T)
                normalise(i, "b3")
                gain(i, "b3", l3b)
                normalise(i, "x3")
                gain(i, "x3", l3x)
                take(i, ("l3", "q"), lambda s: V.tensor_scalar(l1q, s, qkvb[:, 0:1], D3 ** -0.5, ALU.add, ALU.mult))
                link(i, V.memset(l3v[:, :, :, D3:D3 + 1], 1.0))
                wait_emptied(dve, i, ("l3", "k"))
                for j in range(2):
                    last = V.tensor_scalar(kx[:, j, :], l1k0, quad16[:, j:j + 1], None, ALU.mult)
                    if j < 1:
                        link(i, last)
                last.then_inc(keys_ready, 1)
                attention(i, "l3")
                take(i, ("l3", "x"), lambda s: V.scalar_tensor_tensor(out=x1T, in0=s, scalar=v1("L3_xattn_b_o"), in1=xT["b"][:, :],
                                                                      op0=ALU.add, op1=ALU.add))
                normalise(i, "z3")
                gain(i, "z3", l3x)
                link(i, V.tensor_tensor(x2_all[:, bass.ds(i * GT, GT)].rearrange("p (g t) -> p g t", g=G),
                                        x1T.rearrange("p (g t) -> p g t", g=G),
                                        mod[:, bass.ds(i * G, G)].unsqueeze(2).broadcast_to([128, G, T]), ALU.add))
                wait_filled(dve, i, ("l3", "u"))
                V.tensor_scalar(u_all[:, :, bass.ds(i * G, G)].rearrange("p t g -> p g t"),
                                ps[0:NS, BANK["l3", "u"], :].rearrange("p (g t) -> p g t", g=G), 0.0, None,
                                ALU.add).then_inc(emptied["D"], 1)
                wait_filled(dve, i, ("l3", "u"))
                link(i, V.memset(values[:, :, :, D0:D0 + 1], 1.0))
                assert count[0] == VSTEPS, count

            dve.wait_ge(emptied["D"], GROUPS * EMPTIES["D"])
            V.memset(var_eps[:, 0:1], 1.0).then_inc(scan_add, 1)
            with dve.Fori(1, T) as t:
                dve.wait_ge(scan_silu, t)
                s = u_all[:, bass.ds(t, 1), :].rearrange("p a b -> p (a b)")
                V.tensor_tensor(s, s, state[:, 0, :], ALU.add).then_inc(scan_add, 1)
            with dve.Fori(0, GROUPS) as g:
                dve.wait_ge(fin_mm, g + 1)
                V.tensor_tensor(cT[:, :], ps[:, 1, :], x2_all[:, bass.ds(g * GT, GT)], ALU.add).then_inc(fin_add, 1)
                dve.wait_ge(fin_turn, g + 1)
                V.tensor_scalar(x2_all[:, bass.ds(g * GT, GT)], ps[:, 2, :], 0.0, None, ALU.add).then_inc(fin_copy, 1)


_OUTS = [((B, T, E), "float32")]


def kernel(**inputs):
    import concourse.bacc as _bacc
    from concourse.bass_utils import run_bass_kernel_spmd as _run

    nc = _bacc.Bacc("TRN2", target_bir_lowering=False, num_devices=1)
    arrays, aps = {}, {}
    for name, a in inputs.items():
        if name == "itok_BxS2_4_31999":
            continue
        a = np.ascontiguousarray(a)
        if a.dtype == np.bool_:
            a = a.view(np.uint8)
        arrays[f"in_{name}"] = a
        aps[name] = nc.dram_tensor(f"in_{name}", a.shape, mybir.dt.from_np(a.dtype), kind="ExternalInput").ap()
    out = nc.dram_tensor("out_0", (B, T, E), F32, kind="ExternalOutput").ap()
    build_program(nc, aps, out)
    r = _run(nc, [arrays], core_ids=[0])
    return r.results[0]["out_0"]
```

```python
from contextlib import ExitStack

import numpy as np
import concourse.bass as bass
from concourse import mybir

F32 = mybir.dt.float32
BF16 = mybir.dt.bfloat16
I32 = mybir.dt.int32
U8 = mybir.dt.uint8
ALU = mybir.AluOpType
ACT = mybir.ActivationFunctionType
AX = mybir.AxisListType

B, T, E = 32, 128, 128
G = 4
GROUPS = B // G
GT = G * T
H0, D0 = 16, 64
C0 = H0 * D0 // 128
H1, D1 = 16, 8
H2, D2 = 8, 16
H3, D3 = 8, 16
FC0 = 4
FC2 = 2
NS = 64
NP = 64
BIG = 2.0 ** 100
QUADS = 4 * G
ATTENTIONS = {"sa": (4, 65), "ca": (4, 65), "l1": (4, 9), "l3": (2, 17)}


UNITS = C0 * G // 2


def main_steps():
    steps = [[("in", 0)], [("in", 1)], [("sa", "k", 0)], [("sa", "q", 0)]]
    steps += [[("sa", "v", 0, b)] for b in range(G)]

    def attention(tag):
        for s in range(UNITS + 3):
            c = s // 2 + 1
            first = [(tag, "s", s)] if s < UNITS else []
            if c < C0:
                first.append((tag, "qk"[s % 2 == 0], c))
            elif tag == "sa" and s < UNITS + 2:
                first.append(("ca", "v", 0, s - UNITS + 2))
            second = [(tag, "o", s - 2)] if 2 <= s < UNITS + 2 else []
            if s % 2 == 0 and s >= 4:
                second.append((tag, "ot", s // 2 - 2))
            third = [(tag, "t", s - 1)] if 1 <= s <= UNITS else []
            if tag == "sa" and s % 2 and s < 2 * G:
                third.append((tag, "v", 1, s // 2))
            steps.extend(x for x in (first, second, third) if x)

    attention("sa")
    steps.append([("ln1", "y")])
    steps += [[("ca", "v", 1, b)] for b in range(G)]
    steps += [[("ln1", "norm"), ("ca", "k", 0)], [("ln1", "n")], [("ca", "q", 0)]]
    attention("ca")
    steps += [[("ln2", "y")], [], [], [("ln2", "norm")], [("ln2", "n")], []]
    steps += [[("ffn", 0), ("ffn", 1)], [("ffn", 2), ("ffn", 3)], []]
    steps += [[("ln3", "y")], [], [], [("ln3", "norm")], [("ln3", "n")]]
    return steps


MAIN_STEPS = main_steps()
SIDE_STEPS = 81


class Stream:

    def __init__(self, fills):
        self.order = [name for name, _, _ in fills]
        self.fill = {name: n + 1 for n, name in enumerate(self.order)}
        self.bank = {name: bank for name, bank, _ in fills}
        self.by = {name: by for name, _, by in fills}
        self.total = {"A": 0, "D": 0}
        self.rank = {}
        for name, _, by in fills:
            self.total[by] += 1
            self.rank[name] = self.total[by]
        self.fills = len(fills)
        self.before, last = {}, {}
        for name, bank, _ in fills:
            self.before[name] = last.get(bank)
            last[bank] = name


def main_fills():
    order, n = [], 0
    for item in (x for step in MAIN_STEPS for x in step if x[1] != "norm"):
        tag, kind = item[:2]
        if kind == "s":
            bank = item[2] % 2
        elif kind == "o":
            bank = 3
        elif kind == "y":
            bank = 0
        else:
            bank, n = (2, 4)[n % 2], n + 1
        if kind in ("v", "o", "y", "n"):
            by = "D"
        elif kind == "k" or tag in ("ffn", "in"):
            by = "AD"[item[-1] % 2]
        else:
            by = "A"
        order.append((item, bank, by))
    return order


def side_fills():
    order = []

    def attention(tag):
        for u in range(QUADS + 2):
            if u >= 2 and u % 4 == 1:
                order.append(((tag, "o", u // 4 - 1), 7, "D"))
            if 1 <= u <= QUADS:
                order.append(((tag, "t", u - 1), 6, "AD"[u % 2]))
            if u < QUADS:
                order.append(((tag, "s", u), 5, "A"))

    order += [(("l1", "q"), 5, "D"), (("l1", "k"), 6, "A"), (("l1", "v"), 7, "A")]
    attention("l1")
    for blk in ("en", "d0", "d1"):
        order += [((blk, "q"), 5, "D"), ((blk, "k"), 6, "D"), ((blk, "v"), 7, "A"),
                  ((blk, "kv", 0), 5, "D"), ((blk, "kv", 1), 6, "D"),
                  ((blk, "o", 0), 7, "D"), ((blk, "o", 1), 5, "D"), ((blk, "ot"), 6, "A"),
                  ((blk, "y"), 7, "D"), ((blk, "n"), 5, "D")]
        if blk != "d0":
            order += [((blk, "f", 0), 6, "A"), ((blk, "f", 1), 7, "A"),
                      ((blk + "f", "y"), 5, "D"), ((blk + "f", "n"), 6, "D")]
    order += [(("b3", "y"), 5, "D"), (("x3", "y"), 7, "D"), (("b3", "n"), 6, "D"), (("x3", "n"), 5, "D"),
              (("l3", "q"), 6, "D"), (("l3", "k"), 7, "A"), (("l3", "v"), 5, "A")]
    attention("l3")
    order += [(("l3", "ot"), 5, "A"), (("l3", "x"), 6, "D"), (("z3", "y"), 7, "D"), (("z3", "n"), 5, "D"),
              (("l3", "z"), 6, "A"), (("l3", "u"), 7, "D")]
    return order


MAIN, SIDE = Stream(main_fills()), Stream(side_fills())
MAIN_LN = ("ln1", "ln2", "ln3")
SIDE_LN = ("en", "enf", "d0", "d1", "d1f", "b3", "x3", "z3")
RESIDUALS = ("en", "enf", "d0", "d1", "d1f")

COLUMNS = ("L0_xattn_sa_bq", "L0_xattn_sa_bk", "L0_xattn_ca_bq", "L0_xattn_ca_bk", "L0_xattn_ffn_b1")
VECTORS = ("L0_xattn_ln1_g", "L0_xattn_ln1_b", "L0_xattn_ln2_g", "L0_xattn_ln2_b", "L0_xattn_ln3_g",
           "L0_xattn_ln3_b", "L1_xattn_bq", "L1_xattn_bk", "L2_xattn_e_g1", "L2_xattn_e_b1",
           "L2_xattn_e_g2", "L2_xattn_e_b2", "L2_xattn_d_g0", "L2_xattn_d_b0", "L2_xattn_d_g1",
           "L2_xattn_d_b1", "L2_xattn_d_g2", "L2_xattn_d_b2", "L3_xattn_b_in", "L3_xattn_b_o",
           "L3_xattn_b_prog", "L3_xattn_g1", "L3_xattn_beta1", "L3_xattn_g2", "L3_xattn_beta2")
COLUMN_WIDTH = {n: FC0 if n.endswith("ffn_b1") else C0 for n in COLUMNS}
COLUMN_WIDTH["L3_xattn_b_qkv"] = 3
COLUMN_WIDTH.update({n: 1 for n in VECTORS})
COLUMN_AT, NCOLS = {}, 0
for _name, _width in COLUMN_WIDTH.items():
    COLUMN_AT[_name] = NCOLS
    NCOLS += _width
ROWS = ("L0_xattn_sa_bo", "L0_xattn_ca_bo", "L0_xattn_ffn_b2", "L1_xattn_bv")
GB = {"ln1": ("L0_xattn_ln1_g", "L0_xattn_ln1_b"), "ln2": ("L0_xattn_ln2_g", "L0_xattn_ln2_b"),
      "ln3": ("L0_xattn_ln3_g", "L0_xattn_ln3_b"), "en": ("L2_xattn_e_g1", "L2_xattn_e_b1"),
      "enf": ("L2_xattn_e_g2", "L2_xattn_e_b2"), "d0": ("L2_xattn_d_g0", "L2_xattn_d_b0"),
      "d1": ("L2_xattn_d_g1", "L2_xattn_d_b1"), "d1f": ("L2_xattn_d_g2", "L2_xattn_d_b2"),
      "b3": ("L3_xattn_g1", "L3_xattn_beta1"), "x3": ("L3_xattn_g1", "L3_xattn_beta1"),
      "z3": ("L3_xattn_g2", "L3_xattn_beta2")}
EPS = {"ln1": 1e-12, "ln2": 1e-12, "ln3": 1e-12}
SQUARES = ("L2_xattn_e_wq", "L2_xattn_e_wk", "L2_xattn_e_wv", "L2_xattn_e_wm", "L2_xattn_d_wq0",
           "L2_xattn_d_wk0", "L2_xattn_d_wv0", "L2_xattn_d_wm0", "L2_xattn_d_wq1", "L2_xattn_d_wk1",
           "L2_xattn_d_wv1", "L2_xattn_d_wm1")
L2W = {"en": "L2_xattn_e_w{}", "d0": "L2_xattn_d_w{}0", "d1": "L2_xattn_d_w{}1"}
TURNED = (("L1_xattn_Wq", 128, 128, 0), ("L1_xattn_Wk", 128, 128, 0), ("L1_xattn_Wv", 128, 128, 0),
          ("L3_xattn_W_qkv", 128, 128, 0), ("L3_xattn_W_qkv", 128, 128, 128),
          ("L3_xattn_W_qkv", 128, 128, 256), ("L3_xattn_W_o", 128, 128, 0),
          ("L3_xattn_W_in", 128, 128, 0), ("L3_xattn_W_prog", 128, 64, 0), ("L3_xattn_A", 64, 64, 0))
TURN = {(n, r0): k for k, (n, _, _, r0) in enumerate(TURNED)}

MAIN_VSTEPS = 43
SIDE_VSTEPS = 41
SETUP_FIRST = 8
SETUP_VSTEPS = 18
SCAN_UNROLL = 16


class Pass:

    def __init__(self, r, offset):
        self.r, self.offset = r, offset

    def at(self, each, n):
        known = self.offset * each + n
        return known if self.r is None else self.r * each + known


def interleave(main, side):
    taken = 0
    for n, _ in enumerate(main):
        while side is not None and taken * len(MAIN_STEPS) < (n + 1) * SIDE_STEPS:
            next(side)
            taken += 1
    assert side is None or next(side, "end") == "end"


def alone(stream):
    return sum(1 for _ in stream)


def build_program(nc, I, out):
    with ExitStack() as ctx:
        def sb(name, shape, dt=F32):
            return ctx.enter_context(nc.sbuf_tensor(name, shape, dt))

        def sem(name):
            return ctx.enter_context(nc.semaphore(name))

        ps = ctx.enter_context(nc.psum_tensor("ps", [128, 8, 512], F32))

        ident = sb("ident", [128, 128])
        ident_h = sb("ident_h", [128, 128], BF16)
        causal = sb("causal", [128, 128], BF16)
        head16 = sb("head16", [128, 8])
        head8 = sb("head8", [128, 16])
        quad8 = sb("quad8", [128, 4])
        quad16 = sb("quad16", [128, 2])
        ones = sb("ones", [128, 128])
        mean_col = sb("mean_col", [128, 1])
        minus_half = sb("minus_half", [128, G])
        w_qkv = {t: sb(f"w_qkv_{t}", [128, 3, H0 * D0]) for t in ("sa", "ca")}
        w_o = {t: sb(f"w_o_{t}", [128, C0, E]) for t in ("sa", "ca")}
        bv_all = {t: sb(f"bv_all_{t}", [128, H0 * D0]) for t in ("sa", "ca")}
        w_f1 = sb("w_f1", [128, FC0 * 128])
        w_f2 = sb("w_f2", [128, FC0, E])
        w_sq = sb("w_sq", [128, len(SQUARES), 128])
        w_l2f1 = {b: sb(f"w_l2f1_{b}", [128, FC2 * 128]) for b in ("en", "d1")}
        w_l2f2 = {b: sb(f"w_l2f2_{b}", [128, FC2, E]) for b in ("en", "d1")}
        turned = sb("turned", [128, len(TURNED), 128])
        w_b = sb("w_b", [128, NS])
        w_c = sb("w_c", [NS, E])
        col_all = sb("col_all", [128, NCOLS])
        cols = {n: col_all[:, COLUMN_AT[n]:COLUMN_AT[n] + w] for n, w in COLUMN_WIDTH.items()}
        qkvb = cols["L3_xattn_b_qkv"]
        rows = sb("rows", [128, 2, 128])
        scaled_bq = {t: sb(f"scaled_bq_{t}", [128, C0]) for t in ("sa", "ca")}
        x_in = sb("x_in", [128, G, E])
        c_in = sb("c_in", [128, G, E])
        valid_in = sb("valid_in", [128, GT], U8)
        skip_in = sb("skip_in", [128, GT], I32)
        cT = sb("cT", [128, GT])
        xT = {n: sb("xT_" + n, [128, GT]) for n in ("a", "b")}
        queries = sb("queries", [128, 2, GT])
        keys = sb("keys", [128, 2, 2, GT])
        headsT = sb("headsT", [128, C0, GT])
        hidden = headsT[:, 0:FC0, :]
        values = sb("values", [128, 2, G * (H0 // 2) * (D0 + 1) + 127 - D0])
        mask_sa = sb("mask_sa", [128, G, T], BF16)
        mask_ca = sb("mask_ca", [128, G, T], BF16)
        row_ok = {"sa": sb("row_ok_sa", [128, G]), "ca": sb("row_ok_ca", [128, G])}
        neg_max = sb("neg_max", [128, 2, 4])
        probs = sb("probs", [128, 2, 512])
        probsT = sb("probsT", [128, 2, 512])
        inv = sb("inv", [128, 4])
        heads = sb("heads", [128, 2, G, 2 * D0])
        col_rows = headsT[0:NCOLS, 0, 0:128]
        stats = sb("stats", [128, 3, G, 6])
        meanvar = sb("meanvar", [128, 3, G, 2])
        var_eps = sb("var_eps", [128, 3, G])
        rstd = sb("rstd", [128, 3, G])
        main_normed = sb("main_normed", [128, G, E])
        scratch = sb("scratch", [128, 1])
        pool_scratch = sb("pool_scratch", [128, 8])
        x_side = sb("x_side", [128, GT])
        c_side = sb("c_side", [128, GT])
        qT = sb("qT", [128, GT])
        attend = qT
        kx = sb("kx", [128, 4, GT])
        l1v = sb("l1v", [128, G, H1, D1 + 1])
        l2v = sb("l2v", [128, G, 129])
        l3v = sb("l3v", [128, G, H3, D3 + 1])
        x1T = sb("x1T", [128, GT])
        encT = sb("encT", [128, GT])
        c2T = encT
        s_max = sb("s_max", [128, 2, 4])
        s_probs = sb("s_probs", [128, 2, 512])
        s_probsT = sb("s_probsT", [128, 2, 512])
        s_inv = sb("s_inv", [128, 2, 16])
        l2z = sb("l2z", [128, 2, 2 * H2])
        tok = sb("tok", [128, GT])
        tokT = kx[:, 3, :]
        k0, neg_q = s_probsT[:, 0, :], s_probsT[:, 1, :]
        residual = neg_q
        normed = [main_normed, tok[:, :].rearrange("p (g e) -> p g e", g=G),
                  s_probs[:, 0, :].rearrange("p (g e) -> p g e", g=G)]
        l2k, kvb = k0, s_probs[:, :, :].rearrange("p a n -> p (a n)")[:, 0:G * 136].rearrange("p (g n) -> p g n", g=G)
        neg = [kx[:, 0, :], kx[:, 1, :]]
        expn = [kx[:, 2, :], kx[:, 3, :]]
        l2h = kx[:, 0:2, :]
        l3b, l3x = encT[:, :], s_probsT[:, 1, :]
        zT = kx[:, 0, :]
        x2_all = sb("x2_all", [128, B * T])
        u_all = sb("u_all", [NS, T, B])
        prog_in = x2_all[:, 0:B * NP].rearrange("p (b n) -> p b n", b=B)
        mod = sb("mod", [128, B])
        state = sb("state", [NS, B])
        prog_mean = state

        loaded_first = sem("loaded_first")
        loaded_ca = sem("loaded_ca")
        loaded_rest = sem("loaded_rest")
        group_in = sem("group_in")
        skip_loaded = sem("skip_loaded")
        masks_taken = sem("masks_taken")
        handed = sem("handed")
        consts_ready = sem("consts_ready")
        setup_filled = sem("setup_filled")
        setup_emptied = sem("setup_emptied")
        setup_step = sem("setup_step")
        filled = {MAIN: sem("filled_main"), SIDE: sem("filled_side")}
        emptied = {(MAIN, "A"): sem("emptied_main_scalar"), (MAIN, "D"): sem("emptied_main_vector"),
                   (SIDE, "A"): sem("emptied_side_scalar"), (SIDE, "D"): sem("emptied_side_vector")}
        main_step, side_step = sem("main_step"), sem("side_step")
        max_ready = {MAIN: sem("max_ready_main"), SIDE: sem("max_ready_side")}
        stats_ready = {MAIN: sem("stats_ready_main"), SIDE: sem("stats_ready_side")}
        rstd_ready = {MAIN: sem("rstd_ready_main"), SIDE: sem("rstd_ready_side")}
        queries_ready = sem("queries_ready")
        keys_ready = sem("keys_ready")
        neg_ready = sem("neg_ready")
        exp_ready = sem("exp_ready")
        residual_ready = sem("residual_ready")
        scan_mm = sem("scan_mm")
        scan_silu = sem("scan_silu")
        scan_add = sem("scan_add")
        fin_mm = sem("fin_mm")
        fin_add = sem("fin_add")
        fin_turn = sem("fin_turn")
        fin_copy = sem("fin_copy")
        stored = sem("stored")
        block = ctx.enter_context(nc.Block())

        def v1(name):
            return cols[name]

        def row(k):
            return rows[32 * (k % 4):32 * (k % 4) + 1, k // 4, :]

        def ones_at(k):
            return ones[32 * (k % 4):32 * (k % 4) + 1, :]

        def bank(st, name):
            return ps[:, st.bank[name], :]

        def values_of(o, b):
            n = (H0 // 2) * (D0 + 1)
            return values[:, o, b * n:b * n + n].rearrange("p (h d) -> p h d", d=D0 + 1)

        def wait_filled(eng, i, st, name):
            eng.wait_ge(filled[st], i.at(st.fills, st.fill[name]))

        def wait_emptied(eng, i, st, name):
            by = st.by[name]
            eng.wait_ge(emptied[st, by], i.at(st.total[by], st.rank[name]))

        def wait_all_emptied(eng, i, st, names):
            last = {}
            for name in names:
                by = st.by[name]
                last[by] = max(last.get(by, 0), st.rank[name])
            for by, rank in last.items():
                eng.wait_ge(emptied[st, by], i.at(st.total[by], rank))

        def passes(eng, main, side, between):
            interleave(main(Pass(None, 0)), None)
            between()
            with eng.Fori(0, GROUPS - 1) as r:
                interleave(main(Pass(r, 1)), side(Pass(r, 0)))
            assert alone(side(Pass(None, GROUPS - 1))) == SIDE_STEPS

        n_first, n_ca, n_rest, n_const = [0], [0], [0], [0]

        @block.sync
        def _(sp):
            def load(s, n, dst, src):
                sp.dma_start(dst, src).then_inc(s, 16)
                n[0] += 16

            def load_inputs(g):
                for dst, name in ((x_in, "x"), (c_in, "ctx_1024")):
                    sp.dma_start(dst[:, :, :], I[name][g * G:g * G + G, :, :].rearrange("g t e -> t g e")).then_inc(group_in, 16)

            def load_valid(g):
                m = I["mask_BxS2_bf1"].rearrange("b t -> (b t)")[g * GT:g * GT + GT].partition_broadcast(128)
                sp.dma_start(valid_in[:, :], m).then_inc(group_in, 16)

            def load_skip(g):
                m = I["mask_BxS_ik0"].rearrange("b t -> (b t)")[g * GT:g * GT + GT].partition_broadcast(128)
                sp.dma_start(skip_in[:, :], m).then_inc(skip_loaded, 16)

            load_inputs(0)
            load_valid(0)
            for t, s, n in (("sa", loaded_first, n_first), ("ca", loaded_ca, n_ca)):
                for k, c in enumerate("qkv"):
                    load(s, n, w_qkv[t][:, k, :], I[f"L0_xattn_{t}_w{c}"])
                load(s, n, bv_all[t][:, :], I[f"L0_xattn_{t}_bv"].partition_broadcast(128))
                load(s, n, w_o[t][:, :, :], I[f"L0_xattn_{t}_wo"].rearrange("(c p) n -> p c n", p=128))
                if t == "sa":
                    for c, w in COLUMN_WIDTH.items():
                        load(s, n, col_rows[COLUMN_AT[c]:COLUMN_AT[c] + w, :], I[c].rearrange("(c p) -> c p", p=128))
                    for k, c in enumerate(ROWS):
                        load(s, n, row(k), I[c].rearrange("(a n) -> a n", a=1))
                    load(s, n, row(len(ROWS)), I["L3_xattn_b_qkv"].rearrange("(a n) -> a n", a=1)[:, 256:384])
            load(loaded_ca, n_ca, w_f1[:, :], I["L0_xattn_ffn_w1"])
            load(loaded_ca, n_ca, w_f2[:, :, :], I["L0_xattn_ffn_w2"].rearrange("(c p) n -> p c n", p=128))
            for k, c in enumerate(SQUARES):
                load(loaded_rest, n_rest, w_sq[:, k, :], I[c])
            for b, c in (("en", "e"), ("d1", "d")):
                load(loaded_rest, n_rest, w_l2f1[b][:, :], I[f"L2_xattn_{c}_w1"])
                load(loaded_rest, n_rest, w_l2f2[b][:, :, :], I[f"L2_xattn_{c}_w2"].rearrange("(c p) n -> p c n", p=128))
            load(loaded_rest, n_rest, w_b[:, :], I["L3_xattn_Bmat"])
            load(loaded_rest, n_rest, w_c[:, :], I["L3_xattn_Cmat"])
            for k, (c, r, w, r0) in enumerate(TURNED):
                load(loaded_rest, n_rest, kx[0:r, k // 4, (k % 4) * 128:(k % 4) * 128 + w], I[c][r0:r0 + r, :])
            load(loaded_rest, n_rest, prog_in, I["ctxb_2048x64"].rearrange("b t n -> t b n"))
            load_skip(0)
            for g in range(1, GROUPS):
                wait_filled(sp, Pass(None, g - 1), MAIN, ("in", 1))
                load_inputs(g)
                sp.wait_ge(masks_taken, g)
                load_valid(g)
                sp.wait_ge(handed, g)
                load_skip(g)
            o = out.rearrange("b t e -> t b e")
            for g in range(GROUPS):
                sp.wait_ge(fin_copy, g + 1)
                sp.dma_start(o[:, g * G:g * G + G, :],
                             x2_all[:, g * GT:g * GT + GT].rearrange("p (g e) -> p g e", g=G)).then_inc(stored, 16)
            sp.wait_ge(stored, 16 * GROUPS)

        @block.gpsimd
        def _(pool):
            P = nc.gpsimd
            step = [0]

            def link(ins):
                step[0] += 1
                ins.then_inc(consts_ready, 1)
                pool.wait_ge(consts_ready, step[0])

            def select(m, op, fill, base, pattern, mult):
                link(P.affine_select(out=m, in_=m, compare_op=op, fill=fill, base=base, pattern=pattern,
                                     channel_multiplier=mult))

            def band(m, n, width):
                link(P.memset(m, 1.0))
                select(m, ALU.is_ge, 0.0, 0, [[-width, n]], 1)
                select(m, ALU.is_ge, 0.0, width - 1, [[width, n]], -1)

            link(P.memset(ident[:, :], 0.0))
            select(ident[:, :], ALU.not_equal, 1.0, 0, [[-1, 128]], 1)
            link(P.memset(main_normed[:, 0, :], 0.0))
            select(main_normed[:, 0, :], ALU.is_ge, -BIG, 0, [[-1, 128]], 1)
            band(head16[:, :], 8, 16)
            band(head8[:, :], 16, 8)
            link(P.memset(ones[:, :], 1.0))
            link(P.memset(mean_col[:, :], 1.0 / T))
            link(P.memset(minus_half[:, :], -0.5))
            for o in range(2):
                for b in range(G):
                    link(P.memset(values_of(o, b)[:, :, D0:D0 + 1], 1.0))
            link(P.memset(values[:, :, G * (H0 // 2) * (D0 + 1):], 0.0))
            link(P.memset(keys[64:128, :, 0, :], 0.0))
            link(P.memset(keys[0:64, :, 1, :], 0.0))
            link(P.memset(l1v[:, :, :, D1:D1 + 1], 1.0))
            link(P.memset(l2v[:, :, 128:129], 1.0))
            link(P.memset(l3v[:, :, :, D3:D3 + 1], 1.0))
            n_const[0] = step[0]

            def carry_wait(n):
                P.tensor_tensor(pool_scratch[:, n:n + 1], minus_half[:, 0:1], minus_half[:, 0:1], ALU.mult)

            def root(i, st, tag, slot):
                tags = MAIN_LN if st is MAIN else SIDE_LN
                pool.wait_ge(stats_ready[st], i.at(len(tags), tags.index(tag) + 1))
                P.tensor_tensor(rstd[:, slot, :], var_eps[:, slot, :], minus_half[:, :], ALU.pow).then_inc(rstd_ready[st], 1)

            def main(i):
                for step in MAIN_STEPS:
                    for item in step:
                        if item[1] == "y":
                            root(i, MAIN, item[0], 0)
                    yield

            def side(i):
                def spread(n, name, width, quad):
                    wait_emptied(pool, i, SIDE, name)
                    carry_wait(n)
                    for j in range(width):
                        last = P.tensor_scalar(kx[:, j, :], k0[:, :], quad[:, j:j + 1], None, ALU.mult)
                    last.then_inc(keys_ready, 1)

                def keep_residual(k, src, b):
                    carry_wait(3 + k)
                    P.tensor_scalar(residual[:, :], src, v1(b), None, ALU.add).then_inc(residual_ready, 1)

                pool.wait_ge(handed, i.at(1, 1))
                yield
                carry_wait(2)
                P.tensor_scalar(c2T[:, :], c_side[:, :], 2.0, None, ALU.mult).then_inc(keys_ready, 1)
                wait_emptied(pool, i, SIDE, ("l1", "q"))
                P.tensor_tensor(qT[:, :], neg_q, attend[:, :], ALU.mult).then_inc(queries_ready, 1)
                spread(0, ("l1", "k"), 4, quad8)
                yield
                for _ in range(QUADS + 2):
                    yield
                for blk in ("en", "d0", "d1"):
                    if blk == "en":
                        pool.wait_ge(keys_ready, i.at(3, 1))
                        wait_emptied(pool, i, SIDE, ("l1", "o", G - 1))
                        keep_residual(0, c2T[:, :], GB["en"][1])
                    elif blk == "d0":
                        wait_emptied(pool, i, SIDE, ("enf", "n"))
                        keep_residual(1, x1T[:, :], GB["d0"][1])
                    else:
                        wait_emptied(pool, i, SIDE, ("d0", "n"))
                        keep_residual(2, x_side[:, :], GB["d1"][1])
                    for _ in range(6):
                        yield
                    root(i, SIDE, blk, 1)
                    yield
                    yield
                    if blk != "d0":
                        src = encT if blk == "en" else x1T
                        wait_emptied(pool, i, SIDE, (blk, "n"))
                        keep_residual(3 + (blk == "d1"), src[:, :], GB[blk + "f"][1])
                        yield
                        root(i, SIDE, blk + "f", 1)
                        yield
                        yield
                        yield
                root(i, SIDE, "b3", 1)
                root(i, SIDE, "x3", 2)
                yield
                yield
                yield
                spread(1, ("l3", "k"), 2, quad16)
                yield
                for _ in range(QUADS + 2):
                    yield
                yield
                yield
                root(i, SIDE, "z3", 1)
                yield
                yield
                yield
                yield
                yield

            passes(pool, main, side, lambda: None)

        @block.tensor
        def _(pe):
            mm = nc.tensor.matmul
            pe.wait_ge(consts_ready, n_const[0])
            pe.wait_ge(loaded_first, n_first[0])
            nc.tensor.transpose(ps[:, 5, 0:NCOLS], col_rows[:, :], ident[0:NCOLS, 0:NCOLS]).then_inc(setup_filled, 1)

            def turn4(st, name, src):
                for b in range(G):
                    last = nc.tensor.transpose(bank(st, name)[:, b * 128:b * 128 + 128], src(b), ident[:, :])
                last.then_inc(filled[st], 1)

            def one(st, name, lhs, rhs):
                mm(bank(st, name)[0:lhs.shape[-1], :], lhs, rhs, start=True, stop=True).then_inc(filled[st], 1)

            def sums(st, tag, terms, bias=None):
                for b in range(G):
                    dst = bank(st, (tag, "y"))[:, b * 128:b * 128 + 128]
                    todo = list(terms(b))
                    if bias is not None:
                        todo.append((ones_at(bias), row(bias)))
                    for n, (l, r) in enumerate(todo):
                        last = mm(dst, l, r, start=(n == 0), stop=(n == len(todo) - 1))
                last.then_inc(filled[st], 1)

            def norm_turn(i, st, tag, slot):
                wait_emptied(pe, i, st, (tag, "y"))
                turn4(st, (tag, "n"), lambda b: normed[slot][:, b, :])

            def token(x, b):
                return x[:, b * T:b * T + T]

            def before_filling(i, item, *needed):
                held = [MAIN.before[item]] if MAIN.before[item] is not None else []
                wait_all_emptied(pe, i, MAIN, held + list(needed))

            def project(i, item):
                tag, kind, n = item[:3]
                x = {"sa": xT["a"], "ca": xT["b"] if kind == "q" else cT}[tag]
                if item == ("ca", "v", 0, 0):
                    pe.wait_ge(loaded_ca, n_ca[0])
                needed = {("sa", "k", 0): [("in", 0), ("in", 1)], ("ca", "q", 0): [("ln1", "n")]}
                before_filling(i, item, *needed.get(item, []))
                if kind == "v":
                    one(MAIN, item, token(x, item[3]), w_qkv[tag][:, 2, n * 512:n * 512 + 512])
                else:
                    one(MAIN, item, w_qkv[tag][:, "qk".index(kind), n * 128:n * 128 + 128], x[:, :])

            def scores(i, item):
                tag, _, u = item
                c, b0 = u // 2, 2 * (u % 2)
                before_filling(i, item, (tag, "k", c), (tag, "q", c))
                for n in range(2):
                    at = slice((b0 + n) * T, (b0 + n) * T + T)
                    mm(bank(MAIN, item)[:, n * 256:n * 256 + 256], queries[:, c % 2, at], keys[:, c % 2, :, at],
                       start=(n == 0), stop=False, skip_group_check=True)
                mask = (mask_sa if tag == "sa" else mask_ca)[:, b0:b0 + 2, :]
                mm(bank(MAIN, item), ident_h[:, :], mask.unsqueeze(2).broadcast_to([128, 2, 2, T]),
                   start=False, stop=True, skip_group_check=True).then_inc(filled[MAIN], 1)

            def turn(i, item):
                tag, _, u = item
                before_filling(i, item, (tag, "s", u))
                for h in range(4):
                    last = nc.tensor.transpose(bank(MAIN, item)[:, h * 128:h * 128 + 128],
                                               probs[:, u % 2, h * 128:h * 128 + 128], ident[:, :])
                last.then_inc(filled[MAIN], 1)

            def outputs(i, item):
                tag, _, u = item
                c, b0 = u // 2, 2 * (u % 2)
                first_use = [(tag, "v", c // 4, b) for b in range(G)] if u % (UNITS // 2) == 0 else []
                before_filling(i, item, (tag, "t", u), *first_use)
                for n in range(2):
                    for h in range(2):
                        at = ((b0 + n) * (H0 // 2) + 2 * (c % 4) + h) * (D0 + 1)
                        last = mm(bank(MAIN, item)[:, (2 * n + h) * 128:(2 * n + h) * 128 + 128],
                                  probsT[:, u % 2, (2 * n + h) * 128:(2 * n + h) * 128 + 128],
                                  values[:, c // 4, at:at + 128], start=True, stop=True)
                last.then_inc(filled[MAIN], 1)

            def turn_heads(i, item):
                tag, _, c = item
                before_filling(i, item, (tag, "o", 2 * c + 1))
                turn4(MAIN, item, lambda b: heads[:, c % 2, b, :])

            def main(i):
                for step in MAIN_STEPS:
                    for item in step:
                        tag, kind = item[:2]
                        if tag == "in":
                            if kind == 0:
                                pe.wait_ge(group_in, i.at(48, 48))
                            turn4(MAIN, item, lambda b: (c_in if kind else x_in)[:, b, :])
                        elif tag == "ffn":
                            before_filling(i, item, ("ln2", "n"))
                            one(MAIN, item, w_f1[:, kind * 128:kind * 128 + 128], xT["a"][:, :])
                        elif kind in ("q", "k", "v"):
                            if item == ("sa", "v", 0, 0):
                                pe.wait_ge(masks_taken, i.at(1, 1))
                            project(i, item)
                        elif kind == "s":
                            scores(i, item)
                        elif kind == "t":
                            turn(i, item)
                        elif kind == "o":
                            outputs(i, item)
                        elif kind == "ot":
                            turn_heads(i, item)
                        elif kind == "y":
                            if tag == "ln3":
                                before_filling(i, item, *[("ffn", c) for c in range(FC0)])
                                sums(MAIN, tag, lambda b: [(token(hidden[:, c, :], b), w_f2[:, c, :]) for c in range(FC0)]
                                     + [(token(xT["a"], b), ident[:, :])], 2)
                            else:
                                t, x, k = ("sa", xT["a"], 0) if tag == "ln1" else ("ca", xT["b"], 1)
                                before_filling(i, item, *[(t, "ot", c) for c in range(C0)])
                                sums(MAIN, tag, lambda b: [(token(headsT[:, c, :], b), w_o[t][:, c, :]) for c in range(C0)]
                                     + [(token(x, b), ident[:, :])], k)
                        elif kind == "n":
                            before_filling(i, item, (tag, "y"))
                            turn4(MAIN, item, lambda b: main_normed[:, b, :])
                            if tag == "ln3":
                                wait_emptied(pe, i, MAIN, item)
                    yield

            def attention_small(i, tag, width, value):
                hpb, d1 = ATTENTIONS[tag]
                for s in range(QUADS + 2):
                    if s >= 2:
                        u = s - 2
                        b, q = u // 4, u % 4
                        wait_emptied(pe, i, SIDE, (tag, "t", u))
                        if q == 0 and b:
                            wait_emptied(pe, i, SIDE, (tag, "o", b - 1))
                        for h in range(hpb):
                            at = (q * hpb + h) * d1
                            last = mm(bank(SIDE, (tag, "o", b))[:, at:at + d1], s_probsT[:, u % 2, h * 128:h * 128 + 128],
                                      value[:, b, q * hpb + h, :], start=True, stop=True)
                        if q == 3:
                            last.then_inc(filled[SIDE], 1)
                    if 1 <= s <= QUADS:
                        u = s - 1
                        wait_emptied(pe, i, SIDE, (tag, "s", u))
                        if u:
                            wait_emptied(pe, i, SIDE, (tag, "t", u - 1))
                        for h in range(hpb):
                            last = nc.tensor.transpose(bank(SIDE, (tag, "t", u))[:, h * 128:h * 128 + 128],
                                                       s_probs[:, u % 2, h * 128:h * 128 + 128], ident[:, :])
                        last.then_inc(filled[SIDE], 1)
                    if s < QUADS:
                        b, q = s // 4, s % 4
                        part = slice(32 * q, 32 * q + 32)
                        mm(bank(SIDE, (tag, "s", s))[:, 0:width * 128], qT[part, b * T:b * T + T],
                           kx[part, 0:width, b * T:b * T + T], start=True, stop=True).then_inc(filled[SIDE], 1)
                    yield
                wait_emptied(pe, i, SIDE, (tag, "o", G - 1))

            def token_values(name, src, w, bias):
                for b in range(G):
                    dst = bank(SIDE, name)[:, b * 128:b * 128 + 128]
                    mm(dst, token(src, b), w, start=True, stop=False)
                    last = mm(dst, ones_at(bias), row(bias), start=False, stop=True)
                last.then_inc(filled[SIDE], 1)

            def wT(n, r0=0):
                return turned[:, TURN[n, r0], :]

            def side(i):
                pe.wait_ge(handed, i.at(1, 1))
                one(SIDE, ("l1", "q"), wT("L1_xattn_Wq"), x_side[:, :])
                one(SIDE, ("l1", "k"), wT("L1_xattn_Wk"), c_side[:, :])
                token_values(("l1", "v"), c_side, wT("L1_xattn_Wv"), 3)
                yield
                yield
                pe.wait_ge(queries_ready, i.at(1, 1))
                pe.wait_ge(keys_ready, i.at(3, 2))
                wait_emptied(pe, i, SIDE, ("l1", "v"))
                yield from attention_small(i, "l1", 4, l1v)
                for blk, q_src, kv_src in (("en", c2T, c2T), ("d0", x1T, x1T), ("d1", x_side, encT)):
                    def w(k):
                        return w_sq[:, SQUARES.index(L2W[blk].format(k)), :]
                    if blk == "d1":
                        wait_emptied(pe, i, SIDE, ("d0", "n"))
                    one(SIDE, (blk, "q"), w("q"), q_src[:, :])
                    for k in "kv":
                        for b in range(G):
                            last = mm(bank(SIDE, (blk, k))[:, b * 128:b * 128 + 128], token(kv_src, b), w(k),
                                      start=True, stop=True)
                        last.then_inc(filled[SIDE], 1)
                    yield
                    yield
                    wait_emptied(pe, i, SIDE, (blk, "k"))
                    wait_emptied(pe, i, SIDE, (blk, "v"))
                    for b in range(G):
                        last = mm(bank(SIDE, (blk, "kv", b // 2))[:, (b % 2) * 129:(b % 2) * 129 + 129],
                                  l2k[:, b * 128:b * 128 + 128], l2v[:, b, :], start=True, stop=True)
                        if b % 2:
                            last.then_inc(filled[SIDE], 1)
                    yield
                    for n in range(2):
                        wait_emptied(pe, i, SIDE, (blk, "kv", n))
                    for b in range(G):
                        last = mm(bank(SIDE, (blk, "o", b // 2))[:, (b % 2) * 136:(b % 2) * 136 + 136],
                                  token(qT, b), kvb[:, b, :], start=True, stop=True)
                        if b % 2:
                            last.then_inc(filled[SIDE], 1)
                    yield
                    for n in range(2):
                        wait_emptied(pe, i, SIDE, (blk, "o", n))
                    turn4(SIDE, (blk, "ot"), lambda b: token(tok, b))
                    yield
                    wait_emptied(pe, i, SIDE, (blk, "ot"))
                    sums(SIDE, blk, lambda b: [(token(tokT, b), w("m"))])
                    yield
                    yield
                    norm_turn(i, SIDE, blk, 1)
                    yield
                    wait_emptied(pe, i, SIDE, (blk, "n"))
                    if blk != "d0":
                        src = encT if blk == "en" else x1T
                        for c in range(FC2):
                            one(SIDE, (blk, "f", c), w_l2f1[blk][:, c * 128:c * 128 + 128], src[:, :])
                        yield
                        wait_emptied(pe, i, SIDE, (blk, "f", FC2 - 1))
                        sums(SIDE, blk + "f", lambda b: [(token(l2h[:, c, :], b), w_l2f2[blk][:, c, :])
                                                         for c in range(FC2)])
                        yield
                        yield
                        norm_turn(i, SIDE, blk + "f", 1)
                        yield
                        wait_emptied(pe, i, SIDE, (blk + "f", "n"))
                turn4(SIDE, ("b3", "y"), lambda b: token(c_side, b))
                turn4(SIDE, ("x3", "y"), lambda b: token(x_side, b))
                yield
                norm_turn(i, SIDE, "b3", 1)
                norm_turn(i, SIDE, "x3", 2)
                yield
                wait_emptied(pe, i, SIDE, ("x3", "n"))
                one(SIDE, ("l3", "q"), wT("L3_xattn_W_qkv"), l3x)
                one(SIDE, ("l3", "k"), wT("L3_xattn_W_qkv", 128), l3b)
                token_values(("l3", "v"), l3b, wT("L3_xattn_W_qkv", 256), len(ROWS))
                yield
                yield
                pe.wait_ge(keys_ready, i.at(3, 3))
                wait_emptied(pe, i, SIDE, ("l3", "v"))
                wait_emptied(pe, i, SIDE, ("l3", "q"))
                yield from attention_small(i, "l3", 2, l3v)
                turn4(SIDE, ("l3", "ot"), lambda b: token(tok, b))
                yield
                wait_emptied(pe, i, SIDE, ("l3", "ot"))
                one(SIDE, ("l3", "x"), wT("L3_xattn_W_o"), tokT[:, :])
                yield
                wait_emptied(pe, i, SIDE, ("l3", "x"))
                turn4(SIDE, ("z3", "y"), lambda b: token(x1T, b))
                yield
                yield
                norm_turn(i, SIDE, "z3", 1)
                yield
                wait_emptied(pe, i, SIDE, ("z3", "n"))
                one(SIDE, ("l3", "z"), wT("L3_xattn_W_in"), l3x)
                yield
                wait_emptied(pe, i, SIDE, ("l3", "z"))
                one(SIDE, ("l3", "u"), w_b[:, :], zT)
                yield
                wait_emptied(pe, i, SIDE, ("l3", "u"))

            def setup_side():
                pe.wait_ge(loaded_rest, n_rest[0])
                for k, (n, r, c, r0) in enumerate(TURNED):
                    last = nc.tensor.transpose(ps[0:c, 5 + k // 4, (k % 4) * 128:(k % 4) * 128 + r],
                                               kx[0:r, k // 4, (k % 4) * 128:(k % 4) * 128 + c], ident[0:r, 0:r])
                last.then_inc(setup_filled, 1)
                pe.wait_ge(setup_emptied, 1)
                for b in range(B):
                    last = mm(ps[0:NP, 5, b:b + 1], prog_in[:, b, :], mean_col[:, :], start=True, stop=True)
                last.then_inc(setup_filled, 1)
                pe.wait_ge(setup_emptied, 2)
                mm(ps[:, 6, 0:B], turned[0:NP, TURN["L3_xattn_W_prog", 0], :], prog_mean[:, :],
                   start=True, stop=True).then_inc(setup_filled, 1)
                pe.wait_ge(setup_emptied, 3)

            passes(pe, main, side, setup_side)

            aT = turned[0:NS, TURN["L3_xattn_A", 0], :]

            def scan_step(t, k):
                pe.wait_ge(scan_add, t + k)
                mm(ps[:, 0, 0:B], aT, u_all[:, bass.ds(t + (k - 1), 1), :].rearrange("p a b -> p (a b)"),
                   start=True, stop=True).then_inc(scan_mm, 1)

            for k in range(1, SCAN_UNROLL):
                scan_step(0, k)
            with pe.Fori(0, T // SCAN_UNROLL - 1) as r:
                for k in range(SCAN_UNROLL):
                    scan_step(r * SCAN_UNROLL, SCAN_UNROLL + k)
            pe.wait_ge(scan_add, T)
            ub = u_all[:, :, :].rearrange("p t b -> p b t")
            with pe.Fori(0, GROUPS) as g:
                mm(ps[:, 1, :], w_c[:, :], ub[:, bass.ds(g * G, G), :], start=True, stop=True).then_inc(fin_mm, 1)
                pe.wait_ge(fin_add, g + 1)
                for b in range(G):
                    last = nc.tensor.transpose(ps[:, 2, b * 128:b * 128 + 128], cT[:, b * T:b * T + T], ident[:, :])
                last.then_inc(fin_turn, 1)
                pe.wait_ge(fin_copy, g + 1)

        @block.scalar
        def _(act):
            A = nc.scalar.activation
            act.wait_ge(setup_step, SETUP_FIRST)

            def take(i, st, name, dst, fn, view=None, width=512, **kw):
                wait_filled(act, i, st, name)
                s = bank(st, name)[:, 0:width]
                A(dst, view(s) if view else s, fn, **kw).then_inc(emptied[st, "A"], 1)

            def exps(i, st, tag, n, u, src_max, dst, hpb):
                act.wait_ge(max_ready[st], i.at(2 * QUADS, n * QUADS + u + 1))
                for h in range(hpb):
                    last = A(dst[:, u % 2, h * 128:h * 128 + 128], bank(st, (tag, "s", u))[:, h * 128:h * 128 + 128],
                             ACT.Exp, bias=src_max[:, u % 2, h:h + 1], scale=1.0)
                last.then_inc(emptied[st, "A"], 1)

            def main(i):
                for step in MAIN_STEPS:
                    for item in step:
                        if item[1] == "norm" or MAIN.by[item] == "D":
                            continue
                        tag, kind = item[:2]
                        if tag == "in":
                            take(i, MAIN, item, (cT if kind else xT["a"])[:, :], ACT.Copy)
                        elif tag == "ffn":
                            take(i, MAIN, item, hidden[:, kind, :], ACT.Relu,
                                 bias=cols["L0_xattn_ffn_b1"][:, kind:kind + 1], scale=1.0)
                        elif kind == "q":
                            c = item[2]
                            take(i, MAIN, item, queries[:, c % 2, :], ACT.Identity,
                                 bias=scaled_bq[tag][:, c:c + 1], scale=D0 ** -0.5)
                        elif kind == "k":
                            c = item[2]
                            wait_filled(act, i, MAIN, item)
                            for h in range(2):
                                rows_of = slice(64 * h, 64 * h + 64)
                                last = A(keys[rows_of, c % 2, h, :], bank(MAIN, item)[rows_of, :], ACT.Identity,
                                         bias=cols[f"L0_xattn_{tag}_bk"][rows_of, c:c + 1], scale=1.0)
                            last.then_inc(emptied[MAIN, "A"], 1)
                        elif kind == "s":
                            exps(i, MAIN, tag, 0 if tag == "sa" else 1, item[2], neg_max, probs, 4)
                        elif kind == "t":
                            take(i, MAIN, item, probsT[:, item[2] % 2, :], ACT.Copy)
                        elif kind == "ot":
                            take(i, MAIN, item, headsT[:, item[2], :], ACT.Copy)
                    yield

            def attention_small(i, tag, n):
                hpb, d1 = ATTENTIONS[tag]
                for s in range(QUADS + 2):
                    if 1 <= s <= QUADS and SIDE.by[tag, "t", s - 1] == "A":
                        take(i, SIDE, (tag, "t", s - 1), s_probsT[:, (s - 1) % 2, 0:hpb * 128], ACT.Copy, width=hpb * 128)
                    if s < QUADS:
                        exps(i, SIDE, tag, n, s, s_max, s_probs, hpb)
                    yield

            def side(i):
                take(i, SIDE, ("l1", "k"), k0[:, :], ACT.Relu, bias=v1("L1_xattn_bk"), scale=1.0)
                take(i, SIDE, ("l1", "v"), l1v[:, :, :, 0:D1], ACT.Relu,
                     view=lambda s: s.rearrange("p (g h d) -> p g h d", g=G, h=H1))
                yield
                yield
                yield from attention_small(i, "l1", 0)
                for n, blk in enumerate(("en", "d0", "d1")):
                    for m in range(2):
                        act.wait_ge(neg_ready, i.at(6, 2 * n + m + 1))
                        A(expn[m], neg[m], ACT.Exp).then_inc(exp_ready, 1)
                    take(i, SIDE, (blk, "v"), l2v[:, :, 0:128], ACT.Copy,
                         view=lambda s: s.rearrange("p (g n) -> p g n", g=G))
                    for _ in range(4):
                        yield
                    take(i, SIDE, (blk, "ot"), tokT[:, :], ACT.Copy)
                    yield
                    yield
                    yield
                    yield
                    if blk != "d0":
                        for c in range(FC2):
                            take(i, SIDE, (blk, "f", c), l2h[:, c, :], ACT.Relu)
                        yield
                        yield
                        yield
                        yield
                yield
                yield
                take(i, SIDE, ("l3", "k"), k0[:, :], ACT.Identity, bias=qkvb[:, 1:2], scale=1.0)
                take(i, SIDE, ("l3", "v"), l3v[:, :, :, 0:D3], ACT.Copy,
                     view=lambda s: s.rearrange("p (g h d) -> p g h d", g=G, h=H3))
                yield
                yield
                yield from attention_small(i, "l3", 1)
                take(i, SIDE, ("l3", "ot"), tokT[:, :], ACT.Copy)
                yield
                yield
                yield
                yield
                yield
                take(i, SIDE, ("l3", "z"), zT, ACT.Identity, bias=v1("L3_xattn_b_in"), scale=1.0)
                yield
                yield

            passes(act, main, side, lambda: None)

            def scan_step(t, k):
                act.wait_ge(scan_mm, t + k)
                A(state[:, :], ps[0:NS, 0, 0:B], ACT.Silu).then_inc(scan_silu, 1)

            for k in range(1, SCAN_UNROLL):
                scan_step(0, k)
            with act.Fori(0, T // SCAN_UNROLL - 1) as r:
                for k in range(SCAN_UNROLL):
                    scan_step(r * SCAN_UNROLL, SCAN_UNROLL + k)

        @block.vector
        def _(dve):
            V = nc.vector
            count = {setup_step: 0, main_step: 0, side_step: 0}
            each = {setup_step: SETUP_VSTEPS, main_step: MAIN_VSTEPS, side_step: SIDE_VSTEPS}

            def link(i, s, ins):
                count[s] += 1
                ins.then_inc(s, 1)
                dve.wait_ge(s, i.at(each[s], count[s]))

            once = Pass(None, 0)
            dve.wait_ge(consts_ready, n_const[0])
            link(once, setup_step, V.tensor_copy(ident_h[:, :], ident[:, :]))
            link(once, setup_step, V.tensor_copy(causal[:, :], main_normed[:, 0, :]))
            link(once, setup_step, V.tensor_reduce(quad8[:, :], head8[:, :].rearrange("p (g j) -> p j g", j=4), AX.X, ALU.add))
            link(once, setup_step, V.tensor_reduce(quad16[:, :], head16[:, :].rearrange("p (g j) -> p j g", j=2), AX.X, ALU.add))
            link(once, setup_step, V.memset(var_eps[:, :, :], 1.0))
            dve.wait_ge(setup_filled, 1)
            link(once, setup_step, V.tensor_copy(col_all[:, :], ps[:, 5, 0:NCOLS]))
            for t in ("sa", "ca"):
                link(once, setup_step, V.tensor_scalar(scaled_bq[t][:, :], cols[f"L0_xattn_{t}_bq"], D0 ** -0.5, None, ALU.mult))
            assert count[setup_step] == SETUP_FIRST, count

            def setup_side():
                dve.wait_ge(setup_filled, 2)
                for k, (n, r, c, r0) in enumerate(TURNED):
                    link(once, setup_step, V.tensor_copy(turned[0:c, k, 0:r],
                                                         ps[0:c, 5 + k // 4, (k % 4) * 128:(k % 4) * 128 + r]))
                V.memset(turned[0:NS, TURN["L3_xattn_A", 0], NS:128], 0.0).then_inc(setup_emptied, 1)
                dve.wait_ge(setup_filled, 3)
                V.tensor_copy(prog_mean[:, :], ps[0:NP, 5, 0:B]).then_inc(setup_emptied, 1)
                dve.wait_ge(setup_filled, 4)
                V.tensor_scalar(mod[:, :], ps[:, 6, 0:B], v1("L3_xattn_b_prog"), None, ALU.add).then_inc(setup_emptied, 1)

            def take(i, st, name, fn):
                wait_filled(dve, i, st, name)
                fn(bank(st, name)).then_inc(emptied[st, "D"], 1)

            def maxes(i, st, tag, u, dst, hpb):
                wait_filled(dve, i, st, (tag, "s", u))
                V.tensor_reduce(dst[:, u % 2, 0:hpb], bank(st, (tag, "s", u))[:, 0:hpb * 128].rearrange(
                    "p (h k) -> p h k", h=hpb), AX.X, ALU.max, negate=True).then_inc(max_ready[st], 1)

            def moments(i, st, tag, slot, step):
                wait_filled(dve, i, st, (tag, "y"))
                for b in range(G):
                    last = V.bn_stats(stats[:, slot, b, :], bank(st, (tag, "y"))[:, b * 128:b * 128 + 128])
                link(i, step, last)
                V.memset(scratch[:, 0:1], 0.0)
                for b in range(G):
                    last = V.bn_aggr(meanvar[:, slot, b, :], stats[:, slot, b, :])
                link(i, step, last)
                V.tensor_scalar(var_eps[:, slot, :].unsqueeze(2), meanvar[:, slot, :, 1:2], 1e-12 if st is MAIN else 1e-5,
                                None, ALU.add).then_inc(stats_ready[st], 1)

            def normalise(i, st, tag, slot):
                tags = MAIN_LN if st is MAIN else SIDE_LN
                dve.wait_ge(rstd_ready[st], i.at(len(tags), tags.index(tag) + 1))
                for b in range(G):
                    last = V.tensor_scalar(normed[slot][:, b, :], bank(st, (tag, "y"))[:, b * 128:b * 128 + 128],
                                           meanvar[:, slot, b, 0:1], rstd[:, slot, b:b + 1], ALU.subtract, ALU.mult)
                last.then_inc(emptied[st, "D"], 1)

            def gain(i, st, tag, dst):
                g, b = (v1(n) for n in GB[tag])
                if tag in RESIDUALS:
                    dve.wait_ge(residual_ready, i.at(len(RESIDUALS), RESIDUALS.index(tag) + 1))
                    take(i, st, (tag, "n"), lambda s: V.scalar_tensor_tensor(
                        out=dst, in0=s, scalar=g, in1=residual[:, :], op0=ALU.mult, op1=ALU.add))
                else:
                    take(i, st, (tag, "n"), lambda s: V.tensor_scalar(dst, s, g, b, ALU.mult, ALU.add))

            def norm_heads(i, item):
                tag, _, u = item
                c, b0 = u // 2, 2 * (u % 2)
                wait_filled(dve, i, MAIN, item)
                o = bank(MAIN, item).rearrange("p (h d) -> p h d", d=128)
                link(i, main_step, V.reciprocal(inv[:, :].unsqueeze(2), o[:, :, D0:D0 + 1]))
                for n in range(2):
                    two = slice(2 * n, 2 * n + 2)
                    last = V.scalar_tensor_tensor(out=heads[:, c % 2, b0 + n, :].rearrange("p (h d) -> p h d", d=D0),
                                                  in0=o[:, two, 0:D0], scalar=row_ok[tag][:, b0 + n:b0 + n + 1],
                                                  in1=inv[:, two].unsqueeze(2).broadcast_to([128, 2, D0]),
                                                  op0=ALU.mult, op1=ALU.mult)
                last.then_inc(emptied[MAIN, "D"], 1)

            def make_masks(i):
                dve.wait_ge(group_in, i.at(48, 48))
                link(i, main_step, V.tensor_scalar(mask_ca[:, :, :].rearrange("p g t -> p (g t)"), valid_in[:, :], 0.0, -BIG,
                                                   ALU.is_equal, ALU.mult))
                link(i, main_step, V.tensor_tensor(mask_sa[:, :, :], mask_ca[:, :, :],
                                                   causal[:, :].unsqueeze(1).broadcast_to([128, G, T]), ALU.min))
                for t, m in (("sa", mask_sa), ("ca", mask_ca)):
                    link(i, main_step, V.tensor_reduce(row_ok[t][:, :], m[:, :, :], AX.X, ALU.max))
                    last = V.tensor_scalar(row_ok[t][:, :], row_ok[t][:, :], -1.0, None, ALU.is_ge)
                    if t == "sa":
                        link(i, main_step, last)
                last.then_inc(masks_taken, 1)
                dve.wait_ge(masks_taken, i.at(1, 1))

            def main(i):
                count[main_step] = 0
                make_masks(i)
                for step in MAIN_STEPS:
                    for item in step:
                        if item[1] != "norm" and MAIN.by[item] == "A" and item[1] != "s":
                            continue
                        tag, kind = item[:2]
                        if tag == "in":
                            take(i, MAIN, item, lambda s: V.tensor_copy((cT if kind else xT["a"])[:, :], s))
                        elif tag == "ffn":
                            take(i, MAIN, item, lambda s: V.tensor_scalar(
                                hidden[:, kind, :], s, cols["L0_xattn_ffn_b1"][:, kind:kind + 1], 0.0, ALU.add, ALU.max))
                        elif kind == "s":
                            maxes(i, MAIN, tag, item[2], neg_max, 4)
                        elif kind == "q":
                            c = item[2]
                            take(i, MAIN, item, lambda s: V.tensor_scalar(
                                queries[:, c % 2, :], s, cols[f"L0_xattn_{tag}_bq"][:, c:c + 1], D0 ** -0.5, ALU.add, ALU.mult))
                        elif kind == "k":
                            c = item[2]
                            wait_filled(dve, i, MAIN, item)
                            for h in range(2):
                                rows_of = slice(64 * h, 64 * h + 64)
                                last = V.tensor_scalar(keys[rows_of, c % 2, h, :], bank(MAIN, item)[rows_of, :],
                                                       cols[f"L0_xattn_{tag}_bk"][rows_of, c:c + 1], None, ALU.add)
                            last.then_inc(emptied[MAIN, "D"], 1)
                        elif kind == "v":
                            o, b = item[2:]
                            take(i, MAIN, item, lambda s: V.tensor_tensor(
                                values_of(o, b)[:, :, 0:D0], s.rearrange("p (h d) -> p h d", d=D0),
                                bv_all[tag][:, o * 512:o * 512 + 512].rearrange("p (h d) -> p h d", d=D0), ALU.add))
                        elif kind == "t":
                            take(i, MAIN, item, lambda s: V.tensor_copy(probsT[:, item[2] % 2, :], s))
                        elif kind == "ot":
                            take(i, MAIN, item, lambda s: V.tensor_copy(headsT[:, item[2], :], s))
                        elif kind == "o":
                            norm_heads(i, item)
                        elif kind == "y":
                            moments(i, MAIN, tag, 0, main_step)
                        elif kind == "norm":
                            normalise(i, MAIN, tag, 0)
                        elif kind == "n":
                            gain(i, MAIN, tag, xT["a" if tag == "ln2" else "b"][:, :])
                    yield
                assert count[main_step] == MAIN_VSTEPS, count

            def hand_over(i):
                wait_emptied(dve, i, MAIN, ("ln3", "n"))
                V.tensor_scalar(x_side[:, :], xT["b"][:, :], 1.0, None, ALU.mult)
                V.tensor_scalar(c_side[:, :], cT[:, :], 1.0, None, ALU.mult)
                dve.wait_ge(skip_loaded, i.at(16, 16))
                V.tensor_scalar(attend[:, :], skip_in[:, :], 0.0, D1 ** -0.5, ALU.not_equal, ALU.mult).then_inc(handed, 1)

            def attention_small(i, tag):
                hpb, d1 = ATTENTIONS[tag]
                n, d = 4 * hpb, d1 - 1
                for s in range(QUADS + 2):
                    if s >= 2 and s % 4 == 1:
                        b = s // 4 - 1
                        wait_filled(dve, i, SIDE, (tag, "o", b))
                        o = bank(SIDE, (tag, "o", b))[:, 0:n * d1].rearrange("p (h d) -> p h d", d=d1)
                        link(i, side_step, V.reciprocal(s_inv[:, b % 2, 0:n].unsqueeze(2), o[:, :, d:d1]))
                        at = slice(b * T, b * T + T)
                        last = V.tensor_tensor(tok[:, at].rearrange("p (h d) -> p h d", d=d), o[:, :, 0:d],
                                               s_inv[:, b % 2, 0:n].unsqueeze(2).broadcast_to([128, n, d]), ALU.mult)
                        if tag == "l1":
                            link(i, side_step, last)
                            last = V.tensor_tensor(x1T[:, at], tok[:, at], x_side[:, at], ALU.add)
                        last.then_inc(emptied[SIDE, "D"], 1)
                    if 1 <= s <= QUADS and SIDE.by[tag, "t", s - 1] == "D":
                        take(i, SIDE, (tag, "t", s - 1), lambda x: V.tensor_copy(
                            s_probsT[:, (s - 1) % 2, 0:hpb * 128], x[:, 0:hpb * 128]))
                    if s < QUADS:
                        maxes(i, SIDE, tag, s, s_max, hpb)
                    yield

            def side(i):
                count[side_step] = 0
                wait_filled(dve, i, SIDE, ("l1", "q"))
                dve.wait_ge(handed, i.at(1, 1))
                V.tensor_scalar(neg_q, bank(SIDE, ("l1", "q")), v1("L1_xattn_bq"), 0.0, ALU.add, ALU.max).then_inc(emptied[SIDE, "D"], 1)
                yield
                yield
                yield from attention_small(i, "l1")
                for n, blk in enumerate(("en", "d0", "d1")):
                    both = (((blk, "q"), qT[:, :]), ((blk, "k"), l2k[:, :]))
                    for m, (name, _) in enumerate(both):
                        wait_filled(dve, i, SIDE, name)
                        V.tensor_scalar(neg[m], bank(SIDE, name), 0.0, None, ALU.min).then_inc(neg_ready, 1)
                    yield
                    for m, (name, dst) in enumerate(both):
                        dve.wait_ge(exp_ready, i.at(6, 2 * n + m + 1))
                        V.scalar_tensor_tensor(out=dst, in0=bank(SIDE, name), scalar=0.0, in1=expn[m],
                                               op0=ALU.max, op1=ALU.add).then_inc(emptied[SIDE, "D"], 1)
                    yield
                    for m in range(2):
                        name = (blk, "kv", m)
                        wait_filled(dve, i, SIDE, name)
                        s = bank(SIDE, name)[:, 0:258].rearrange("p (g n) -> p g n", g=2)
                        for g in range(2):
                            V.tensor_tensor(kvb[:, 2 * m + g, 0:128].rearrange("p (h d) -> p h d", d=D2),
                                            s[:, g, 0:128].rearrange("p (h d) -> p h d", d=D2),
                                            head16[:, :].unsqueeze(2).broadcast_to([128, H2, D2]), ALU.mult)
                        V.tensor_tensor(kvb[:, 2 * m:2 * m + 2, 128:136], s[:, :, 128:129].broadcast_to([128, 2, 8]),
                                        head16[:, :].unsqueeze(1).broadcast_to([128, 2, 8]), ALU.mult).then_inc(emptied[SIDE, "D"], 1)
                    yield
                    for m in range(2):
                        name = (blk, "o", m)
                        wait_filled(dve, i, SIDE, name)
                        s = bank(SIDE, name)[:, 0:272].rearrange("p (g n) -> p g n", g=2)
                        z = l2z[:, m, :].rearrange("p (g h) -> p g h", g=2)
                        link(i, side_step, V.tensor_scalar(z, s[:, :, 128:136], 1e-6, None, ALU.add))
                        link(i, side_step, V.reciprocal(z, z))
                        V.tensor_tensor(tok[:, 2 * m * 128:2 * m * 128 + 256].rearrange("p (g h d) -> p g h d", g=2, d=D2),
                                        s[:, :, 0:128].rearrange("p g (h d) -> p g h d", d=D2),
                                        z.unsqueeze(3).broadcast_to([128, 2, H2, D2]), ALU.mult).then_inc(emptied[SIDE, "D"], 1)
                    yield
                    yield
                    moments(i, SIDE, blk, 1, side_step)
                    yield
                    normalise(i, SIDE, blk, 1)
                    yield
                    gain(i, SIDE, blk, {"en": encT, "d0": x_side, "d1": x1T}[blk][:, :])
                    yield
                    if blk != "d0":
                        yield
                        moments(i, SIDE, blk + "f", 1, side_step)
                        yield
                        normalise(i, SIDE, blk + "f", 1)
                        yield
                        gain(i, SIDE, blk + "f", {"en": encT, "d1": x_side}[blk][:, :])
                        yield
                moments(i, SIDE, "b3", 1, side_step)
                moments(i, SIDE, "x3", 2, side_step)
                normalise(i, SIDE, "b3", 1)
                normalise(i, SIDE, "x3", 2)
                yield
                gain(i, SIDE, "b3", l3b)
                gain(i, SIDE, "x3", l3x)
                yield
                take(i, SIDE, ("l3", "q"), lambda s: V.tensor_scalar(qT[:, :], s, qkvb[:, 0:1], D3 ** -0.5, ALU.add, ALU.mult))
                yield
                yield
                yield from attention_small(i, "l3")
                yield
                take(i, SIDE, ("l3", "x"), lambda s: V.scalar_tensor_tensor(
                    out=x1T[:, :], in0=s, scalar=v1("L3_xattn_b_o"), in1=x_side[:, :], op0=ALU.add, op1=ALU.add))
                yield
                moments(i, SIDE, "z3", 1, side_step)
                yield
                normalise(i, SIDE, "z3", 1)
                yield
                gain(i, SIDE, "z3", l3x)
                yield
                yield
                def group(n):
                    return slice(i.offset * n, i.offset * n + n) if i.r is None else bass.ds(i.r * n + i.offset * n, n)
                link(i, side_step, V.tensor_tensor(x2_all[:, group(GT)].rearrange("p (g t) -> p g t", g=G),
                                                   x1T[:, :].rearrange("p (g t) -> p g t", g=G),
                                                   mod[:, group(G)].unsqueeze(2).broadcast_to([128, G, T]), ALU.add))
                take(i, SIDE, ("l3", "u"), lambda s: V.tensor_scalar(
                    u_all[:, :, group(G)].rearrange("p t g -> p g t"), s[0:NS, :].rearrange("p (g t) -> p g t", g=G),
                    0.0, None, ALU.add))
                assert count[side_step] == SIDE_VSTEPS, count
                yield

            interleave(main(once), None)
            setup_side()
            hand_over(once)
            with dve.Fori(0, GROUPS - 1) as r:
                interleave(main(Pass(r, 1)), side(Pass(r, 0)))
                hand_over(Pass(r, 1))
            assert alone(side(Pass(None, GROUPS - 1))) == SIDE_STEPS

            dve.wait_ge(emptied[SIDE, "D"], GROUPS * SIDE.total["D"])
            V.memset(scratch[:, 0:1], 1.0).then_inc(scan_add, 1)

            def scan_step(t, k):
                dve.wait_ge(scan_silu, t + k)
                s = u_all[:, bass.ds(t + k, 1), :].rearrange("p a b -> p (a b)")
                V.tensor_tensor(s, s, state[:, :], ALU.add).then_inc(scan_add, 1)

            for k in range(1, SCAN_UNROLL):
                scan_step(0, k)
            with dve.Fori(0, T // SCAN_UNROLL - 1) as r:
                for k in range(SCAN_UNROLL):
                    scan_step(r * SCAN_UNROLL, SCAN_UNROLL + k)
            with dve.Fori(0, GROUPS) as g:
                dve.wait_ge(fin_mm, g + 1)
                V.tensor_tensor(cT[:, :], ps[:, 1, :], x2_all[:, bass.ds(g * GT, GT)], ALU.add).then_inc(fin_add, 1)
                dve.wait_ge(fin_turn, g + 1)
                V.tensor_scalar(x2_all[:, bass.ds(g * GT, GT)], ps[:, 2, :], 0.0, None, ALU.add).then_inc(fin_copy, 1)


def kernel(**inputs):
    import concourse.bacc as _bacc
    from concourse.bass_utils import run_bass_kernel_spmd as _run

    nc = _bacc.Bacc("TRN2", target_bir_lowering=False, num_devices=1)
    arrays, aps = {}, {}
    for name, a in inputs.items():
        if name == "itok_BxS2_4_31999":
            continue
        a = np.ascontiguousarray(a)
        if a.dtype == np.bool_:
            a = a.view(np.uint8)
        arrays[f"in_{name}"] = a
        aps[name] = nc.dram_tensor(f"in_{name}", a.shape, mybir.dt.from_np(a.dtype), kind="ExternalInput").ap()
    out = nc.dram_tensor("out_0", (B, T, E), F32, kind="ExternalOutput").ap()
    build_program(nc, aps, out)
    r = _run(nc, [arrays], core_ids=[0])
    return r.results[0]["out_0"]
```

```python
from contextlib import ExitStack

import numpy as np
import concourse.bass as bass
from concourse import mybir

F32 = mybir.dt.float32
BF16 = mybir.dt.bfloat16
I32 = mybir.dt.int32
U8 = mybir.dt.uint8
ALU = mybir.AluOpType
ACT = mybir.ActivationFunctionType
AX = mybir.AxisListType

B, T, E = 32, 128, 128
G = 4
GROUPS = B // G
GT = G * T
H0, D0 = 16, 64
C0 = H0 * D0 // 128
H1, D1 = 16, 8
H2, D2 = 8, 16
H3, D3 = 8, 16
FC0 = 4
FC2 = 2
NS = 64
NP = 64
BIG = 2.0 ** 100
SMALL = {"l1": (H1 // 4, D1 + 1), "l3": (H3 // 4, D3 + 1)}
SMALL_UNITS = G * (H1 + H3) // 4
UNITS = C0 * G // 2


def main_steps():
    steps = [[("in", 0)], [("in", 1)], [("sa", "k", 0)], [("sa", "q", 0)]]
    steps += [[("sa", "v", 0, b)] for b in range(G)]

    def attention(tag):
        for s in range(UNITS + 3):
            c = s // 2 + 1
            first = [(tag, "s", s)] if s < UNITS else []
            if c < C0:
                first.append((tag, "qk"[s % 2 == 0], c))
            elif tag == "sa" and s < UNITS + 2:
                first.append(("ca", "v", 0, s - UNITS + 2))
            second = [(tag, "scale", s - 1)] if 1 <= s <= UNITS else []
            if 2 <= s < UNITS + 2:
                second.append((tag, "t", s - 2))
            third = [(tag, "o", s - 3)] if s >= 3 else []
            if tag == "sa" and s % 2 and s < 2 * G:
                third.append((tag, "v", 1, s // 2))
            steps.extend(x for x in (first, second, third) if x)

    attention("sa")
    steps.append([("ln1", "y")])
    steps += [[("ca", "v", 1, b)] for b in range(G)]
    steps += [[("ln1", "norm"), ("ca", "k", 0)], [("ln1", "n")], [("ca", "q", 0)]]
    attention("ca")
    steps += [[("ln2", "y")], [], [], [("ln2", "norm")], [("ln2", "n")], []]
    steps += [[("ffn", 0), ("ffn", 1)], [("ffn", 2), ("ffn", 3)], []]
    steps += [[("ln3", "y")], [], [], [("ln3", "norm")], [("ln3", "n")]]
    return steps


MAIN_STEPS = main_steps()
NO_FILL = ("scale", "norm")
IDLE = 1
SIDE_PACE = ([8] * (2 + IDLE) + [4] * (SMALL["l1"][0] * G + 2) + [3] * 37
             + [4] * (SMALL["l3"][0] * G + 2) + [4] * 7)
SIDE_STEPS = len(SIDE_PACE)
SETUP_STEPS = 9


class Stream:

    def __init__(self, fills):
        self.order = [name for name, _, _ in fills]
        self.fill = {name: n + 1 for n, name in enumerate(self.order)}
        self.bank = {name: bank for name, bank, _ in fills}
        self.by = {name: by for name, _, by in fills}
        self.total = {"A": 0, "D": 0}
        self.rank = {}
        for name, _, by in fills:
            self.total[by] += 1
            self.rank[name] = self.total[by]
        self.fills = len(fills)
        self.before, last = {}, {}
        for name, bank, _ in fills:
            self.before[name] = last.get(bank)
            last[bank] = name


def main_fills():
    order, n = [], 0
    for item in (x for step in MAIN_STEPS for x in step if x[1] not in NO_FILL):
        tag, kind = item[:2]
        if kind == "s":
            bank = item[2] % 2
        elif kind == "o":
            bank = 3
        elif kind == "y":
            bank = 0
        elif item[:3] == ("ca", "v", 1) and item[3] < 2:
            bank = (1, 3)[item[3]]
        else:
            bank, n = (2, 4)[n % 2], n + 1
        if kind in ("v", "y", "n"):
            by = "D"
        elif kind in ("k", "o") or tag in ("ffn", "in"):
            by = "AD"[item[-1] % 2]
        else:
            by = "A"
        order.append((item, bank, by))
    return order


def side_fills():
    order = []

    def attention(tag):
        per = SMALL[tag][0]
        for u in range(per * G + 2):
            if u >= 2 and (u - 1) % per == 0:
                order.append(((tag, "o", (u - 2) // per), 7, "D"))
            if 1 <= u <= per * G:
                order.append(((tag, "t", u - 1), 6, "AD"[u % 2]))
            if u < per * G:
                order.append(((tag, "s", u), 5, "A"))

    order += [(("l1", "q"), 5, "D"), (("l1", "k"), 6, "A"), (("l1", "v"), 7, "A")]
    attention("l1")
    for blk in ("en", "d0", "d1"):
        order += [((blk, "q"), 5, "D"), ((blk, "k"), 6, "D"), ((blk, "v"), 7, "A"),
                  ((blk, "kv", 0), 5, "D"), ((blk, "kv", 1), 6, "D"),
                  ((blk, "o", 0), 7, "D"), ((blk, "o", 1), 5, "D"), ((blk, "ot"), 6, "A"),
                  ((blk, "y"), 7, "D"), ((blk, "n"), 5, "D")]
        if blk != "d0":
            order += [((blk, "f", 0), 6, "A"), ((blk, "f", 1), 7, "A"),
                      ((blk + "f", "y"), 5, "D"), ((blk + "f", "n"), 6, "D")]
    order += [(("b3", "y"), 5, "D"), (("x3", "y"), 7, "D"), (("b3", "n"), 6, "D"), (("x3", "n"), 5, "D"),
              (("l3", "q"), 6, "D"), (("l3", "k"), 7, "A"), (("l3", "v"), 5, "A")]
    attention("l3")
    order += [(("l3", "ot"), 5, "A"), (("l3", "x"), 6, "D"), (("z3", "y"), 7, "D"), (("z3", "n"), 5, "D"),
              (("l3", "z"), 6, "A"), (("l3", "u"), 7, "D")]
    return order


MAIN, SIDE = Stream(main_fills()), Stream(side_fills())
MAIN_LN = ("ln1", "ln2", "ln3")
SIDE_LN = ("en", "enf", "d0", "d1", "d1f", "b3", "x3", "z3")
RESIDUALS = ("en", "enf", "d0", "d1", "d1f")

COLUMNS = ("L0_xattn_sa_bo", "L0_xattn_ca_bo", "L0_xattn_ffn_b2", "L0_xattn_sa_bq", "L0_xattn_sa_bk",
           "L0_xattn_ca_bq", "L0_xattn_ca_bk", "L0_xattn_ffn_b1")
VECTORS = ("L0_xattn_ln1_g", "L0_xattn_ln1_b", "L0_xattn_ln2_g", "L0_xattn_ln2_b", "L0_xattn_ln3_g",
           "L0_xattn_ln3_b", "L1_xattn_bq", "L1_xattn_bk", "L2_xattn_e_g1", "L2_xattn_e_b1",
           "L2_xattn_e_g2", "L2_xattn_e_b2", "L2_xattn_d_g0", "L2_xattn_d_b0", "L2_xattn_d_g1",
           "L2_xattn_d_b1", "L2_xattn_d_g2", "L2_xattn_d_b2", "L3_xattn_b_in", "L3_xattn_b_o",
           "L3_xattn_b_prog", "L3_xattn_g1", "L3_xattn_beta1", "L3_xattn_g2", "L3_xattn_beta2")
COLUMN_WIDTH = {n: {"bo": 1, "b2": 1, "b1": FC0}.get(n[-2:], C0) for n in COLUMNS}
COLUMN_WIDTH["L3_xattn_b_qkv"] = 3
COLUMN_WIDTH.update({n: 1 for n in VECTORS})
COLUMN_AT, NCOLS = {}, 0
for _name, _width in COLUMN_WIDTH.items():
    COLUMN_AT[_name] = NCOLS
    NCOLS += _width
ROWS = ("L1_xattn_bv",)
GB = {"ln1": ("L0_xattn_ln1_g", "L0_xattn_ln1_b"), "ln2": ("L0_xattn_ln2_g", "L0_xattn_ln2_b"),
      "ln3": ("L0_xattn_ln3_g", "L0_xattn_ln3_b"), "en": ("L2_xattn_e_g1", "L2_xattn_e_b1"),
      "enf": ("L2_xattn_e_g2", "L2_xattn_e_b2"), "d0": ("L2_xattn_d_g0", "L2_xattn_d_b0"),
      "d1": ("L2_xattn_d_g1", "L2_xattn_d_b1"), "d1f": ("L2_xattn_d_g2", "L2_xattn_d_b2"),
      "b3": ("L3_xattn_g1", "L3_xattn_beta1"), "x3": ("L3_xattn_g1", "L3_xattn_beta1"),
      "z3": ("L3_xattn_g2", "L3_xattn_beta2")}
SQUARES = ("L2_xattn_e_wq", "L2_xattn_e_wk", "L2_xattn_e_wv", "L2_xattn_e_wm", "L2_xattn_d_wq0",
           "L2_xattn_d_wk0", "L2_xattn_d_wv0", "L2_xattn_d_wm0", "L2_xattn_d_wq1", "L2_xattn_d_wk1",
           "L2_xattn_d_wv1", "L2_xattn_d_wm1")
L2W = {"en": "L2_xattn_e_w{}", "d0": "L2_xattn_d_w{}0", "d1": "L2_xattn_d_w{}1"}
TURNED = (("L1_xattn_Wq", 128, 128, 0), ("L1_xattn_Wk", 128, 128, 0), ("L1_xattn_Wv", 128, 128, 0),
          ("L3_xattn_W_qkv", 128, 128, 0), ("L3_xattn_W_qkv", 128, 128, 128),
          ("L3_xattn_W_qkv", 128, 128, 256), ("L3_xattn_W_o", 128, 128, 0),
          ("L3_xattn_W_in", 128, 128, 0), ("L3_xattn_W_prog", 128, 64, 0), ("L3_xattn_A", 64, 64, 0))
TURN = {(n, r0): k for k, (n, _, _, r0) in enumerate(TURNED)}

MAIN_VSTEPS = 43
SIDE_VSTEPS = 41
SETUP_FIRST = 8
SETUP_VSTEPS = 18
SCAN_UNROLL = 16


class Pass:

    def __init__(self, r, offset):
        self.r, self.offset = r, offset

    def at(self, each, n):
        known = self.offset * each + n
        return known if self.r is None else self.r * each + known


def interleave(main, side, pace=SIDE_PACE):
    taken, due = 0, 0
    for n, _ in enumerate(main):
        while side is not None and taken < len(pace) and due * len(MAIN_STEPS) < (n + 1) * sum(pace):
            next(side)
            due += pace[taken]
            taken += 1
    assert side is None or next(side, "end") == "end"


def alone(stream):
    return sum(1 for _ in stream)


def build_program(nc, I, out):
    with ExitStack() as ctx:
        def sb(name, shape, dt=F32):
            return ctx.enter_context(nc.sbuf_tensor(name, shape, dt))

        def sem(name):
            return ctx.enter_context(nc.semaphore(name))

        ps = ctx.enter_context(nc.psum_tensor("ps", [128, 8, 512], F32))

        ident = sb("ident", [128, 128])
        ident_h = sb("ident_h", [128, 128], BF16)
        causal = sb("causal", [128, 128], BF16)
        head16 = sb("head16", [128, 8])
        head8 = sb("head8", [128, 16])
        quad8 = sb("quad8", [128, 4])
        quad16 = sb("quad16", [128, 4])
        ones = sb("ones", [64, 128])
        mean_col = sb("mean_col", [128, 1])
        minus_half = sb("minus_half", [128, G])
        w_qkv = {t: sb(f"w_qkv_{t}", [128, 3, H0 * D0]) for t in ("sa", "ca")}
        w_o = {t: sb(f"w_o_{t}", [128, C0, E]) for t in ("sa", "ca")}
        bv_all = {t: sb(f"bv_all_{t}", [128, H0 * D0]) for t in ("sa", "ca")}
        w_f1 = sb("w_f1", [128, FC0 * 128])
        w_f2 = sb("w_f2", [128, FC0, E])
        w_sq = sb("w_sq", [128, len(SQUARES), 128])
        w_l2f1 = {b: sb(f"w_l2f1_{b}", [128, FC2 * 128]) for b in ("en", "d1")}
        w_l2f2 = {b: sb(f"w_l2f2_{b}", [128, FC2, E]) for b in ("en", "d1")}
        turned = sb("turned", [128, len(TURNED), 128])
        w_b = sb("w_b", [128, NS])
        w_c = sb("w_c", [NS, E])
        col_all = sb("col_all", [128, NCOLS])
        cols = {n: col_all[:, COLUMN_AT[n]:COLUMN_AT[n] + w] for n, w in COLUMN_WIDTH.items()}
        qkvb = cols["L3_xattn_b_qkv"]
        rows = sb("rows", [64, 128])
        scaled_bq = {t: sb(f"scaled_bq_{t}", [128, C0]) for t in ("sa", "ca")}
        x_in = sb("x_in", [128, G, E])
        c_in = sb("c_in", [128, G, E])
        valid_in = sb("valid_in", [128, GT], U8)
        skip_in = sb("skip_in", [128, GT], I32)
        cT = sb("cT", [128, GT])
        main_residual = sb("main_residual", [128, GT])
        xT = {n: sb("xT_" + n, [128, GT]) for n in ("a", "b")}
        queries = sb("queries", [128, 2, GT])
        keys = sb("keys", [128, 2, 2, GT])
        headsT = sb("headsT", [128, C0, GT])
        hidden = headsT[:, 0:FC0, :]
        values = sb("values", [128, 2, G, H0 * D0 // 2])
        mask_sa = sb("mask_sa", [128, G, T], BF16)
        mask_ca = sb("mask_ca", [128, G, T], BF16)
        row_ok = {"sa": sb("row_ok_sa", [128, G]), "ca": sb("row_ok_ca", [128, G])}
        neg_max = sb("neg_max", [128, 2, 4])
        probs = sb("probs", [128, 3, 512])
        probsT = sb("probsT", [128, 2, 512])
        prob_sums = sb("prob_sums", [128, 3, 4])
        inv = sb("inv", [128, 3, 4])
        col_rows = headsT[0:NCOLS, 0, 0:128]
        stats = sb("stats", [128, 3, G, 6])
        meanvar = sb("meanvar", [128, 3, G, 2])
        var_eps = sb("var_eps", [128, 3, G])
        rstd = sb("rstd", [128, 3, G])
        main_normed = sb("main_normed", [128, G, E])
        scratch = sb("scratch", [128, 1])
        pool_scratch = sb("pool_scratch", [128, 8])
        x_side = sb("x_side", [128, GT])
        c_side = sb("c_side", [128, GT])
        qT = sb("qT", [128, GT])
        attend = qT
        kx = sb("kx", [128, 4, GT])
        l1v = sb("l1v", [128, G, H1, D1 + 1])
        l2v = sb("l2v", [128, G, 129])
        l3v = sb("l3v", [128, G, H3, D3 + 1])
        x1T = sb("x1T", [128, GT])
        encT = sb("encT", [128, GT])
        c2T = encT
        s_max = sb("s_max", [128, 2, 4])
        s_probs = sb("s_probs", [128, 2, 512])
        s_probsT = sb("s_probsT", [128, 2, 512])
        s_inv = sb("s_inv", [128, 2, 16])
        l2z = sb("l2z", [128, 2, 2 * H2])
        tok = sb("tok", [128, GT])
        tokT = kx[:, 3, :]
        k0, neg_q = s_probsT[:, 0, :], s_probsT[:, 1, :]
        residual = neg_q
        normed = [main_normed, tok[:, :].rearrange("p (g e) -> p g e", g=G),
                  s_probs[:, 0, :].rearrange("p (g e) -> p g e", g=G)]
        l2k, kvb = k0, s_probs[:, :, :].rearrange("p a n -> p (a n)")[:, 0:G * 136].rearrange("p (g n) -> p g n", g=G)
        neg = [kx[:, 0, :], kx[:, 1, :]]
        expn = [kx[:, 2, :], kx[:, 3, :]]
        fin_sum = cT, c_side
        l2h = kx[:, 0:2, :]
        l3b, l3x = encT[:, :], s_probsT[:, 1, :]
        zT = kx[:, 0, :]
        x2_all = sb("x2_all", [128, B * T])
        u_all = sb("u_all", [NS, T, B])
        prog_in = x2_all[:, 0:B * NP].rearrange("p (b n) -> p b n", b=B)
        mod = sb("mod", [128, B])
        state = sb("state", [NS, 2, B])
        prog_mean = state[:, 0, :]

        loaded_first = sem("loaded_first")
        loaded_ca = sem("loaded_ca")
        loaded_rest = sem("loaded_rest")
        group_in = sem("group_in")
        skip_loaded = sem("skip_loaded")
        masks_taken = sem("masks_taken")
        handed = sem("handed")
        consts_ready = sem("consts_ready")
        setup_filled = sem("setup_filled")
        setup_emptied = sem("setup_emptied")
        setup_step = sem("setup_step")
        filled = {MAIN: sem("filled_main"), SIDE: sem("filled_side")}
        emptied = {(MAIN, "A"): sem("emptied_main_scalar"), (MAIN, "D"): sem("emptied_main_vector"),
                   (SIDE, "A"): sem("emptied_side_scalar"), (SIDE, "D"): sem("emptied_side_vector")}
        main_step, side_step = sem("main_step"), sem("side_step")
        max_ready = {MAIN: sem("max_ready_main"), SIDE: sem("max_ready_side")}
        scaled = sem("scaled")
        stats_ready = {MAIN: sem("stats_ready_main"), SIDE: sem("stats_ready_side")}
        rstd_ready = {MAIN: sem("rstd_ready_main"), SIDE: sem("rstd_ready_side")}
        queries_ready = sem("queries_ready")
        keys_ready = sem("keys_ready")
        neg_ready = sem("neg_ready")
        exp_ready = sem("exp_ready")
        residual_ready = sem("residual_ready")
        main_residual_ready = sem("main_residual_ready")
        scan_mm = sem("scan_mm")
        scan_silu = sem("scan_silu")
        scan_add = sem("scan_add")
        fin_mm = sem("fin_mm")
        fin_add = sem("fin_add")
        fin_turn = sem("fin_turn")
        fin_copy = sem("fin_copy")
        stored = sem("stored")
        block = ctx.enter_context(nc.Block())

        def v1(name):
            return cols[name]

        def row(k):
            return rows[32 * k:32 * k + 1, :]

        def ones_at(k):
            return ones[32 * k:32 * k + 1, :]

        def bank(st, name):
            return ps[:, st.bank[name], :]

        def wait_filled(eng, i, st, name):
            eng.wait_ge(filled[st], i.at(st.fills, st.fill[name]))

        def wait_emptied(eng, i, st, name):
            by = st.by[name]
            eng.wait_ge(emptied[st, by], i.at(st.total[by], st.rank[name]))

        def head_of(item, h):
            c, b0 = item[2] // 2, 2 * (item[2] % 2)
            part = slice(64 * h, 64 * h + 64)
            return (headsT[part, c, b0 * T:(b0 + 2) * T].rearrange("p (b q) -> p b q", b=2),
                    bank(MAIN, item)[part, :].rearrange("p (b h q) -> p b h q", b=2, h=2)[:, :, h, :])

        def wait_all_emptied(eng, i, st, names):
            last = {}
            for name in names:
                by = st.by[name]
                last[by] = max(last.get(by, 0), st.rank[name])
            for by, rank in last.items():
                eng.wait_ge(emptied[st, by], i.at(st.total[by], rank))

        def passes(eng, main, side, setup):
            interleave(main(Pass(None, 0)), setup, [1] * SETUP_STEPS)
            with eng.Fori(0, GROUPS - 1) as r:
                interleave(main(Pass(r, 1)), side(Pass(r, 0)))
            assert alone(side(Pass(None, GROUPS - 1))) == SIDE_STEPS

        n_first, n_ca, n_rest, n_const = [0], [0], [0], [0]

        @block.sync
        def _(sp):
            def load(s, n, dst, src):
                sp.dma_start(dst, src).then_inc(s, 16)
                n[0] += 16

            def load_inputs(g):
                for dst, name in ((x_in, "x"), (c_in, "ctx_1024")):
                    sp.dma_start(dst[:, :, :], I[name][g * G:g * G + G, :, :].rearrange("g t e -> t g e")).then_inc(group_in, 16)

            def load_valid(g):
                m = I["mask_BxS2_bf1"].rearrange("b t -> (b t)")[g * GT:g * GT + GT].partition_broadcast(128)
                sp.dma_start(valid_in[:, :], m).then_inc(group_in, 16)

            def load_skip(g):
                m = I["mask_BxS_ik0"].rearrange("b t -> (b t)")[g * GT:g * GT + GT].partition_broadcast(128)
                sp.dma_start(skip_in[:, :], m).then_inc(skip_loaded, 16)

            load_inputs(0)
            load_valid(0)
            for t, s, n in (("sa", loaded_first, n_first), ("ca", loaded_ca, n_ca)):
                for k, c in enumerate("qkv"):
                    load(s, n, w_qkv[t][:, k, :], I[f"L0_xattn_{t}_w{c}"])
                load(s, n, bv_all[t][:, :], I[f"L0_xattn_{t}_bv"].partition_broadcast(128))
                if t == "ca":
                    for o in ("sa", "ca"):
                        load(s, n, w_o[o][:, :, :], I[f"L0_xattn_{o}_wo"].rearrange("(c p) n -> p c n", p=128))
                if t == "sa":
                    for c, w in COLUMN_WIDTH.items():
                        load(s, n, col_rows[COLUMN_AT[c]:COLUMN_AT[c] + w, :], I[c].rearrange("(c p) -> c p", p=128))
            load(loaded_ca, n_ca, w_f1[:, :], I["L0_xattn_ffn_w1"])
            load(loaded_ca, n_ca, w_f2[:, :, :], I["L0_xattn_ffn_w2"].rearrange("(c p) n -> p c n", p=128))
            for k, c in enumerate(ROWS):
                load(loaded_rest, n_rest, row(k), I[c].rearrange("(a n) -> a n", a=1))
            load(loaded_rest, n_rest, row(len(ROWS)), I["L3_xattn_b_qkv"].rearrange("(a n) -> a n", a=1)[:, 256:384])
            for k, c in enumerate(SQUARES):
                load(loaded_rest, n_rest, w_sq[:, k, :], I[c])
            for b, c in (("en", "e"), ("d1", "d")):
                load(loaded_rest, n_rest, w_l2f1[b][:, :], I[f"L2_xattn_{c}_w1"])
                load(loaded_rest, n_rest, w_l2f2[b][:, :, :], I[f"L2_xattn_{c}_w2"].rearrange("(c p) n -> p c n", p=128))
            load(loaded_rest, n_rest, w_b[:, :], I["L3_xattn_Bmat"])
            load(loaded_rest, n_rest, w_c[:, :], I["L3_xattn_Cmat"])
            for k, (c, r, w, r0) in enumerate(TURNED):
                load(loaded_rest, n_rest, kx[0:r, k // 4, (k % 4) * 128:(k % 4) * 128 + w], I[c][r0:r0 + r, :])
            load(loaded_rest, n_rest, prog_in, I["ctxb_2048x64"].rearrange("b t n -> t b n"))
            load_skip(0)
            for g in range(1, GROUPS):
                wait_filled(sp, Pass(None, g - 1), MAIN, ("in", 1))
                load_inputs(g)
                sp.wait_ge(masks_taken, g)
                load_valid(g)
                sp.wait_ge(handed, g)
                load_skip(g)
            o = out.rearrange("b t e -> t b e")
            for g in range(GROUPS):
                sp.wait_ge(fin_copy, g + 1)
                sp.dma_start(o[:, g * G:g * G + G, :],
                             x2_all[:, g * GT:g * GT + GT].rearrange("p (g e) -> p g e", g=G)).then_inc(stored, 16)
            sp.wait_ge(stored, 16 * GROUPS)

        @block.gpsimd
        def _(pool):
            P = nc.gpsimd
            step = [0]

            def link(ins):
                step[0] += 1
                ins.then_inc(consts_ready, 1)
                pool.wait_ge(consts_ready, step[0])

            def select(m, op, fill, base, pattern, mult):
                link(P.affine_select(out=m, in_=m, compare_op=op, fill=fill, base=base, pattern=pattern,
                                     channel_multiplier=mult))

            def band(m, n, width):
                link(P.memset(m, 1.0))
                select(m, ALU.is_ge, 0.0, 0, [[-width, n]], 1)
                select(m, ALU.is_ge, 0.0, width - 1, [[width, n]], -1)

            link(P.memset(ident[:, :], 0.0))
            select(ident[:, :], ALU.not_equal, 1.0, 0, [[-1, 128]], 1)
            link(P.memset(main_normed[:, 0, :], 0.0))
            select(main_normed[:, 0, :], ALU.is_ge, -BIG, 0, [[-1, 128]], 1)
            band(head16[:, :], 8, 16)
            band(head8[:, :], 16, 8)
            link(P.memset(ones[:, :], 1.0))
            link(P.memset(mean_col[:, :], 1.0 / T))
            link(P.memset(minus_half[:, :], -0.5))
            link(P.memset(keys[64:128, :, 0, :], 0.0))
            link(P.memset(keys[0:64, :, 1, :], 0.0))
            link(P.memset(l1v[:, :, :, D1:D1 + 1], 1.0))
            link(P.memset(l2v[:, :, 128:129], 1.0))
            link(P.memset(l3v[:, :, :, D3:D3 + 1], 1.0))
            n_const[0] = step[0]

            def carry_wait(n):
                P.tensor_tensor(pool_scratch[:, n:n + 1], minus_half[:, 0:1], minus_half[:, 0:1], ALU.mult)

            def root(i, st, tag, slot):
                tags = MAIN_LN if st is MAIN else SIDE_LN
                pool.wait_ge(stats_ready[st], i.at(len(tags), tags.index(tag) + 1))
                P.tensor_tensor(rstd[:, slot, :], var_eps[:, slot, :], minus_half[:, :], ALU.pow).then_inc(rstd_ready[st], 1)

            def main(i):
                kept = {("in", 0): ("a", "sa_bo"), ("ln1", "n"): ("b", "ca_bo"), ("ln2", "n"): ("a", "ffn_b2")}
                for step in MAIN_STEPS:
                    for item in step:
                        if item[1] == "y":
                            root(i, MAIN, item[0], 0)
                        if item in kept:
                            x, bias = kept[item]
                            wait_emptied(pool, i, MAIN, item)
                            carry_wait(5 + [*kept].index(item))
                            P.tensor_scalar(main_residual[:, :], xT[x][:, :], v1("L0_xattn_" + bias), None,
                                            ALU.add).then_inc(main_residual_ready, 1)
                    yield

            def side(i):
                def spread(n, name, quad):
                    wait_emptied(pool, i, SIDE, name)
                    carry_wait(n)
                    for j in range(4):
                        last = P.tensor_scalar(kx[:, j, :], k0[:, :], quad[:, j:j + 1], None, ALU.mult)
                    last.then_inc(keys_ready, 1)

                def keep_residual(k, src, b):
                    carry_wait(3 + k)
                    P.tensor_scalar(residual[:, :], src, v1(b), None, ALU.add).then_inc(residual_ready, 1)

                pool.wait_ge(handed, i.at(1, 1))
                yield
                carry_wait(2)
                P.tensor_scalar(c2T[:, :], c_side[:, :], 2.0, None, ALU.mult).then_inc(keys_ready, 1)
                wait_emptied(pool, i, SIDE, ("l1", "q"))
                P.tensor_tensor(qT[:, :], neg_q, attend[:, :], ALU.mult).then_inc(queries_ready, 1)
                spread(0, ("l1", "k"), quad8)
                yield
                for _ in range(IDLE):
                    yield
                for _ in range(SMALL["l1"][0] * G + 2):
                    yield
                for blk in ("en", "d0", "d1"):
                    if blk == "en":
                        pool.wait_ge(keys_ready, i.at(3, 1))
                        wait_emptied(pool, i, SIDE, ("l1", "o", G - 1))
                        keep_residual(0, c2T[:, :], GB["en"][1])
                    elif blk == "d0":
                        wait_emptied(pool, i, SIDE, ("enf", "n"))
                        keep_residual(1, x1T[:, :], GB["d0"][1])
                    else:
                        wait_emptied(pool, i, SIDE, ("d0", "n"))
                        keep_residual(2, x_side[:, :], GB["d1"][1])
                    for _ in range(6):
                        yield
                    root(i, SIDE, blk, 1)
                    yield
                    yield
                    if blk != "d0":
                        src = encT if blk == "en" else x1T
                        wait_emptied(pool, i, SIDE, (blk, "n"))
                        keep_residual(3 + (blk == "d1"), src[:, :], GB[blk + "f"][1])
                        yield
                        root(i, SIDE, blk + "f", 1)
                        yield
                        yield
                        yield
                root(i, SIDE, "b3", 1)
                root(i, SIDE, "x3", 2)
                yield
                yield
                yield
                yield
                spread(1, ("l3", "k"), quad16)
                yield
                for _ in range(SMALL["l3"][0] * G + 2):
                    yield
                yield
                yield
                root(i, SIDE, "z3", 1)
                yield
                yield
                yield
                yield
                yield

            passes(pool, main, side, None)

        @block.tensor
        def _(pe):
            mm = nc.tensor.matmul
            pe.wait_ge(consts_ready, n_const[0])
            pe.wait_ge(loaded_first, n_first[0])
            nc.tensor.transpose(ps[:, 5, 0:NCOLS], col_rows[:, :], ident[0:NCOLS, 0:NCOLS]).then_inc(setup_filled, 1)

            def turn4(st, name, src):
                for b in range(G):
                    last = nc.tensor.transpose(bank(st, name)[:, b * 128:b * 128 + 128], src(b), ident[:, :])
                last.then_inc(filled[st], 1)

            def one(st, name, lhs, rhs):
                mm(bank(st, name)[0:lhs.shape[-1], :], lhs, rhs, start=True, stop=True).then_inc(filled[st], 1)

            def sums(st, tag, terms):
                for b in range(G):
                    dst = bank(st, (tag, "y"))[:, b * 128:b * 128 + 128]
                    todo = list(terms(b))
                    for n, (l, r) in enumerate(todo):
                        last = mm(dst, l, r, start=(n == 0), stop=(n == len(todo) - 1))
                last.then_inc(filled[st], 1)

            def norm_turn(i, st, tag, slot):
                wait_emptied(pe, i, st, (tag, "y"))
                turn4(st, (tag, "n"), lambda b: normed[slot][:, b, :])

            def token(x, b):
                return x[:, b * T:b * T + T]

            def before_filling(i, item, *needed):
                held = [MAIN.before[item]] if MAIN.before[item] is not None else []
                wait_all_emptied(pe, i, MAIN, held + list(needed))

            def project(i, item):
                tag, kind, n = item[:3]
                x = {"sa": xT["a"], "ca": xT["b"] if kind == "q" else cT}[tag]
                if item == ("ca", "v", 0, 0):
                    pe.wait_ge(loaded_ca, n_ca[0])
                needed = {("sa", "k", 0): [("in", 0), ("in", 1)], ("ca", "q", 0): [("ln1", "n")]}
                before_filling(i, item, *needed.get(item, []))
                if kind == "v":
                    one(MAIN, item, token(x, item[3]), w_qkv[tag][:, 2, n * 512:n * 512 + 512])
                else:
                    one(MAIN, item, w_qkv[tag][:, "qk".index(kind), n * 128:n * 128 + 128], x[:, :])

            def scores(i, item):
                tag, _, u = item
                c, b0 = u // 2, 2 * (u % 2)
                before_filling(i, item, (tag, "k", c), (tag, "q", c))
                for n in range(2):
                    at = slice((b0 + n) * T, (b0 + n) * T + T)
                    mm(bank(MAIN, item)[:, n * 256:n * 256 + 256], queries[:, c % 2, at], keys[:, c % 2, :, at],
                       start=(n == 0), stop=False, skip_group_check=True)
                mask = (mask_sa if tag == "sa" else mask_ca)[:, b0:b0 + 2, :]
                mm(bank(MAIN, item), ident_h[:, :], mask.unsqueeze(2).broadcast_to([128, 2, 2, T]),
                   start=False, stop=True, skip_group_check=True).then_inc(filled[MAIN], 1)

            def turn(i, item):
                tag, _, u = item
                before_filling(i, item)
                pe.wait_ge(scaled, i.at(2 * UNITS, u + 1 + (0 if tag == "sa" else UNITS)))
                for h in range(4):
                    last = nc.tensor.transpose(bank(MAIN, item)[:, h * 128:h * 128 + 128],
                                               probs[:, u % 3, h * 128:h * 128 + 128], ident[:, :])
                last.then_inc(filled[MAIN], 1)

            def outputs(i, item):
                tag, _, u = item
                c, b0 = u // 2, 2 * (u % 2)
                first_use = [(tag, "v", c // 4, b) for b in range(G)] if u % (UNITS // 2) == 0 else []
                before_filling(i, item, (tag, "t", u), *first_use)
                for n in range(2):
                    last = mm(bank(MAIN, item)[:, n * 256:n * 256 + 256],
                              values[:, c // 4, b0 + n, (c % 4) * 128:(c % 4) * 128 + 128],
                              probsT[:, u % 2, n * 256:n * 256 + 256], start=True, stop=True)
                last.then_inc(filled[MAIN], 1)

            def main(i):
                for step in MAIN_STEPS:
                    for item in step:
                        tag, kind = item[:2]
                        if tag == "in":
                            if kind == 0:
                                pe.wait_ge(group_in, i.at(48, 48))
                            turn4(MAIN, item, lambda b: (c_in if kind else x_in)[:, b, :])
                        elif tag == "ffn":
                            before_filling(i, item, ("ln2", "n"))
                            one(MAIN, item, w_f1[:, kind * 128:kind * 128 + 128], xT["a"][:, :])
                        elif kind in ("q", "k", "v"):
                            if item == ("sa", "v", 0, 0):
                                pe.wait_ge(masks_taken, i.at(1, 1))
                            project(i, item)
                        elif kind == "s":
                            scores(i, item)
                        elif kind == "t":
                            turn(i, item)
                        elif kind == "o":
                            outputs(i, item)
                        elif kind == "y":
                            pe.wait_ge(main_residual_ready, i.at(3, MAIN_LN.index(tag) + 1))
                            if tag == "ln3":
                                before_filling(i, item, *[("ffn", c) for c in range(FC0)])
                                sums(MAIN, tag, lambda b: [(token(hidden[:, c, :], b), w_f2[:, c, :]) for c in range(FC0)]
                                     + [(token(main_residual, b), ident[:, :])])
                            else:
                                t = "sa" if tag == "ln1" else "ca"
                                before_filling(i, item, *[(t, "o", u) for u in range(UNITS)])
                                sums(MAIN, tag, lambda b: [(token(headsT[:, c, :], b), w_o[t][:, c, :]) for c in range(C0)]
                                     + [(token(main_residual, b), ident[:, :])])
                        elif kind == "n":
                            before_filling(i, item, (tag, "y"))
                            turn4(MAIN, item, lambda b: main_normed[:, b, :])
                            if tag == "ln3":
                                wait_emptied(pe, i, MAIN, item)
                    yield

            def attention_small(i, tag, value):
                per, d1 = SMALL[tag]
                features = 128 // per
                for s in range(per * G + 2):
                    if s >= 2:
                        u = s - 2
                        b, q = u // per, u % per
                        wait_emptied(pe, i, SIDE, (tag, "t", u))
                        if q == 0 and b:
                            wait_emptied(pe, i, SIDE, (tag, "o", b - 1))
                        for h in range(4):
                            at = (q * 4 + h) * d1
                            last = mm(bank(SIDE, (tag, "o", b))[:, at:at + d1], s_probsT[:, u % 2, h * 128:h * 128 + 128],
                                      value[:, b, q * 4 + h, :], start=True, stop=True)
                        if q == per - 1:
                            last.then_inc(filled[SIDE], 1)
                    if 1 <= s <= per * G:
                        u = s - 1
                        wait_emptied(pe, i, SIDE, (tag, "s", u))
                        if u:
                            wait_emptied(pe, i, SIDE, (tag, "t", u - 1))
                        for h in range(4):
                            last = nc.tensor.transpose(bank(SIDE, (tag, "t", u))[:, h * 128:h * 128 + 128],
                                                       s_probs[:, u % 2, h * 128:h * 128 + 128], ident[:, :])
                        last.then_inc(filled[SIDE], 1)
                    if s < per * G:
                        b, q = s // per, s % per
                        part = slice(features * q, features * q + features)
                        mm(bank(SIDE, (tag, "s", s)), qT[part, b * T:b * T + T],
                           kx[part, :, b * T:b * T + T], start=True, stop=True).then_inc(filled[SIDE], 1)
                    yield
                wait_emptied(pe, i, SIDE, (tag, "o", G - 1))

            def token_values(name, src, w, bias):
                for b in range(G):
                    dst = bank(SIDE, name)[:, b * 128:b * 128 + 128]
                    mm(dst, token(src, b), w, start=True, stop=False)
                    last = mm(dst, ones_at(bias), row(bias), start=False, stop=True)
                last.then_inc(filled[SIDE], 1)

            def wT(n, r0=0):
                return turned[:, TURN[n, r0], :]

            def side(i):
                pe.wait_ge(handed, i.at(1, 1))
                one(SIDE, ("l1", "q"), wT("L1_xattn_Wq"), x_side[:, :])
                one(SIDE, ("l1", "k"), wT("L1_xattn_Wk"), c_side[:, :])
                token_values(("l1", "v"), c_side, wT("L1_xattn_Wv"), 0)
                yield
                yield
                for _ in range(IDLE):
                    yield
                pe.wait_ge(queries_ready, i.at(1, 1))
                pe.wait_ge(keys_ready, i.at(3, 2))
                wait_emptied(pe, i, SIDE, ("l1", "v"))
                yield from attention_small(i, "l1", l1v)
                for blk, q_src, kv_src in (("en", c2T, c2T), ("d0", x1T, x1T), ("d1", x_side, encT)):
                    def w(k):
                        return w_sq[:, SQUARES.index(L2W[blk].format(k)), :]
                    if blk == "d1":
                        wait_emptied(pe, i, SIDE, ("d0", "n"))
                    one(SIDE, (blk, "q"), w("q"), q_src[:, :])
                    for k in "kv":
                        for b in range(G):
                            last = mm(bank(SIDE, (blk, k))[:, b * 128:b * 128 + 128], token(kv_src, b), w(k),
                                      start=True, stop=True)
                        last.then_inc(filled[SIDE], 1)
                    yield
                    yield
                    wait_emptied(pe, i, SIDE, (blk, "k"))
                    wait_emptied(pe, i, SIDE, (blk, "v"))
                    for b in range(G):
                        last = mm(bank(SIDE, (blk, "kv", b // 2))[:, (b % 2) * 129:(b % 2) * 129 + 129],
                                  l2k[:, b * 128:b * 128 + 128], l2v[:, b, :], start=True, stop=True)
                        if b % 2:
                            last.then_inc(filled[SIDE], 1)
                    yield
                    for n in range(2):
                        wait_emptied(pe, i, SIDE, (blk, "kv", n))
                    for b in range(G):
                        last = mm(bank(SIDE, (blk, "o", b // 2))[:, (b % 2) * 136:(b % 2) * 136 + 136],
                                  token(qT, b), kvb[:, b, :], start=True, stop=True)
                        if b % 2:
                            last.then_inc(filled[SIDE], 1)
                    yield
                    for n in range(2):
                        wait_emptied(pe, i, SIDE, (blk, "o", n))
                    turn4(SIDE, (blk, "ot"), lambda b: token(tok, b))
                    yield
                    wait_emptied(pe, i, SIDE, (blk, "ot"))
                    sums(SIDE, blk, lambda b: [(token(tokT, b), w("m"))])
                    yield
                    yield
                    norm_turn(i, SIDE, blk, 1)
                    yield
                    wait_emptied(pe, i, SIDE, (blk, "n"))
                    if blk != "d0":
                        src = encT if blk == "en" else x1T
                        for c in range(FC2):
                            one(SIDE, (blk, "f", c), w_l2f1[blk][:, c * 128:c * 128 + 128], src[:, :])
                        yield
                        wait_emptied(pe, i, SIDE, (blk, "f", FC2 - 1))
                        sums(SIDE, blk + "f", lambda b: [(token(l2h[:, c, :], b), w_l2f2[blk][:, c, :])
                                                         for c in range(FC2)])
                        yield
                        yield
                        norm_turn(i, SIDE, blk + "f", 1)
                        yield
                        wait_emptied(pe, i, SIDE, (blk + "f", "n"))
                turn4(SIDE, ("b3", "y"), lambda b: token(c_side, b))
                turn4(SIDE, ("x3", "y"), lambda b: token(x_side, b))
                yield
                yield
                norm_turn(i, SIDE, "b3", 1)
                norm_turn(i, SIDE, "x3", 2)
                yield
                wait_emptied(pe, i, SIDE, ("x3", "n"))
                one(SIDE, ("l3", "q"), wT("L3_xattn_W_qkv"), l3x)
                one(SIDE, ("l3", "k"), wT("L3_xattn_W_qkv", 128), l3b)
                token_values(("l3", "v"), l3b, wT("L3_xattn_W_qkv", 256), len(ROWS))
                yield
                yield
                pe.wait_ge(keys_ready, i.at(3, 3))
                wait_emptied(pe, i, SIDE, ("l3", "v"))
                wait_emptied(pe, i, SIDE, ("l3", "q"))
                yield from attention_small(i, "l3", l3v)
                turn4(SIDE, ("l3", "ot"), lambda b: token(tok, b))
                yield
                wait_emptied(pe, i, SIDE, ("l3", "ot"))
                one(SIDE, ("l3", "x"), wT("L3_xattn_W_o"), tokT[:, :])
                yield
                wait_emptied(pe, i, SIDE, ("l3", "x"))
                turn4(SIDE, ("z3", "y"), lambda b: token(x1T, b))
                yield
                yield
                norm_turn(i, SIDE, "z3", 1)
                yield
                wait_emptied(pe, i, SIDE, ("z3", "n"))
                one(SIDE, ("l3", "z"), wT("L3_xattn_W_in"), l3x)
                yield
                wait_emptied(pe, i, SIDE, ("l3", "z"))
                one(SIDE, ("l3", "u"), w_b[:, :], zT)
                yield
                wait_emptied(pe, i, SIDE, ("l3", "u"))

            def setup_side():
                for _ in range(SETUP_STEPS - 4):
                    yield
                pe.wait_ge(loaded_rest, n_rest[0])
                for k, (n, r, c, r0) in enumerate(TURNED):
                    last = nc.tensor.transpose(ps[0:c, 5 + k // 4, (k % 4) * 128:(k % 4) * 128 + r],
                                               kx[0:r, k // 4, (k % 4) * 128:(k % 4) * 128 + c], ident[0:r, 0:r])
                last.then_inc(setup_filled, 1)
                yield
                pe.wait_ge(setup_emptied, 1)
                for b in range(B):
                    last = mm(ps[0:NP, 5, b:b + 1], prog_in[:, b, :], mean_col[:, :], start=True, stop=True)
                last.then_inc(setup_filled, 1)
                yield
                pe.wait_ge(setup_emptied, 2)
                mm(ps[:, 6, 0:B], turned[0:NP, TURN["L3_xattn_W_prog", 0], :], prog_mean,
                   start=True, stop=True).then_inc(setup_filled, 1)
                yield
                pe.wait_ge(setup_emptied, 3)
                yield

            passes(pe, main, side, setup_side())

            aT = turned[0:NS, TURN["L3_xattn_A", 0], :]

            def scan_step(t, k):
                first = k == 1
                last = mm(ps[:, k % 2, 0:B], aT, u_all[:, bass.ds(t + (k - 1), 1), :].rearrange("p a b -> p (a b)"),
                          start=True, stop=first, skip_group_check=True)
                if not first:
                    pe.wait_ge(scan_silu, t + (k - 1))
                    last = mm(ps[:, k % 2, 0:B], aT, state[:, (k - 1) % 2, :], start=False, stop=True,
                              skip_group_check=True)
                last.then_inc(scan_mm, 1)

            for k in range(1, SCAN_UNROLL):
                scan_step(0, k)
            with pe.Fori(0, T // SCAN_UNROLL - 1) as r:
                for k in range(SCAN_UNROLL):
                    scan_step(r * SCAN_UNROLL, SCAN_UNROLL + k)
            pe.wait_ge(scan_add, T - 1)
            ub = u_all[:, :, :].rearrange("p t b -> p b t")
            with pe.Fori(0, GROUPS // 2) as g:
                for n in range(2):
                    mm(ps[:, n, :], w_c[:, :], ub[:, bass.ds(g * 2 * G + n * G, G), :], start=True, stop=True).then_inc(fin_mm, 1)
                for n in range(2):
                    pe.wait_ge(fin_add, g * 2 + (n + 1))
                    for b in range(G):
                        last = nc.tensor.transpose(ps[:, 2 + n, b * 128:b * 128 + 128],
                                                   fin_sum[n][:, b * T:b * T + T], ident[:, :])
                    last.then_inc(fin_turn, 1)
                pe.wait_ge(fin_copy, g * 2 + 2)

        @block.scalar
        def _(act):
            A = nc.scalar.activation
            act.wait_ge(setup_step, SETUP_FIRST)

            def take(i, st, name, dst, fn, view=None, width=512, **kw):
                wait_filled(act, i, st, name)
                s = bank(st, name)[:, 0:width]
                A(dst, view(s) if view else s, fn, **kw).then_inc(emptied[st, "A"], 1)

            def exps(i, st, tag, before, u, src_max, dst, sums=None):
                act.wait_ge(max_ready[st], i.at(2 * UNITS if st is MAIN else SMALL_UNITS, before + u + 1))
                for h in range(4):
                    last = A(dst[:, u % dst.shape[1], h * 128:h * 128 + 128], bank(st, (tag, "s", u))[:, h * 128:h * 128 + 128],
                             ACT.Exp, bias=src_max[:, u % 2, h:h + 1], scale=1.0,
                             **({} if sums is None else {"accum_out": sums[:, u % 3, h:h + 1]}))
                last.then_inc(emptied[st, "A"], 1)

            def main(i):
                for step in MAIN_STEPS:
                    for item in step:
                        if item[1] in NO_FILL or MAIN.by[item] == "D":
                            continue
                        tag, kind = item[:2]
                        if tag == "in":
                            take(i, MAIN, item, (cT if kind else xT["a"])[:, :], ACT.Copy)
                        elif tag == "ffn":
                            take(i, MAIN, item, hidden[:, kind, :], ACT.Relu,
                                 bias=cols["L0_xattn_ffn_b1"][:, kind:kind + 1], scale=1.0)
                        elif kind == "q":
                            c = item[2]
                            take(i, MAIN, item, queries[:, c % 2, :], ACT.Identity,
                                 bias=scaled_bq[tag][:, c:c + 1], scale=D0 ** -0.5)
                        elif kind == "k":
                            c = item[2]
                            wait_filled(act, i, MAIN, item)
                            for h in range(2):
                                rows_of = slice(64 * h, 64 * h + 64)
                                last = A(keys[rows_of, c % 2, h, :], bank(MAIN, item)[rows_of, :], ACT.Identity,
                                         bias=cols[f"L0_xattn_{tag}_bk"][rows_of, c:c + 1], scale=1.0)
                            last.then_inc(emptied[MAIN, "A"], 1)
                        elif kind == "s":
                            exps(i, MAIN, tag, 0 if tag == "sa" else UNITS, item[2], neg_max, probs, prob_sums)
                        elif kind == "o":
                            wait_filled(act, i, MAIN, item)
                            for h in range(2):
                                dst, src = head_of(item, h)
                                last = A(dst, src, ACT.Copy)
                            last.then_inc(emptied[MAIN, "A"], 1)
                        elif kind == "t":
                            take(i, MAIN, item, probsT[:, item[2] % 2, :], ACT.Copy)
                    yield

            def attention_small(i, tag, before):
                units = SMALL[tag][0] * G
                for s in range(units + 2):
                    if 1 <= s <= units and SIDE.by[tag, "t", s - 1] == "A":
                        take(i, SIDE, (tag, "t", s - 1), s_probsT[:, (s - 1) % 2, :], ACT.Copy)
                    if s < units:
                        exps(i, SIDE, tag, before, s, s_max, s_probs)
                    yield

            def side(i):
                take(i, SIDE, ("l1", "k"), k0[:, :], ACT.Relu, bias=v1("L1_xattn_bk"), scale=1.0)
                take(i, SIDE, ("l1", "v"), l1v[:, :, :, 0:D1], ACT.Relu,
                     view=lambda s: s.rearrange("p (g h d) -> p g h d", g=G, h=H1))
                yield
                yield
                for _ in range(IDLE):
                    yield
                yield from attention_small(i, "l1", 0)
                for n, blk in enumerate(("en", "d0", "d1")):
                    for m in range(2):
                        act.wait_ge(neg_ready, i.at(6, 2 * n + m + 1))
                        A(expn[m], neg[m], ACT.Exp).then_inc(exp_ready, 1)
                    take(i, SIDE, (blk, "v"), l2v[:, :, 0:128], ACT.Copy,
                         view=lambda s: s.rearrange("p (g n) -> p g n", g=G))
                    for _ in range(4):
                        yield
                    take(i, SIDE, (blk, "ot"), tokT[:, :], ACT.Copy)
                    yield
                    yield
                    yield
                    yield
                    if blk != "d0":
                        for c in range(FC2):
                            take(i, SIDE, (blk, "f", c), l2h[:, c, :], ACT.Relu)
                        yield
                        yield
                        yield
                        yield
                yield
                yield
                yield
                take(i, SIDE, ("l3", "k"), k0[:, :], ACT.Identity, bias=qkvb[:, 1:2], scale=1.0)
                take(i, SIDE, ("l3", "v"), l3v[:, :, :, 0:D3], ACT.Copy,
                     view=lambda s: s.rearrange("p (g h d) -> p g h d", g=G, h=H3))
                yield
                yield
                yield from attention_small(i, "l3", SMALL["l1"][0] * G)
                take(i, SIDE, ("l3", "ot"), tokT[:, :], ACT.Copy)
                yield
                yield
                yield
                yield
                yield
                take(i, SIDE, ("l3", "z"), zT, ACT.Identity, bias=v1("L3_xattn_b_in"), scale=1.0)
                yield
                yield

            passes(act, main, side, None)

            def scan_step(t, k):
                act.wait_ge(scan_mm, t + k)
                if k > 2:
                    act.wait_ge(scan_add, t + (k - 2))
                A(state[:, k % 2, :], ps[0:NS, k % 2, 0:B], ACT.Silu).then_inc(scan_silu, 1)

            for k in range(1, SCAN_UNROLL):
                scan_step(0, k)
            with act.Fori(0, T // SCAN_UNROLL - 1) as r:
                for k in range(SCAN_UNROLL):
                    scan_step(r * SCAN_UNROLL, SCAN_UNROLL + k)

        @block.vector
        def _(dve):
            V = nc.vector
            count = {setup_step: 0, main_step: 0, side_step: 0}
            each = {setup_step: SETUP_VSTEPS, main_step: MAIN_VSTEPS, side_step: SIDE_VSTEPS}

            def link(i, s, ins):
                count[s] += 1
                ins.then_inc(s, 1)
                dve.wait_ge(s, i.at(each[s], count[s]))

            once = Pass(None, 0)
            dve.wait_ge(consts_ready, n_const[0])
            link(once, setup_step, V.tensor_copy(ident_h[:, :], ident[:, :]))
            link(once, setup_step, V.tensor_copy(causal[:, :], main_normed[:, 0, :]))
            link(once, setup_step, V.tensor_reduce(quad8[:, :], head8[:, :].rearrange("p (g j) -> p j g", j=4), AX.X, ALU.add))
            link(once, setup_step, V.tensor_reduce(quad16[:, :], head16[:, :].rearrange("p (g j) -> p j g", j=4), AX.X, ALU.add))
            link(once, setup_step, V.memset(var_eps[:, :, :], 1.0))
            dve.wait_ge(setup_filled, 1)
            link(once, setup_step, V.tensor_copy(col_all[:, :], ps[:, 5, 0:NCOLS]))
            for t in ("sa", "ca"):
                link(once, setup_step, V.tensor_scalar(scaled_bq[t][:, :], cols[f"L0_xattn_{t}_bq"], D0 ** -0.5, None, ALU.mult))
            assert count[setup_step] == SETUP_FIRST, count

            def setup_side():
                for _ in range(SETUP_STEPS - 3):
                    yield
                dve.wait_ge(setup_filled, 2)
                for k, (n, r, c, r0) in enumerate(TURNED):
                    link(once, setup_step, V.tensor_copy(turned[0:c, k, 0:r],
                                                         ps[0:c, 5 + k // 4, (k % 4) * 128:(k % 4) * 128 + r]))
                V.memset(turned[0:NS, TURN["L3_xattn_A", 0], NS:128], 0.0).then_inc(setup_emptied, 1)
                yield
                dve.wait_ge(setup_filled, 3)
                V.tensor_copy(prog_mean, ps[0:NP, 5, 0:B]).then_inc(setup_emptied, 1)
                yield
                dve.wait_ge(setup_filled, 4)
                V.tensor_scalar(mod[:, :], ps[:, 6, 0:B], v1("L3_xattn_b_prog"), None, ALU.add).then_inc(setup_emptied, 1)
                yield

            def take(i, st, name, fn):
                wait_filled(dve, i, st, name)
                fn(bank(st, name)).then_inc(emptied[st, "D"], 1)

            def maxes(i, st, tag, u, dst):
                wait_filled(dve, i, st, (tag, "s", u))
                V.tensor_reduce(dst[:, u % 2, :], bank(st, (tag, "s", u)).rearrange(
                    "p (h k) -> p h k", h=4), AX.X, ALU.max, negate=True).then_inc(max_ready[st], 1)

            def moments(i, st, tag, slot, step):
                wait_filled(dve, i, st, (tag, "y"))
                for b in range(G):
                    last = V.bn_stats(stats[:, slot, b, :], bank(st, (tag, "y"))[:, b * 128:b * 128 + 128])
                link(i, step, last)
                V.memset(scratch[:, 0:1], 0.0)
                for b in range(G):
                    last = V.bn_aggr(meanvar[:, slot, b, :], stats[:, slot, b, :])
                link(i, step, last)
                V.tensor_scalar(var_eps[:, slot, :].unsqueeze(2), meanvar[:, slot, :, 1:2], 1e-12 if st is MAIN else 1e-5,
                                None, ALU.add).then_inc(stats_ready[st], 1)

            def normalise(i, st, tag, slot):
                tags = MAIN_LN if st is MAIN else SIDE_LN
                dve.wait_ge(rstd_ready[st], i.at(len(tags), tags.index(tag) + 1))
                for b in range(G):
                    last = V.tensor_scalar(normed[slot][:, b, :], bank(st, (tag, "y"))[:, b * 128:b * 128 + 128],
                                           meanvar[:, slot, b, 0:1], rstd[:, slot, b:b + 1], ALU.subtract, ALU.mult)
                last.then_inc(emptied[st, "D"], 1)

            def gain(i, st, tag, dst):
                g, b = (v1(n) for n in GB[tag])
                if tag in RESIDUALS:
                    dve.wait_ge(residual_ready, i.at(len(RESIDUALS), RESIDUALS.index(tag) + 1))
                    take(i, st, (tag, "n"), lambda s: V.scalar_tensor_tensor(
                        out=dst, in0=s, scalar=g, in1=residual[:, :], op0=ALU.mult, op1=ALU.add))
                else:
                    take(i, st, (tag, "n"), lambda s: V.tensor_scalar(dst, s, g, b, ALU.mult, ALU.add))

            def scale_probs(i, item):
                tag, _, u = item
                b0 = 2 * (u % 2)
                wait_emptied(dve, i, MAIN, (tag, "s", u))
                link(i, main_step, V.reciprocal(inv[:, u % 3, :], prob_sums[:, u % 3, :]))
                for n in range(2):
                    p = probs[:, u % 3, n * 256:n * 256 + 256].rearrange("p (h k) -> p h k", h=2)
                    last = V.scalar_tensor_tensor(out=p, in0=p, scalar=row_ok[tag][:, b0 + n:b0 + n + 1],
                                                  in1=inv[:, u % 3, 2 * n:2 * n + 2].unsqueeze(2).broadcast_to([128, 2, T]),
                                                  op0=ALU.mult, op1=ALU.mult)
                last.then_inc(scaled, 1)

            def make_masks(i):
                dve.wait_ge(group_in, i.at(48, 48))
                link(i, main_step, V.tensor_scalar(mask_ca[:, :, :].rearrange("p g t -> p (g t)"), valid_in[:, :], 0.0, -BIG,
                                                   ALU.is_equal, ALU.mult))
                link(i, main_step, V.tensor_tensor(mask_sa[:, :, :], mask_ca[:, :, :],
                                                   causal[:, :].unsqueeze(1).broadcast_to([128, G, T]), ALU.min))
                for t, m in (("sa", mask_sa), ("ca", mask_ca)):
                    link(i, main_step, V.tensor_reduce(row_ok[t][:, :], m[:, :, :], AX.X, ALU.max))
                    last = V.tensor_scalar(row_ok[t][:, :], row_ok[t][:, :], -1.0, None, ALU.is_ge)
                    if t == "sa":
                        link(i, main_step, last)
                last.then_inc(masks_taken, 1)
                dve.wait_ge(masks_taken, i.at(1, 1))

            def main(i):
                count[main_step] = 0
                make_masks(i)
                for step in MAIN_STEPS:
                    for item in step:
                        if item[1] not in NO_FILL + ("s",) and MAIN.by[item] == "A":
                            continue
                        tag, kind = item[:2]
                        if tag == "in":
                            take(i, MAIN, item, lambda s: V.tensor_copy((cT if kind else xT["a"])[:, :], s))
                        elif tag == "ffn":
                            take(i, MAIN, item, lambda s: V.tensor_scalar(
                                hidden[:, kind, :], s, cols["L0_xattn_ffn_b1"][:, kind:kind + 1], 0.0, ALU.add, ALU.max))
                        elif kind == "s":
                            maxes(i, MAIN, tag, item[2], neg_max)
                        elif kind == "q":
                            c = item[2]
                            take(i, MAIN, item, lambda s: V.tensor_scalar(
                                queries[:, c % 2, :], s, cols[f"L0_xattn_{tag}_bq"][:, c:c + 1], D0 ** -0.5, ALU.add, ALU.mult))
                        elif kind == "k":
                            c = item[2]
                            wait_filled(dve, i, MAIN, item)
                            for h in range(2):
                                rows_of = slice(64 * h, 64 * h + 64)
                                last = V.tensor_scalar(keys[rows_of, c % 2, h, :], bank(MAIN, item)[rows_of, :],
                                                       cols[f"L0_xattn_{tag}_bk"][rows_of, c:c + 1], None, ALU.add)
                            last.then_inc(emptied[MAIN, "D"], 1)
                        elif kind == "v":
                            o, b = item[2:]
                            take(i, MAIN, item, lambda s: V.tensor_tensor(
                                values[:, o, b, :], s, bv_all[tag][:, o * 512:o * 512 + 512], ALU.add))
                        elif kind == "t":
                            take(i, MAIN, item, lambda s: V.tensor_copy(probsT[:, item[2] % 2, :], s))
                        elif kind == "scale":
                            scale_probs(i, item)
                        elif kind == "o":
                            wait_filled(dve, i, MAIN, item)
                            for h in range(2):
                                dst, src = head_of(item, h)
                                last = V.tensor_copy(dst, src)
                            last.then_inc(emptied[MAIN, "D"], 1)
                        elif kind == "y":
                            moments(i, MAIN, tag, 0, main_step)
                        elif kind == "norm":
                            normalise(i, MAIN, tag, 0)
                        elif kind == "n":
                            gain(i, MAIN, tag, xT["a" if tag == "ln2" else "b"][:, :])
                    yield
                assert count[main_step] == MAIN_VSTEPS, count

            def hand_over(i):
                wait_emptied(dve, i, MAIN, ("ln3", "n"))
                V.tensor_scalar(x_side[:, :], xT["b"][:, :], 1.0, None, ALU.mult)
                V.tensor_scalar(c_side[:, :], cT[:, :], 1.0, None, ALU.mult)
                dve.wait_ge(skip_loaded, i.at(16, 16))
                V.tensor_scalar(attend[:, :], skip_in[:, :], 0.0, D1 ** -0.5, ALU.not_equal, ALU.mult).then_inc(handed, 1)

            def attention_small(i, tag):
                per, d1 = SMALL[tag]
                n, d = 4 * per, d1 - 1
                for s in range(per * G + 2):
                    if s >= 2 and (s - 1) % per == 0:
                        b = (s - 2) // per
                        wait_filled(dve, i, SIDE, (tag, "o", b))
                        o = bank(SIDE, (tag, "o", b))[:, 0:n * d1].rearrange("p (h d) -> p h d", d=d1)
                        link(i, side_step, V.reciprocal(s_inv[:, b % 2, 0:n].unsqueeze(2), o[:, :, d:d1]))
                        at = slice(b * T, b * T + T)
                        last = V.tensor_tensor(tok[:, at].rearrange("p (h d) -> p h d", d=d), o[:, :, 0:d],
                                               s_inv[:, b % 2, 0:n].unsqueeze(2).broadcast_to([128, n, d]), ALU.mult)
                        if tag == "l1":
                            link(i, side_step, last)
                            last = V.tensor_tensor(x1T[:, at], tok[:, at], x_side[:, at], ALU.add)
                        last.then_inc(emptied[SIDE, "D"], 1)
                    if 1 <= s <= per * G and SIDE.by[tag, "t", s - 1] == "D":
                        take(i, SIDE, (tag, "t", s - 1), lambda x: V.tensor_copy(
                            s_probsT[:, (s - 1) % 2, :], x))
                    if s < per * G:
                        maxes(i, SIDE, tag, s, s_max)
                    yield

            def side(i):
                count[side_step] = 0
                wait_filled(dve, i, SIDE, ("l1", "q"))
                dve.wait_ge(handed, i.at(1, 1))
                V.tensor_scalar(neg_q, bank(SIDE, ("l1", "q")), v1("L1_xattn_bq"), 0.0, ALU.add, ALU.max).then_inc(emptied[SIDE, "D"], 1)
                yield
                yield
                for _ in range(IDLE):
                    yield
                yield from attention_small(i, "l1")
                for n, blk in enumerate(("en", "d0", "d1")):
                    both = (((blk, "q"), qT[:, :]), ((blk, "k"), l2k[:, :]))
                    for m, (name, _) in enumerate(both):
                        wait_filled(dve, i, SIDE, name)
                        V.tensor_scalar(neg[m], bank(SIDE, name), 0.0, None, ALU.min).then_inc(neg_ready, 1)
                    yield
                    for m, (name, dst) in enumerate(both):
                        dve.wait_ge(exp_ready, i.at(6, 2 * n + m + 1))
                        V.scalar_tensor_tensor(out=dst, in0=bank(SIDE, name), scalar=0.0, in1=expn[m],
                                               op0=ALU.max, op1=ALU.add).then_inc(emptied[SIDE, "D"], 1)
                    yield
                    for m in range(2):
                        name = (blk, "kv", m)
                        wait_filled(dve, i, SIDE, name)
                        s = bank(SIDE, name)[:, 0:258].rearrange("p (g n) -> p g n", g=2)
                        for g in range(2):
                            V.tensor_tensor(kvb[:, 2 * m + g, 0:128].rearrange("p (h d) -> p h d", d=D2),
                                            s[:, g, 0:128].rearrange("p (h d) -> p h d", d=D2),
                                            head16[:, :].unsqueeze(2).broadcast_to([128, H2, D2]), ALU.mult)
                        V.tensor_tensor(kvb[:, 2 * m:2 * m + 2, 128:136], s[:, :, 128:129].broadcast_to([128, 2, 8]),
                                        head16[:, :].unsqueeze(1).broadcast_to([128, 2, 8]), ALU.mult).then_inc(emptied[SIDE, "D"], 1)
                    yield
                    for m in range(2):
                        name = (blk, "o", m)
                        wait_filled(dve, i, SIDE, name)
                        s = bank(SIDE, name)[:, 0:272].rearrange("p (g n) -> p g n", g=2)
                        z = l2z[:, m, :].rearrange("p (g h) -> p g h", g=2)
                        link(i, side_step, V.tensor_scalar(z, s[:, :, 128:136], 1e-6, None, ALU.add))
                        link(i, side_step, V.reciprocal(z, z))
                        V.tensor_tensor(tok[:, 2 * m * 128:2 * m * 128 + 256].rearrange("p (g h d) -> p g h d", g=2, d=D2),
                                        s[:, :, 0:128].rearrange("p g (h d) -> p g h d", d=D2),
                                        z.unsqueeze(3).broadcast_to([128, 2, H2, D2]), ALU.mult).then_inc(emptied[SIDE, "D"], 1)
                    yield
                    yield
                    moments(i, SIDE, blk, 1, side_step)
                    yield
                    normalise(i, SIDE, blk, 1)
                    yield
                    gain(i, SIDE, blk, {"en": encT, "d0": x_side, "d1": x1T}[blk][:, :])
                    yield
                    if blk != "d0":
                        yield
                        moments(i, SIDE, blk + "f", 1, side_step)
                        yield
                        normalise(i, SIDE, blk + "f", 1)
                        yield
                        gain(i, SIDE, blk + "f", {"en": encT, "d1": x_side}[blk][:, :])
                        yield
                moments(i, SIDE, "b3", 1, side_step)
                moments(i, SIDE, "x3", 2, side_step)
                yield
                normalise(i, SIDE, "b3", 1)
                normalise(i, SIDE, "x3", 2)
                yield
                gain(i, SIDE, "b3", l3b)
                gain(i, SIDE, "x3", l3x)
                yield
                take(i, SIDE, ("l3", "q"), lambda s: V.tensor_scalar(qT[:, :], s, qkvb[:, 0:1], D3 ** -0.5, ALU.add, ALU.mult))
                yield
                yield
                yield from attention_small(i, "l3")
                yield
                take(i, SIDE, ("l3", "x"), lambda s: V.scalar_tensor_tensor(
                    out=x1T[:, :], in0=s, scalar=v1("L3_xattn_b_o"), in1=x_side[:, :], op0=ALU.add, op1=ALU.add))
                yield
                moments(i, SIDE, "z3", 1, side_step)
                yield
                normalise(i, SIDE, "z3", 1)
                yield
                gain(i, SIDE, "z3", l3x)
                yield
                yield
                def group(n):
                    return slice(i.offset * n, i.offset * n + n) if i.r is None else bass.ds(i.r * n + i.offset * n, n)
                link(i, side_step, V.tensor_tensor(x2_all[:, group(GT)].rearrange("p (g t) -> p g t", g=G),
                                                   x1T[:, :].rearrange("p (g t) -> p g t", g=G),
                                                   mod[:, group(G)].unsqueeze(2).broadcast_to([128, G, T]), ALU.add))
                take(i, SIDE, ("l3", "u"), lambda s: V.tensor_scalar(
                    u_all[:, :, group(G)].rearrange("p t g -> p g t"), s[0:NS, :].rearrange("p (g t) -> p g t", g=G),
                    0.0, None, ALU.add))
                assert count[side_step] == SIDE_VSTEPS, count
                yield

            interleave(main(once), setup_side(), [1] * SETUP_STEPS)
            hand_over(once)
            with dve.Fori(0, GROUPS - 1) as r:
                interleave(main(Pass(r, 1)), side(Pass(r, 0)))
                hand_over(Pass(r, 1))
            assert alone(side(Pass(None, GROUPS - 1))) == SIDE_STEPS

            dve.wait_ge(emptied[SIDE, "D"], GROUPS * SIDE.total["D"])

            def scan_step(t, k):
                dve.wait_ge(scan_mm, t + k)
                s = u_all[:, bass.ds(t + (k - 1), 1), :].rearrange("p a b -> p (a b)")
                V.tensor_tensor(s, s, state[:, (k - 1) % 2, :], ALU.add).then_inc(scan_add, 1)

            for k in range(2, SCAN_UNROLL):
                scan_step(0, k)
            with dve.Fori(0, T // SCAN_UNROLL - 1) as r:
                for k in range(SCAN_UNROLL):
                    scan_step(r * SCAN_UNROLL, SCAN_UNROLL + k)
            dve.wait_ge(scan_silu, T - 1)
            V.tensor_tensor(u_all[:, T - 1, :], u_all[:, T - 1, :], state[:, (T - 1) % 2, :], ALU.add).then_inc(scan_add, 1)
            with dve.Fori(0, GROUPS // 2) as g:
                at = [bass.ds(g * 2 * GT + n * GT, GT) for n in range(2)]
                for n in range(2):
                    dve.wait_ge(fin_mm, g * 2 + (n + 1))
                    V.tensor_tensor(fin_sum[n][:, :], ps[:, n, :], x2_all[:, at[n]], ALU.add).then_inc(fin_add, 1)
                for n in range(2):
                    dve.wait_ge(fin_turn, g * 2 + (n + 1))
                    V.tensor_scalar(x2_all[:, at[n]], ps[:, 2 + n, :], 0.0, None, ALU.add).then_inc(fin_copy, 1)


def kernel(**inputs):
    import concourse.bacc as _bacc
    from concourse.bass_utils import run_bass_kernel_spmd as _run

    nc = _bacc.Bacc("TRN2", target_bir_lowering=False, num_devices=1)
    arrays, aps = {}, {}
    for name, a in inputs.items():
        if name == "itok_BxS2_4_31999":
            continue
        a = np.ascontiguousarray(a)
        if a.dtype == np.bool_:
            a = a.view(np.uint8)
        arrays[f"in_{name}"] = a
        aps[name] = nc.dram_tensor(f"in_{name}", a.shape, mybir.dt.from_np(a.dtype), kind="ExternalInput").ap()
    out = nc.dram_tensor("out_0", (B, T, E), F32, kind="ExternalOutput").ap()
    build_program(nc, aps, out)
    r = _run(nc, [arrays], core_ids=[0])
    return r.results[0]["out_0"]
```
